# Optimizing a Trainium2 kernel written in Bass

```python
import numpy as np
import jax
import jax.numpy as jnp

def _softmax(x, axis=-1):
    return jax.nn.softmax(x, axis=axis)

def _gelu(x):
    return jax.nn.gelu(x, approximate=True)

def _silu(x):
    return jax.nn.silu(x)

def _sigmoid(x):
    return jax.nn.sigmoid(x)

def _layernorm(x, axis=-1, eps=1e-05):
    m = jnp.mean(x, axis=axis, keepdims=True)
    v = jnp.var(x, axis=axis, keepdims=True)
    return (x - m) / jnp.sqrt(v + eps)

def _scatter_add(tgt, idx, src, axis=0):
    return tgt.at[idx].add(src)

def _segment_sum(src, seg, n):
    return jax.ops.segment_sum(src, seg, n)
kernel_name = 'mk_recurrent_d2_jaxref_r8_da40d3'

def setup_inputs(seed: int=0):
    np.random.seed(seed)
    _w = jnp.asarray

    def _L0_attn_setup():
        import jax, jax.numpy as jnp
        import numpy as np
        B, L, DIM = (8, 128, 128)
        D_MODEL = DIM // 2
        D_INNER = 2 * D_MODEL
        D_STATE = 16
        D_CONV = 4
        DT_RANK = D_MODEL // 16

        def _mamba_params(key, scale=0.02):
            ks = jax.random.split(key, 7)
            p = {'Win': jax.random.normal(ks[0], (DIM, 2 * D_INNER), jnp.float32) * scale, 'Wconv': jax.random.normal(ks[1], (D_INNER, D_CONV), jnp.float32) * scale, 'bconv': jnp.zeros((D_INNER,), jnp.float32), 'Wx': jax.random.normal(ks[2], (D_INNER, DT_RANK + 2 * D_STATE), jnp.float32) * scale, 'Wdt': jax.random.normal(ks[3], (DT_RANK, D_INNER), jnp.float32) * scale, 'bdt': jax.random.normal(ks[4], (D_INNER,), jnp.float32) * 0.1, 'Alog': jnp.log(jnp.broadcast_to(jnp.arange(1, D_STATE + 1, dtype=jnp.float32), (D_INNER, D_STATE))), 'Dp': jnp.ones((D_INNER,), jnp.float32), 'Wout': jax.random.normal(ks[5], (D_INNER, D_MODEL), jnp.float32) * scale}
            return p

        def _layernorm(x, g, b, eps=1e-05):
            mu = jnp.mean(x, axis=-1, keepdims=True)
            var = jnp.var(x, axis=-1, keepdims=True)
            return (x - mu) * jax.lax.rsqrt(var + eps) * g + b

        def _mamba(h, Win, Wconv, bconv, Wx, Wdt, bdt, Alog, Dp, Wout):
            xz = h @ Win
            x, z = jnp.split(xz, 2, axis=-1)
            xp = jnp.pad(x, ((0, 0), (D_CONV - 1, 0), (0, 0)))
            x = sum((xp[:, k:k + h.shape[1], :] * Wconv[None, None, :, k] for k in range(D_CONV))) + bconv
            x = jax.nn.silu(x)
            dbc = x @ Wx
            dt = jax.nn.softplus(dbc[..., :DT_RANK] @ Wdt + bdt)
            Bm = dbc[..., DT_RANK:DT_RANK + D_STATE]
            Cm = dbc[..., DT_RANK + D_STATE:]
            A = -jnp.exp(Alog)
            dA = jnp.exp(dt[..., None] * A)
            dBx = dt[..., None] * Bm[:, :, None, :] * x[..., None]

            def step(hc, ins):
                dA_t, dBx_t, C_t = ins
                hc = dA_t * hc + dBx_t
                y = jnp.einsum('bdn,bn->bd', hc, C_t)
                return (hc, y)
            h0 = jnp.zeros((x.shape[0], D_INNER, D_STATE), x.dtype)
            _, ys = jax.lax.scan(step, h0, (dA.transpose(1, 0, 2, 3), dBx.transpose(1, 0, 2, 3), Cm.transpose(1, 0, 2)))
            y = ys.transpose(1, 0, 2)
            y = (y + Dp * x) * jax.nn.silu(z)
            return y @ Wout
        key = jax.random.key(seed)
        kx, k1, k2 = jax.random.split(key, 3)
        inp = {'x': jax.random.normal(kx, (B, L, DIM), jnp.float32), 'ln_g': jnp.ones((DIM,), jnp.float32), 'ln_b': jnp.zeros((DIM,), jnp.float32)}
        for tag, k in (('m1', k1), ('m2', k2)):
            for name, v in _mamba_params(k).items():
                inp[f'{tag}_{name}'] = v
        return inp
    _L0_attn_in = _L0_attn_setup()

    def _L0_ffn_setup():
        import jax, jax.numpy as jnp
        import numpy as np
        B, N, C, H, REG = (1, 2309, 128, 16, 5)
        D = C // H
        key = jax.random.key(seed)
        k0, k1, k2, k3 = jax.random.split(key, 4)
        x = jax.random.normal(k0, (B, N, C), dtype=jnp.float32)
        g_info = jax.random.normal(k1, (12, 2, C), dtype=jnp.float32)
        W_qkv = jax.random.normal(k2, (C, 3 * C), dtype=jnp.float32) * 0.02
        W_proj = jax.random.normal(k3, (C, C), dtype=jnp.float32) * 0.02
        b_proj = jnp.zeros((C,), dtype=jnp.float32)
        return {'x': x, 'g_info': g_info, 'W_qkv': W_qkv, 'W_proj': W_proj, 'b_proj': b_proj}
    _L0_ffn_in = _L0_ffn_setup()

    def _L1_attn_setup():
        import jax, jax.numpy as jnp
        import numpy as np
        L, H, D_MODEL, FFN = (2, 8, 128, 512)
        HD = D_MODEL // H
        SCALE_BASE = 64
        EPS = 1e-05

        def _layernorm(x, w, b):
            mu = x.mean(-1, keepdims=True)
            var = ((x - mu) ** 2).mean(-1, keepdims=True)
            return (x - mu) * jax.lax.rsqrt(var + EPS) * w + b

        def _groupnorm(y, w, b):
            B, S, _ = y.shape
            yg = y.reshape(B, S, H, HD)
            mu = yg.mean(-1, keepdims=True)
            var = ((yg - mu) ** 2).mean(-1, keepdims=True)
            yn = ((yg - mu) * jax.lax.rsqrt(var + EPS)).reshape(B, S, H * HD)
            return yn * w + b

        def _xpos_tables(S):
            scale_vec = (np.arange(0, HD, 2) + 0.4 * HD) / (1.4 * HD)
            power = (np.arange(S, dtype=np.float64) / SCALE_BASE)[:, None]
            scale = scale_vec[None, :] ** power
            half = HD // 2
            inv_freq = 1.0 / 10000.0 ** (np.arange(half, dtype=np.float64) / half)
            ang = np.arange(S, dtype=np.float64)[:, None] * inv_freq[None, :]
            sin, cos = (np.sin(ang), np.cos(ang))
            dup = lambda m: jnp.asarray(np.repeat(m, 2, axis=-1).astype(np.float32))
            return (dup(sin * scale), dup(cos * scale), dup(sin / scale), dup(cos / scale))

        def _rotate_every_two(x):
            x1, x2 = (x[..., ::2], x[..., 1::2])
            return jnp.stack((-x2, x1), axis=-1).reshape(x.shape)

        def _decay_mask(S):
            gammas = 1.0 - np.exp(np.linspace(np.log(1.0 / 32), np.log(1.0 / 64), H))
            n = np.arange(S)[:, None]
            m = np.arange(S)[None, :]
            diff = (n - m).astype(np.float64)
            D = np.where(n >= m, gammas[:, None, None] ** diff[None], 0.0)
            return jnp.asarray(D.astype(np.float32))
        key = jax.random.key(seed)
        ks = jax.random.split(key, 8)
        B, S = (2, 256)
        rn = lambda k, shape, s: jax.random.normal(k, shape, dtype=jnp.float32) * s
        return {'X': rn(ks[0], (B, S, D_MODEL), 1.0), 'ln1_w': jnp.ones((L, D_MODEL), jnp.float32), 'ln1_b': jnp.zeros((L, D_MODEL), jnp.float32), 'ln2_w': jnp.ones((L, D_MODEL), jnp.float32), 'ln2_b': jnp.zeros((L, D_MODEL), jnp.float32), 'WQ': rn(ks[1], (L, H, D_MODEL, HD), 1.0 / D_MODEL), 'WK': rn(ks[2], (L, H, D_MODEL, HD), 1.0 / D_MODEL), 'WV': rn(ks[3], (L, H, D_MODEL, HD), 1.0 / D_MODEL), 'gn_w': jnp.ones((L, D_MODEL), jnp.float32), 'gn_b': jnp.zeros((L, D_MODEL), jnp.float32), 'WG': rn(ks[4], (L, D_MODEL, D_MODEL), 1.0 / D_MODEL), 'WO': rn(ks[5], (L, D_MODEL, D_MODEL), 1.0 / D_MODEL), 'ffn_w1': rn(ks[6], (L, D_MODEL, FFN), 1.0 / np.sqrt(D_MODEL)), 'ffn_b1': jnp.zeros((L, FFN), jnp.float32), 'ffn_w2': rn(ks[7], (L, FFN, D_MODEL), 1.0 / np.sqrt(FFN)), 'ffn_b2': jnp.zeros((L, D_MODEL), jnp.float32)}
    _L1_attn_in = _L1_attn_setup()

    def _L1_ffn_setup():
        import jax, jax.numpy as jnp
        import numpy as np
        B, M, D = (4, 256, 128)
        N, P = (64, 32)
        key = jax.random.key(seed)
        k1, k2, k3, k4 = jax.random.split(key, 4)
        x = jax.random.normal(k1, (B, M, D), dtype=jnp.float32)
        phi = jax.random.normal(k2, (D, N, P), dtype=jnp.float32) * (1.0 / np.sqrt(D))
        W = jax.random.normal(k3, (N, D, D), dtype=jnp.float32) * (1.0 / np.sqrt(D))
        b = jax.random.normal(k4, (N, D), dtype=jnp.float32) * 0.01
        return {'x': x, 'phi': phi, 'W': W, 'b': b}
    _L1_ffn_in = _L1_ffn_setup()
    _d = {'L0_attn_x': _L0_attn_in['x'], 'L0_attn_ln_g': _L0_attn_in['ln_g'], 'L0_attn_ln_b': _L0_attn_in['ln_b'], 'L0_attn_m1_Win': _L0_attn_in['m1_Win'], 'L0_attn_m1_Wconv': _L0_attn_in['m1_Wconv'], 'L0_attn_m1_bconv': _L0_attn_in['m1_bconv'], 'L0_attn_m1_Wx': _L0_attn_in['m1_Wx'], 'L0_attn_m1_Wdt': _L0_attn_in['m1_Wdt'], 'L0_attn_m1_bdt': _L0_attn_in['m1_bdt'], 'L0_attn_m1_Alog': _L0_attn_in['m1_Alog'], 'L0_attn_m1_Dp': _L0_attn_in['m1_Dp'], 'L0_attn_m1_Wout': _L0_attn_in['m1_Wout'], 'L0_attn_m2_Win': _L0_attn_in['m2_Win'], 'L0_attn_m2_Wconv': _L0_attn_in['m2_Wconv'], 'L0_attn_m2_bconv': _L0_attn_in['m2_bconv'], 'L0_attn_m2_Wx': _L0_attn_in['m2_Wx'], 'L0_attn_m2_Wdt': _L0_attn_in['m2_Wdt'], 'L0_attn_m2_bdt': _L0_attn_in['m2_bdt'], 'L0_attn_m2_Alog': _L0_attn_in['m2_Alog'], 'L0_attn_m2_Dp': _L0_attn_in['m2_Dp'], 'L0_attn_m2_Wout': _L0_attn_in['m2_Wout'], 'L0_ffn_g_info': _L0_ffn_in['g_info'], 'L0_ffn_W_qkv': _L0_ffn_in['W_qkv'], 'L0_ffn_W_proj': _L0_ffn_in['W_proj'], 'L0_ffn_b_proj': _L0_ffn_in['b_proj'], 'L1_attn_ln1_w': _L1_attn_in['ln1_w'], 'L1_attn_ln1_b': _L1_attn_in['ln1_b'], 'L1_attn_ln2_w': _L1_attn_in['ln2_w'], 'L1_attn_ln2_b': _L1_attn_in['ln2_b'], 'L1_attn_WQ': _L1_attn_in['WQ'], 'L1_attn_WK': _L1_attn_in['WK'], 'L1_attn_WV': _L1_attn_in['WV'], 'L1_attn_gn_w': _L1_attn_in['gn_w'], 'L1_attn_gn_b': _L1_attn_in['gn_b'], 'L1_attn_WG': _L1_attn_in['WG'], 'L1_attn_WO': _L1_attn_in['WO'], 'L1_attn_ffn_w1': _L1_attn_in['ffn_w1'], 'L1_attn_ffn_b1': _L1_attn_in['ffn_b1'], 'L1_attn_ffn_w2': _L1_attn_in['ffn_w2'], 'L1_attn_ffn_b2': _L1_attn_in['ffn_b2'], 'L1_ffn_phi': _L1_ffn_in['phi'], 'L1_ffn_W': _L1_ffn_in['W'], 'L1_ffn_b': _L1_ffn_in['b']}
    _x0 = _d['L0_attn_x']
    _d['L0_attn_x'] = jax.random.normal(jax.random.fold_in(jax.random.key(seed), 1), (4, 1024, 128), dtype=_x0.dtype)
    del _x0
    return _d

def reference(L0_attn_x, L0_attn_ln_g, L0_attn_ln_b, L0_attn_m1_Win, L0_attn_m1_Wconv, L0_attn_m1_bconv, L0_attn_m1_Wx, L0_attn_m1_Wdt, L0_attn_m1_bdt, L0_attn_m1_Alog, L0_attn_m1_Dp, L0_attn_m1_Wout, L0_attn_m2_Win, L0_attn_m2_Wconv, L0_attn_m2_bconv, L0_attn_m2_Wx, L0_attn_m2_Wdt, L0_attn_m2_bdt, L0_attn_m2_Alog, L0_attn_m2_Dp, L0_attn_m2_Wout, L0_ffn_g_info, L0_ffn_W_qkv, L0_ffn_W_proj, L0_ffn_b_proj, L1_attn_ln1_w, L1_attn_ln1_b, L1_attn_ln2_w, L1_attn_ln2_b, L1_attn_WQ, L1_attn_WK, L1_attn_WV, L1_attn_gn_w, L1_attn_gn_b, L1_attn_WG, L1_attn_WO, L1_attn_ffn_w1, L1_attn_ffn_b1, L1_attn_ffn_w2, L1_attn_ffn_b2, L1_ffn_phi, L1_ffn_W, L1_ffn_b):

    def _L0_attn_ref(x, ln_g, ln_b, m1_Win, m1_Wconv, m1_bconv, m1_Wx, m1_Wdt, m1_bdt, m1_Alog, m1_Dp, m1_Wout, m2_Win, m2_Wconv, m2_bconv, m2_Wx, m2_Wdt, m2_bdt, m2_Alog, m2_Dp, m2_Wout):
        import jax, jax.numpy as jnp
        import numpy as np
        B, L, DIM = (8, 128, 128)
        D_MODEL = DIM // 2
        D_INNER = 2 * D_MODEL
        D_STATE = 16
        D_CONV = 4
        DT_RANK = D_MODEL // 16

        def _mamba_params(key, scale=0.02):
            ks = jax.random.split(key, 7)
            p = {'Win': jax.random.normal(ks[0], (DIM, 2 * D_INNER), jnp.float32) * scale, 'Wconv': jax.random.normal(ks[1], (D_INNER, D_CONV), jnp.float32) * scale, 'bconv': jnp.zeros((D_INNER,), jnp.float32), 'Wx': jax.random.normal(ks[2], (D_INNER, DT_RANK + 2 * D_STATE), jnp.float32) * scale, 'Wdt': jax.random.normal(ks[3], (DT_RANK, D_INNER), jnp.float32) * scale, 'bdt': jax.random.normal(ks[4], (D_INNER,), jnp.float32) * 0.1, 'Alog': jnp.log(jnp.broadcast_to(jnp.arange(1, D_STATE + 1, dtype=jnp.float32), (D_INNER, D_STATE))), 'Dp': jnp.ones((D_INNER,), jnp.float32), 'Wout': jax.random.normal(ks[5], (D_INNER, D_MODEL), jnp.float32) * scale}
            return p

        def _layernorm(x, g, b, eps=1e-05):
            mu = jnp.mean(x, axis=-1, keepdims=True)
            var = jnp.var(x, axis=-1, keepdims=True)
            return (x - mu) * jax.lax.rsqrt(var + eps) * g + b

        def _mamba(h, Win, Wconv, bconv, Wx, Wdt, bdt, Alog, Dp, Wout):
            xz = h @ Win
            x, z = jnp.split(xz, 2, axis=-1)
            xp = jnp.pad(x, ((0, 0), (D_CONV - 1, 0), (0, 0)))
            x = sum((xp[:, k:k + h.shape[1], :] * Wconv[None, None, :, k] for k in range(D_CONV))) + bconv
            x = jax.nn.silu(x)
            dbc = x @ Wx
            dt = jax.nn.softplus(dbc[..., :DT_RANK] @ Wdt + bdt)
            Bm = dbc[..., DT_RANK:DT_RANK + D_STATE]
            Cm = dbc[..., DT_RANK + D_STATE:]
            A = -jnp.exp(Alog)
            dA = jnp.exp(dt[..., None] * A)
            dBx = dt[..., None] * Bm[:, :, None, :] * x[..., None]

            def step(hc, ins):
                dA_t, dBx_t, C_t = ins
                hc = dA_t * hc + dBx_t
                y = jnp.einsum('bdn,bn->bd', hc, C_t)
                return (hc, y)
            h0 = jnp.zeros((x.shape[0], D_INNER, D_STATE), x.dtype)
            _, ys = jax.lax.scan(step, h0, (dA.transpose(1, 0, 2, 3), dBx.transpose(1, 0, 2, 3), Cm.transpose(1, 0, 2)))
            y = ys.transpose(1, 0, 2)
            y = (y + Dp * x) * jax.nn.silu(z)
            return y @ Wout
        h = _layernorm(x, ln_g, ln_b)
        fwd = _mamba(h, m1_Win, m1_Wconv, m1_bconv, m1_Wx, m1_Wdt, m1_bdt, m1_Alog, m1_Dp, m1_Wout)
        bwd = _mamba(h[:, ::-1, :], m2_Win, m2_Wconv, m2_bconv, m2_Wx, m2_Wdt, m2_bdt, m2_Alog, m2_Dp, m2_Wout)
        out = jnp.concatenate([fwd, bwd], axis=-1) + x
        return jax.nn.gelu(out, approximate=False)

    def _L0_ffn_ref(x, g_info, W_qkv, W_proj, b_proj):
        import jax, jax.numpy as jnp
        import numpy as np
        B, N, C, H, REG = (1, 2309, 128, 16, 5)
        D = C // H
        Bx, Nx, Cx = x.shape
        scale = D ** (-0.5)
        qkv = (x @ W_qkv).reshape(Bx, Nx, 3, H, D)
        q, k, v = (qkv[:, :, 0], qkv[:, :, 1], qkv[:, :, 2])
        g_layer = g_info[0].reshape(-1, H, D)
        q_g = g_layer[0]
        q_pure = q[:, REG:]
        q_n = q_pure / jnp.linalg.norm(q_pure, axis=-1, keepdims=True)
        qg_n = q_g / jnp.linalg.norm(q_g, axis=-1, keepdims=True)
        sim = (qg_n[None, None] * q_n).sum(-1).mean(-1)
        sim = (sim - sim.min()) / (sim.max() - sim.min())
        pos = sim > 0.9
        logits = jnp.einsum('bqhd,bkhd->bhqk', q * scale, k)

        def masked_attn(tok_mask):
            key_mask = jnp.concatenate([jnp.ones((Bx, REG), bool), tok_mask], axis=1)
            l = jnp.where(key_mask[:, None, None, :], logits, -jnp.inf)
            a = jax.nn.softmax(l, axis=-1)
            return jnp.einsum('bhqk,bkhd->bqhd', a, v)
        x_pos = masked_attn(pos)
        x_neg = masked_attn(~pos)
        reg_out = (x_pos[:, :REG] + x_neg[:, :REG]) * 0.5
        tok_out = jnp.where(pos[:, :, None, None], x_pos[:, REG:], x_neg[:, REG:])
        out = jnp.concatenate([reg_out, tok_out], axis=1).reshape(Bx, Nx, Cx)
        return out @ W_proj + b_proj

    def _L1_attn_ref(X, ln1_w, ln1_b, ln2_w, ln2_b, WQ, WK, WV, gn_w, gn_b, WG, WO, ffn_w1, ffn_b1, ffn_w2, ffn_b2):
        import jax, jax.numpy as jnp
        import numpy as np
        L, H, D_MODEL, FFN = (2, 8, 128, 512)
        HD = D_MODEL // H
        SCALE_BASE = 64
        EPS = 1e-05

        def _layernorm(x, w, b):
            mu = x.mean(-1, keepdims=True)
            var = ((x - mu) ** 2).mean(-1, keepdims=True)
            return (x - mu) * jax.lax.rsqrt(var + EPS) * w + b

        def _groupnorm(y, w, b):
            B, S, _ = y.shape
            yg = y.reshape(B, S, H, HD)
            mu = yg.mean(-1, keepdims=True)
            var = ((yg - mu) ** 2).mean(-1, keepdims=True)
            yn = ((yg - mu) * jax.lax.rsqrt(var + EPS)).reshape(B, S, H * HD)
            return yn * w + b

        def _xpos_tables(S):
            scale_vec = (np.arange(0, HD, 2) + 0.4 * HD) / (1.4 * HD)
            power = (np.arange(S, dtype=np.float64) / SCALE_BASE)[:, None]
            scale = scale_vec[None, :] ** power
            half = HD // 2
            inv_freq = 1.0 / 10000.0 ** (np.arange(half, dtype=np.float64) / half)
            ang = np.arange(S, dtype=np.float64)[:, None] * inv_freq[None, :]
            sin, cos = (np.sin(ang), np.cos(ang))
            dup = lambda m: jnp.asarray(np.repeat(m, 2, axis=-1).astype(np.float32))
            return (dup(sin * scale), dup(cos * scale), dup(sin / scale), dup(cos / scale))

        def _rotate_every_two(x):
            x1, x2 = (x[..., ::2], x[..., 1::2])
            return jnp.stack((-x2, x1), axis=-1).reshape(x.shape)

        def _decay_mask(S):
            gammas = 1.0 - np.exp(np.linspace(np.log(1.0 / 32), np.log(1.0 / 64), H))
            n = np.arange(S)[:, None]
            m = np.arange(S)[None, :]
            diff = (n - m).astype(np.float64)
            D = np.where(n >= m, gammas[:, None, None] ** diff[None], 0.0)
            return jnp.asarray(D.astype(np.float32))
        B, S, _ = X.shape
        sinq, cosq, sink, cosk = _xpos_tables(S)
        Dm = _decay_mask(S)
        for i in range(L):
            Xn = _layernorm(X, ln1_w[i], ln1_b[i])
            Q = jnp.einsum('bsd,hdk->bhsk', Xn, WQ[i])
            K = jnp.einsum('bsd,hdk->bhsk', Xn, WK[i])
            V = jnp.einsum('bsd,hdk->bhsk', Xn, WV[i])
            Q = Q * cosq + _rotate_every_two(Q) * sinq
            K = K * cosk + _rotate_every_two(K) * sink
            scores = jnp.einsum('bhsk,bhtk->bhst', Q, K) * Dm[None]
            Yh = jnp.einsum('bhst,bhtk->bhsk', scores, V)
            Y = Yh.transpose(0, 2, 1, 3).reshape(B, S, H * HD)
            Y = _groupnorm(Y, gn_w[i], gn_b[i])
            G = jax.nn.silu(Xn @ WG[i])
            Y = G * Y @ WO[i] + X
            Yn = _layernorm(Y, ln2_w[i], ln2_b[i])
            X = jax.nn.silu(Yn @ ffn_w1[i] + ffn_b1[i]) @ ffn_w2[i] + ffn_b2[i] + Y
        return X

    def _L1_ffn_ref(x, phi, W, b):
        import jax, jax.numpy as jnp
        import numpy as np
        B, M, D = (4, 256, 128)
        N, P = (64, 32)
        logits = jnp.einsum('bmd,dnp->bmnp', x, phi)
        dispatch = jax.nn.softmax(logits, axis=0)
        bsz, m, n, p = logits.shape
        combine = jax.nn.softmax(logits.reshape(bsz, m, n * p), axis=-1).reshape(bsz, m, n, p)
        slots = jnp.einsum('bmd,bmnp->bnpd', x, dispatch)
        y = jnp.einsum('bnpd,nde->bnpe', slots, W) + b[None, :, None, :]
        out = jnp.einsum('bnpd,bmnp->bmd', y, combine)
        return out
    x = L0_attn_x
    xn = _layernorm(x, axis=-1)
    s = _L0_attn_ref(xn, L0_attn_ln_g, L0_attn_ln_b, L0_attn_m1_Win, L0_attn_m1_Wconv, L0_attn_m1_bconv, L0_attn_m1_Wx, L0_attn_m1_Wdt, L0_attn_m1_bdt, L0_attn_m1_Alog, L0_attn_m1_Dp, L0_attn_m1_Wout, L0_attn_m2_Win, L0_attn_m2_Wconv, L0_attn_m2_bconv, L0_attn_m2_Wx, L0_attn_m2_Wdt, L0_attn_m2_bdt, L0_attn_m2_Alog, L0_attn_m2_Dp, L0_attn_m2_Wout)
    g = _silu(_L0_ffn_ref(xn, L0_ffn_g_info, L0_ffn_W_qkv, L0_ffn_W_proj, L0_ffn_b_proj))
    x = x + s * g
    xn = _layernorm(x, axis=-1)
    s = _L1_attn_ref(xn, L1_attn_ln1_w, L1_attn_ln1_b, L1_attn_ln2_w, L1_attn_ln2_b, L1_attn_WQ, L1_attn_WK, L1_attn_WV, L1_attn_gn_w, L1_attn_gn_b, L1_attn_WG, L1_attn_WO, L1_attn_ffn_w1, L1_attn_ffn_b1, L1_attn_ffn_w2, L1_attn_ffn_b2)
    g = _silu(_L1_ffn_ref(xn, L1_ffn_phi, L1_ffn_W, L1_ffn_b))
    x = x + s * g
    return x

_drawn_inputs = setup_inputs


def setup_inputs(seed=0):
    import zlib

    import numpy as np

    out = dict(_drawn_inputs(seed))
    spreads = {'L0_attn_ln_g': (1.0, 0.6),
     'L0_attn_ln_b': (0.0, 0.8),
     'L0_attn_m1_bconv': (0.0, 0.8),
     'L0_attn_m1_Dp': (1.0, 0.6),
     'L0_attn_m2_bconv': (0.0, 0.8),
     'L0_attn_m2_Dp': (1.0, 0.6),
     'L0_ffn_b_proj': (0.0, 0.1),
     'L1_attn_ln1_w': (1.0, 0.6),
     'L1_attn_ln1_b': (0.0, 0.8),
     'L1_attn_ln2_w': (1.0, 0.2),
     'L1_attn_ln2_b': (0.0, 0.314),
     'L1_attn_gn_w': (1.0, 0.6),
     'L1_attn_gn_b': (0.0, 0.8),
     'L1_attn_ffn_b1': (0.0, 0.384),
     'L1_attn_ffn_b2': (0.0, 0.1)}
    factors = {'L0_attn_m1_Win': 8.0,
     'L0_attn_m1_Wconv': 8.0,
     'L0_attn_m1_Wx': 8.0,
     'L0_attn_m1_Wdt': 8.0,
     'L0_attn_m1_bdt': 8.0,
     'L0_attn_m1_Alog': 8.0,
     'L0_attn_m1_Wout': 8.0,
     'L0_attn_m2_Win': 8.0,
     'L0_attn_m2_Wconv': 8.0,
     'L0_attn_m2_Wx': 8.0,
     'L0_attn_m2_Wdt': 8.0,
     'L0_attn_m2_bdt': 8.0,
     'L0_attn_m2_Alog': 8.0,
     'L0_attn_m2_Wout': 8.0,
     'L0_ffn_g_info': 8.0,
     'L0_ffn_W_qkv': 8.0,
     'L0_ffn_W_proj': 8.0,
     'L1_attn_WQ': 8.0,
     'L1_attn_WK': 8.0,
     'L1_attn_WV': 8.0,
     'L1_attn_WG': 8.0,
     'L1_attn_WO': 8.0,
     'L1_ffn_b': 64.0}
    for name, (base, spread) in spreads.items():
        noise = np.random.default_rng([zlib.crc32(name.encode()), seed]).standard_normal(out[name].shape)
        drawn = base * np.exp(spread * noise) if base else spread * noise
        out[name] = jnp.asarray(drawn.astype(out[name].dtype))
    for name, factor in factors.items():
        out[name] = (out[name] * factor).astype(out[name].dtype)
    return out
```

```python
import numpy as np
import concourse.bass as bass
from concourse import mybir
from contextlib import ExitStack

fp32 = mybir.dt.float32
bf16 = mybir.dt.bfloat16
ALU = mybir.AluOpType
ACT = mybir.ActivationFunctionType
AX = mybir.AxisListType

B, L, C = 4, 1024, 128
P = 128
NT = L // P
N = B * L
HALF = 512
EPS = 1e-5

AH, AD, REG = 16, 8, 5
AG = 4
NG = AH // AG
EXTRA = 32
QW = L + EXTRA
ROWS = 9 * AD + 2 + 3
BIG = float(2.0 ** 100)

DI, DS, DR, DC, DM = 128, 16, 4, 4, 64

RL, RH, RD, FFN = 2, 8, 16, 512

ME, MP = 64, 32
MS = ME * MP


def shape_constants():
    c = {}
    reg = np.zeros((P, B, NT), np.float32)
    reg[:REG, :, 0] = 1.0
    c["reg_tok"] = reg.reshape(P, B * NT)
    rr = np.zeros((B * NT, P), np.float32)
    rr[::NT, :REG] = 1.0
    c["reg_row"] = rr
    c["ident"] = np.eye(P, dtype=np.float32)
    part = np.arange(P)
    head = (part // 32) * AG + part % AG
    c["same_head"] = (head[:, None] == head[None, :]).astype(np.float32)
    c["head_of"] = (head[:, None] == np.arange(AH)[None, :]).astype(np.float32)
    sv = (np.arange(0, RD, 2) + 0.4 * RD) / (1.4 * RD)
    scale = sv[None, :] ** (np.arange(L, dtype=np.float64) / 64)[:, None]
    half = RD // 2
    inv = 1.0 / 10000.0 ** (np.arange(half, dtype=np.float64) / half)
    ang = np.arange(L, dtype=np.float64)[:, None] * inv[None, :]
    dup = lambda m: np.tile(np.repeat(m, 2, axis=-1).astype(np.float32).T, (RH, 1))
    c["xpos"] = np.stack([dup(np.cos(ang) * scale), dup(np.sin(ang) * scale),
                          dup(np.cos(ang) / scale), dup(np.sin(ang) / scale)], axis=1).copy()
    gam = 1.0 - np.exp(np.linspace(np.log(1.0 / 32), np.log(1.0 / 64), RH))
    n = np.arange(P)
    d = n[None, :] - n[:, None]
    dec = np.where(d[:, None, :] >= 0, gam[None, :, None] ** np.maximum(d, 0)[:, None, :], 0.0)
    c["decay"] = dec.astype(np.float32)
    hk = part // RD
    c["decay_q"] = (gam[hk][:, None] ** n[None, :]).astype(np.float32)
    c["decay_k"] = (gam[hk][None, :] ** (P - n)[:, None]).astype(np.float32)
    c["decay_s"] = (gam[hk] ** P).astype(np.float32).reshape(P, 1)
    c["rblock"] = (hk[:, None] == hk[None, :]).astype(np.float32)
    c["rhead"] = (hk[:, None] == np.arange(RH)[None, :]).astype(np.float32)
    return c


class Signals:

    def __init__(self, nc, ctx, prefix, names):
        self.nc = nc
        self.all = {}
        for n in names.split():
            self.all[n] = ctx.enter_context(nc.semaphore(f"{prefix}_{n}"))

    def __getitem__(self, name):
        return self.all[name]

    def clear(self):
        for s in self.all.values():
            self.nc.sync.sem_clear(s)
        self.nc.all_engine_barrier()


class Chain:

    def __init__(self, eng, sem):
        self.eng, self.sem, self.n = eng, sem, 0

    def step(self, ins):
        self.n += 1
        ins.then_inc(self.sem, 1)

    def wait(self):
        self.eng.wait_ge(self.sem, self.n)


def flat(ap):
    return ap.rearrange("p o t c -> p (o t) c")


def phase_prepare(nc, d, keep):
    with ExitStack() as ctx:
        sb = lambda n, s, t=fp32: ctx.enter_context(nc.sbuf_tensor(n, s, t))
        S = Signals(nc, ctx, "p", "load w sq nrm nrm_sb pw dir step v0")
        g_col = sb("p_gcol", [P, 4])
        mh = sb("p_mh", [P, 1])
        pN = ctx.enter_context(nc.psum_tensor("p_pN", [P, HALF], fp32))
        K = keep
        with nc.Block() as block:
            @block.sync
            def _(sp):
                loads = [(K["wqkv"][:, :, :], d["W_qkv"].rearrange("c (s n) -> c s n", s=3)),
                         (K["ident"][:, :], d["ident"]), (K["same_head"][:, :], d["same_head"]),
                         (K["head_of"][:, :], d["head_of"]), (K["reg_tok"][:, :], d["reg_tok"]),
                         (K["ln"][:, 0:1], d["ln_g"].rearrange("(c o) -> c o", o=1)),
                         (K["ln"][:, 1:2], d["ln_b"].rearrange("(c o) -> c o", o=1)),
                         (K["x_tok"][:, :, :, :], d["x"].rearrange("b (t p) c -> p b t c", p=P))]
                for dst, src in loads:
                    sp.dma_start(dst, src).then_inc(S["load"], 16)
                with nc.allow_non_contiguous_dma(reason="128 values, once"):
                    for g in range(NG):
                        sp.dma_start(g_col[32 * g:32 * g + 32, 0:1],
                                     d["g_info"][0, 0:1, 32 * g:32 * g + 32].rearrange(
                                         "o (j e) -> e j o", j=AG)).then_inc(S["load"], 16)
                sp.wait_ge(S["load"], 16 * (len(loads) + NG))
                sp.wait_ge(S["dir"], 1)

            @block.vector
            def _(ve):
                ve.wait_ge(S["load"], 16 * (8 + NG))
                for s in range(2):
                    ve.tensor_copy(K["wqk"][:, s, :].rearrange("c (g e j) -> c g e j", g=NG, e=AD),
                                   K["wqkv"][:, s, :].rearrange("c (g j e) -> c g e j", g=NG, j=AG)).then_inc(S["w"], 1)
                ve.memset(mh[:, :], -0.5).then_inc(S["w"], 1)
                ve.tensor_tensor(g_col[:, 1:2], g_col[:, 0:1], g_col[:, 0:1], ALU.mult).then_inc(S["sq"], 1)
                ve.wait_ge(S["nrm"], 1)
                ve.tensor_copy(g_col[:, 2:3], pN[:, 0:1]).then_inc(S["nrm_sb"], 1)
                ve.wait_ge(S["pw"], 1)
                ve.tensor_tensor(g_col[:, 1:2], g_col[:, 0:1], g_col[:, 3:4], ALU.mult).then_inc(S["step"], 1)
                ve.wait_ge(S["step"], 1)
                ve.tensor_scalar(K["gdir"][:, :], K["head_of"][:, :], g_col[:, 1:2], None, ALU.mult).then_inc(S["dir"], 1)

            @block.tensor
            def _(pe):
                pe.wait_ge(S["sq"], 1)
                pe.matmul(pN[:, 0:1], K["same_head"][:, :], g_col[:, 1:2], start=True, stop=True).then_inc(S["nrm"], 1)

            @block.gpsimd
            def _(po):
                po.wait_ge(S["w"], 3)
                po.wait_ge(S["nrm_sb"], 1)
                po.tensor_tensor(g_col[:, 3:4], g_col[:, 2:3], mh[:, :], ALU.pow).then_inc(S["pw"], 1)
        S.clear()


def token_norm(ve, S, src, out, stats, mv, rstd, n):
    for t in range(NT):
        ve.bn_stats(stats[:, t, :], src(t)).then_inc(S["stat"], 1)
    ve.wait_ge(S["stat"], NT * n)
    for t in range(NT):
        ve.bn_aggr(mv[:, t, :], stats[:, t, :]).then_inc(S["aggr"], 1)
    ve.wait_ge(S["aggr"], NT * n)
    ve.wait_ge(S["rstd"], n)
    for t in range(NT):
        ve.tensor_scalar(out(t), src(t), mv[:, t, 0:1], rstd[:, t:t + 1], ALU.subtract, ALU.mult).then_inc(S["normed"], 1)


def inverse_root(nc, po, S, mv, tmp, mhalf, rstd, n):
    po.wait_ge(S["aggr"], NT * n)
    nc.gpsimd.tensor_scalar(tmp[:, :], mv[:, :, 1], EPS, None, ALU.add).then_inc(S["veps"], 1)
    po.wait_ge(S["veps"], n)
    nc.gpsimd.tensor_tensor(rstd[:, :], tmp[:, :], mhalf[:, :], ALU.pow).then_inc(S["rstd"], 1)


def phase_project(nc, d, keep):
    with ExitStack() as ctx:
        sb = lambda n, s, t=fp32: ctx.enter_context(nc.sbuf_tensor(n, s, t))
        ps = lambda n, s, t=fp32: ctx.enter_context(nc.psum_tensor(n, s, t))
        K = keep
        stats, mv, rstd = sb("a_stats", [P, NT, 6]), sb("a_mv", [P, NT, 2]), sb("a_rstd", [P, NT])
        tmp, mhalf = sb("a_tmp", [P, NT]), sb("a_mhalf", [P, NT * AH])
        xn_b, h_b = sb("a_xnb", [P, NT, P]), sb("a_hb", [P, NT, P])
        xn_Tb = sb("a_xntb", [P, L])
        q_f, q_sq = sb("a_qf", [P, L]), sb("a_qsq", [P, L])
        qk_s = sb("a_qks", [P, 2, L])
        r1, r2 = sb("a_r1", [P, 2, L]), sb("a_r2", [P, 2, L])
        sp_q, sp_k = sb("a_spq", [P, 3, L], bf16), sb("a_spk", [P, 3, L], bf16)
        v_b = sb("a_vb", [P, NT, AH, 32])
        nd, rn, dn = sb("a_nd", [P, NT, 2, AH]), sb("a_rn", [P, NT, AH]), sb("a_dn", [P, NT, AH])
        p_x, p_h = ps("a_px", [P, L]), ps("a_ph", [P, L])
        p_q, p_k = ps("a_pq", [P, L]), ps("a_pk", [P, L])
        S = Signals(nc, ctx, "a", "stat aggr veps rstd normed xturn hturn xT hT copyT qmm kmm qf qsq ks vmm vout vset "
                    "half dots ndout rn mul sim hi res1 mid res2 lo stored")
        with nc.Fori(0, B) as b:
            with nc.Block() as block:
                x_b = flat(K["x_tok"][:, bass.ds(b, 1), :, :])

                @block.sync
                def _(sp):
                    sp.wait_ge(S["vout"], 2)
                    sp.dma_start(d["v_tiles"][bass.ds(b, 1), :, :].rearrange("o p n -> p (o n)"),
                                 v_b[:, :, :, :].rearrange("p t h e -> p (t h e)")).then_inc(S["stored"], 16)
                    sp.wait_ge(S["lo"], 2)
                    sp.dma_start(d["q_parts"][bass.ds(b, 1), :, :, :].rearrange("o s p t -> p (o s) t"),
                                 sp_q[:, :, :]).then_inc(S["stored"], 16)
                    sp.dma_start(d["k_parts"][bass.ds(b, 1), :, :, :].rearrange("o s p t -> p (o s) t"),
                                 sp_k[:, :, :]).then_inc(S["stored"], 16)
                    sp.wait_ge(S["stored"], 48)

                @block.gpsimd
                def _(po):
                    po.memset(mhalf[:, :], -0.5).then_inc(S["half"], 1)
                    po.memset(v_b[:, :, :, :], 0.0).then_inc(S["vset"], 1)
                    po.wait_ge(S["vset"], 1)
                    po.memset(v_b[:, :, :, AD:AD + 1], 1.0).then_inc(S["vset"], 1)
                    po.wait_ge(S["half"], 1)
                    for n in (1, 2):
                        inverse_root(nc, po, S, mv, tmp, mhalf[:, 0:NT], rstd, n)
                    po.wait_ge(S["ndout"], 1)
                    nc.gpsimd.tensor_tensor(rn[:, :, :], nd[:, :, 0, :],
                                            mhalf[:, :].rearrange("p (t h) -> p t h", h=AH), ALU.pow).then_inc(S["rn"], 1)

                @block.vector
                def _(ve):
                    token_norm(ve, S, lambda t: x_b[:, t, :], lambda t: xn_b[:, t, :], stats, mv, rstd, 1)
                    ve.wait_ge(S["normed"], NT)
                    token_norm(ve, S, lambda t: xn_b[:, t, :], lambda t: h_b[:, t, :], stats, mv, rstd, 2)
                    for i, (part, have) in enumerate(((sp_q, "qf"), (sp_k, "ks"))):
                        ve.wait_ge(S["hi"], i + 1)
                        ve.wait_ge(S[have], 2 if i == 0 else 1)
                        ve.tensor_tensor(r1[:, i, :], qk_s[:, i, :], part[:, 0, 0:L], ALU.subtract).then_inc(S["res1"], 1)
                    for i, part in enumerate((sp_q, sp_k)):
                        ve.wait_ge(S["mid"], i + 1)
                        ve.wait_ge(S["res1"], i + 1)
                        ve.tensor_tensor(part[:, 2, 0:L], r1[:, i, :], part[:, 1, 0:L], ALU.subtract).then_inc(S["lo"], 1)
                    ve.wait_ge(S["dots"], 1)
                    ve.tensor_copy(nd[:, :, :, :].rearrange("p t k h -> p (t k h)"), p_q[:, 0:NT * 2 * AH]).then_inc(S["ndout"], 1)
                    ve.wait_ge(S["ndout"], 1)
                    ve.wait_ge(S["rn"], 1)
                    ve.tensor_tensor(dn[:, :, :], nd[:, :, 1, :], rn[:, :, :], ALU.mult).then_inc(S["mul"], 1)
                    ve.wait_ge(S["mul"], 1)
                    ve.tensor_reduce(K["sim"][:, bass.ds(b, 1), :].rearrange("p o t -> p (o t)"), dn[:, :, :],
                                     AX.X, ALU.add).then_inc(S["sim"], 1)

                @block.tensor
                def _(pe):
                    pe.wait_ge(S["normed"], NT)
                    for t in range(NT):
                        i = pe.transpose(p_x[:, t * P:(t + 1) * P], xn_b[:, t, :], K["ident"][:, :])
                    i.then_inc(S["xturn"], 1)
                    pe.wait_ge(S["xT"], 1)
                    for s, (pt, name) in enumerate(((p_q, "qmm"), (p_k, "kmm"))):
                        for h in range(2):
                            i = pe.matmul(pt[:, h * HALF:(h + 1) * HALF], K["wqk"][:, s, :],
                                          xn_Tb[:, h * HALF:(h + 1) * HALF], start=True, stop=True)
                        i.then_inc(S[name], 1)
                    pe.wait_ge(S["copyT"], 1)
                    for t in range(NT):
                        i = pe.matmul(p_x[:, t * P:(t + 1) * P], xn_Tb[:, t * P:(t + 1) * P], K["wqkv"][:, 2, :],
                                      start=True, stop=True)
                    i.then_inc(S["vmm"], 1)
                    pe.wait_ge(S["normed"], 2 * NT)
                    for t in range(NT):
                        i = pe.transpose(p_h[:, t * P:(t + 1) * P], h_b[:, t, :], K["ident"][:, :])
                    i.then_inc(S["hturn"], 1)
                    pe.wait_ge(S["qf"], 2)
                    pe.wait_ge(S["qsq"], 1)
                    for t in range(NT):
                        pe.matmul(p_q[:, (2 * t) * AH:(2 * t + 1) * AH], q_sq[:, t * P:(t + 1) * P], K["head_of"][:, :],
                                  start=True, stop=True)
                        i = pe.matmul(p_q[:, (2 * t + 1) * AH:(2 * t + 2) * AH], q_f[:, t * P:(t + 1) * P], K["gdir"][:, :],
                                      start=True, stop=True)
                    i.then_inc(S["dots"], 1)

                @block.scalar
                def _(ac):
                    ac.wait_ge(S["xturn"], 1)
                    ac.activation(xn_Tb[:, :], p_x[:, :], ACT.Copy).then_inc(S["xT"], 1)
                    ac.activation(K["xn_T"][:, bass.ds(b * L, L)], p_x[:, :], ACT.Copy).then_inc(S["copyT"], 1)
                    ac.wait_ge(S["qmm"], 1)
                    ac.activation(q_f[:, :], p_q[:, :], ACT.Copy).then_inc(S["qf"], 1)
                    ac.activation(qk_s[:, 0, :], p_q[:, :], ACT.Copy, scale=float(AD) ** -0.5).then_inc(S["qf"], 1)
                    ac.wait_ge(S["qf"], 2)
                    ac.activation(q_sq[:, :], q_f[:, :], ACT.Square).then_inc(S["qsq"], 1)
                    ac.activation(sp_q[:, 0, 0:L], qk_s[:, 0, :], ACT.Copy).then_inc(S["hi"], 1)
                    ac.wait_ge(S["kmm"], 1)
                    ac.activation(qk_s[:, 1, :], p_k[:, :], ACT.Copy).then_inc(S["ks"], 1)
                    ac.wait_ge(S["ks"], 1)
                    ac.activation(sp_k[:, 0, :], qk_s[:, 1, :], ACT.Copy).then_inc(S["hi"], 1)
                    for i, part in enumerate((sp_q, sp_k)):
                        ac.wait_ge(S["res1"], i + 1)
                        ac.activation(part[:, 1, 0:L], r1[:, i, :], ACT.Copy).then_inc(S["mid"], 1)
                    ac.wait_ge(S["vmm"], 1)
                    ac.wait_ge(S["vset"], 2)
                    for t in range(2):
                        ac.activation(v_b[:, 4 * t:4 * t + 4, :, 0:AD].rearrange("p t h e -> p (t h) e"),
                                      p_x[:, t * HALF:(t + 1) * HALF].rearrange("p (a e) -> p a e", e=AD),
                                      ACT.Copy).then_inc(S["vout"], 1)
                    ac.wait_ge(S["hturn"], 1)
                    ac.activation(K["h_T"][:, bass.ds(b * L, L)], p_h[:, :], ACT.Identity, bias=K["ln"][:, 1:2],
                                  scale=K["ln"][:, 0:1]).then_inc(S["hT"], 1)
            S.clear()


def phase_classes(nc, d, keep):
    with ExitStack() as ctx:
        sb = lambda n, s, t=fp32: ctx.enter_context(nc.sbuf_tensor(n, s, t))
        K = keep
        sim = K["sim"][:, :, :].rearrange("p b t -> p (b t)")
        ext, mm, mmr, rng = sb("c_ext", [P, 2, B * NT]), sb("c_mm", [P, 2]), sb("c_mmr", [P, 2]), sb("c_rng", [P, 2])
        pos, pos_r = sb("c_pos", [P, B * NT]), sb("c_posr", [B * NT, P])
        reg_row = sb("c_regrow", [B * NT, P])
        m = sb("c_m", [B * NT, 3, P])
        mrow = sb("c_mrow", [B * NT, 4, P], bf16)
        ex0, ex1 = sb("c_ex0", [B, EXTRA], bf16), sb("c_ex1", [B, EXTRA], bf16)
        pT = ctx.enter_context(nc.psum_tensor("c_pT", [P, HALF], fp32))
        S = Signals(nc, ctx, "c", "load red all v turn rows st ex")
        with nc.Block() as block:
            @block.sync
            def _(sp):
                sp.dma_start(reg_row[:, :], d["reg_row"]).then_inc(S["load"], 16)
                sp.wait_ge(S["ex"], 2)
                sp.dma_start(d["q_mask"][0, :, L:QW], ex0[:, :]).then_inc(S["st"], 16)
                sp.dma_start(d["q_mask"][1, :, L:QW], ex1[:, :]).then_inc(S["st"], 16)
                sp.wait_ge(S["rows"], 4)
                for r in range(4):
                    dst = (d["k_mask"], d["q_mask"])[r // 2]
                    sp.dma_start(dst[r % 2, :, 0:L].rearrange("b (t p) -> b t p", p=P), mrow[:, r, :]).then_inc(S["st"], 16)
                sp.wait_ge(S["st"], 16 * 6)

            @block.vector
            def _(ve):
                c = Chain(ve, S["v"])
                ve.memset(ex0[:, :], 0.0).then_inc(S["ex"], 1)
                ve.memset(ex1[:, :], 1.0).then_inc(S["ex"], 1)
                c.step(ve.scalar_tensor_tensor(ext[:, 0, :], K["reg_tok"][:, :], -BIG, sim, ALU.mult, ALU.add))
                c.step(ve.scalar_tensor_tensor(ext[:, 1, :], K["reg_tok"][:, :], BIG, sim, ALU.mult, ALU.add))
                c.wait()
                c.step(ve.tensor_reduce(mm[:, 0:1], ext[:, 0, :], AX.X, ALU.max))
                c.step(ve.tensor_reduce(mm[:, 1:2], ext[:, 1, :], AX.X, ALU.min, negate=True))
                c.wait()
                ve.engine_nop().then_inc(S["red"], 1)
                ve.wait_ge(S["all"], 1)
                c.step(ve.tensor_tensor(rng[:, 0:1], mmr[:, 0:1], mmr[:, 1:2], ALU.add))
                c.wait()
                c.step(ve.reciprocal(rng[:, 1:2], rng[:, 0:1]))
                c.wait()
                c.step(ve.tensor_scalar(pos[:, :], sim, mmr[:, 1:2], rng[:, 1:2], ALU.add, ALU.mult))
                c.wait()
                c.step(ve.tensor_scalar(pos[:, :], pos[:, :], 0.9, None, ALU.is_gt))
                c.wait()
                ve.engine_nop().then_inc(S["red"], 1)
                ve.wait_ge(S["turn"], 1)
                c.step(ve.tensor_copy(pos_r[:, :], pT[0:B * NT, 0:P]))
                ve.wait_ge(S["load"], 16)
                c.wait()
                c.step(ve.tensor_tensor(m[:, 0, :], pos_r[:, :], reg_row[:, :], ALU.max))
                c.step(ve.tensor_scalar(m[:, 1, :], reg_row[:, :], BIG, -BIG, ALU.mult, ALU.add))
                c.wait()
                ve.tensor_copy(mrow[:, 2, :], m[:, 0, :]).then_inc(S["rows"], 1)
                ve.tensor_scalar(mrow[:, 3, :], m[:, 0, :], -1.0, 1.0, ALU.mult, ALU.add).then_inc(S["rows"], 1)
                ve.tensor_tensor(mrow[:, 1, :], m[:, 1, :], m[:, 0, :], ALU.mult).then_inc(S["rows"], 1)
                c.step(ve.tensor_scalar(m[:, 2, :], m[:, 0, :], -1.0, 1.0, ALU.mult, ALU.add))
                c.wait()
                ve.tensor_tensor(mrow[:, 0, :], m[:, 1, :], m[:, 2, :], ALU.mult).then_inc(S["rows"], 1)

            @block.gpsimd
            def _(po):
                po.wait_ge(S["red"], 1)
                po.partition_all_reduce(mmr[:, :], mm[:, :], P, bass.bass_isa.ReduceOp.max).then_inc(S["all"], 1)

            @block.tensor
            def _(pe):
                pe.wait_ge(S["red"], 2)
                pe.transpose(pT[0:B * NT, 0:P], pos[:, :], K["ident"][:, :]).then_inc(S["turn"], 1)
        S.clear()


def attention_order():
    span, lag = 33, 5
    jobs = []
    for g in range(NG):
        t0 = g * span
        jobs += [(t0 + i / 2, 0, "max", g, i) for i in range(2 * AG * NT + 2)]
        jobs += [(t0 + span, 1, "maxima", g, 0)]
        t1 = t0 + span + lag
        jobs += [(t1 + n, 2, "score", g, n) for n in range(span)]
        jobs += [(t1 + n + 2, 3, "sum", g, n) for n in range(span)]
        for u, n in enumerate((16, 32, 33)):
            jobs += [(t1 + n + 2.1, 4, "take", g, u), (t1 + n + 4.2, 5, "turn", g, u)]
    return [j[2:] for j in sorted(jobs)]


def phase_attention(nc, d, keep):
    K = keep
    QK = 9 * AD + 2
    LOADS = 3 * (1 + 3 + 3) + 3
    order = attention_order()
    ring = [j for j in order if j[0] in ("max", "maxima", "turn")]
    small_no = {j: k for k, j in enumerate(ring)}
    turn_no = [small_no[("turn", g, u)] for g in range(NG) for u in range(3)]
    score_no = {j[1:]: k for k, j in enumerate([j for j in order if j[0] == "score"])}
    with ExitStack() as ctx:
        sb = lambda n, s, t=fp32: ctx.enter_context(nc.sbuf_tensor(n, s, t))
        ps = lambda n, s, t=fp32: ctx.enter_context(nc.psum_tensor(n, s, t))
        qb = [sb(f"b_q{g}", [P, AG, L], bf16) for g in range(NG)]
        qx = [sb(f"b_qx{g}", [P, AG, EXTRA], bf16) for g in range(NG)]
        kb = [sb(f"b_k{g}", [P, AG, L], bf16) for g in range(NG)]
        v_b = sb("b_v", [P, NT, AH, 32])
        probs = sb("b_probs", [P, 4, 2 * HALF])
        mpart = sb("b_mpart", [P, 2, AG * NT + 1, 2])
        negm = sb("b_negm", [P, 2, AG * NT + 1])
        m_row = sb("b_mrow", [AG * NT + 1, P])
        m_res = sb("b_mres", [AG * NT + 1, 2, P])
        m_parts = sb("b_mparts", [AG * NT + 1, 2, 3, P], bf16)
        o_sb = sb("b_o", [P, 2, HALF])
        rec = sb("b_rec", [P, 4 * AG])
        ex = sb("b_ex", [EXTRA, AG, AD])
        att = sb("b_att", [P, NT, AH, AD])
        small = [ps(f"b_small{i}", [P, HALF]) for i in range(2)]
        score = [ps(f"b_score{i}", [P, 2 * HALF]) for i in range(2)]
        acc = [ps(f"b_acc{i}", [P, HALF]) for i in range(2)]
        S = Signals(nc, ctx, "b", "load0 load1 load2 load3 vload mput small_full small_read score_full score_read sum_done "
                    "acc_read maxp neg mrow mhi mres1 mmid mres2 mparts rec norm exn half done aturn aout ones")

        with nc.Block() as block:
            @block.gpsimd
            def _(po):
                for g in range(NG):
                    po.memset(kb[g][64:96, :, :], 1.0).then_inc(S["ones"], 1)
        S.clear()

        with nc.Fori(0, B) as b:
            with nc.Block() as block:
                @block.sync
                def _(sp):
                    for g in range(NG):
                        ld = S[f"load{g}"]
                        for r in range(3):
                            sp.dma_start(kb[g][24 * r:24 * r + 24, :, :].rearrange("e j t -> e (j t)"),
                                         d["k_parts"][bass.ds(b, 1), :, 32 * g:32 * g + 32, :].rearrange(
                                             "o s (e j) t -> (o s) e (j t)", j=AG)).then_inc(ld, 16)
                            for a in range(3):
                                sp.dma_start(qb[g][24 * r + 8 * a:24 * r + 8 * a + 8, :, :].rearrange("e j t -> e (j t)"),
                                             d["q_parts"][bass.ds(b, 1), r:r + 1, 32 * g:32 * g + 32, :].rearrange(
                                                 "o s (e j) t -> (o s e) (j t)", j=AG)).then_inc(ld, 16)
                                sp.dma_start(qx[g][24 * r + 8 * a:24 * r + 8 * a + 8, :, :],
                                             d["q_parts"][bass.ds(b, 1), r:r + 1, 32 * g:32 * g + 32, 0:EXTRA].rearrange(
                                                 "o s (e j) t -> (o s e) j t", j=AG)).then_inc(ld, 16)
                        sp.dma_start(kb[g][72:74, :, :], d["k_mask"][:, bass.ds(b, 1), :].to_broadcast([2, AG, L])).then_inc(ld, 16)
                        sp.dma_start(qb[g][72:74, :, :], d["q_mask"][:, bass.ds(b, 1), 0:L].to_broadcast([2, AG, L])).then_inc(ld, 16)
                        sp.dma_start(qx[g][72:74, :, :], d["q_mask"][:, bass.ds(b, 1), L:QW].to_broadcast([2, AG, EXTRA])).then_inc(ld, 16)
                        if g == 0:
                            sp.dma_start(v_b[:, :, :, :].rearrange("p t h e -> p (t h e)"),
                                         d["v_tiles"][bass.ds(b, 1), :, :].rearrange("o p n -> p (o n)")).then_inc(S["vload"], 16)
                    for g in range(NG):
                        sp.wait_ge(S["mparts"], g + 1)
                        for s in range(3):
                            sp.dma_start(qb[g][QK + s:QK + s + 1, :, :].rearrange("o j (t p) -> o (j t) p", p=P),
                                         m_parts[0:AG * NT, g % 2, s, :]).then_inc(S["mput"], 16)
                            sp.dma_start(qx[g][QK + s:QK + s + 1, :, :],
                                         m_parts[AG * NT:AG * NT + 1, g % 2, s, :].rearrange("o (j q) -> o j q", j=AG))\
                              .then_inc(S["mput"], 16)
                        sp.wait_ge(S["mput"], 96 * (g + 1))

                @block.tensor
                def _(pe):
                    def small_slot(job):
                        k = small_no[job]
                        if k >= 2:
                            pe.wait_ge(S["small_read"], k - 1)
                        return small[k % 2]

                    for job in order:
                        kind, g, n = job
                        if kind == "max":
                            out = small_slot(job)
                            if n == 0:
                                pe.wait_ge(S[f"load{g}"], LOADS * 16)
                            if n < 2 * AG * NT:
                                j, t, h = n // (2 * NT), n // 2 % NT, n % 2
                                i = pe.matmul(out[:, :], qb[g][0:QK, j, t * P:(t + 1) * P],
                                              kb[g][0:QK, j, h * HALF:(h + 1) * HALF], start=True, stop=True)
                            else:
                                h = n % 2
                                for j in range(AG):
                                    i = pe.matmul(out[32 * j:32 * j + 32, :], qx[g][0:QK, j, :],
                                                  kb[g][0:QK, j, h * HALF:(h + 1) * HALF], start=True, stop=True)
                            i.then_inc(S["small_full"], 1)
                        elif kind == "maxima":
                            out = small_slot(job)
                            pe.wait_ge(S["neg"], g + 1)
                            pe.transpose(out[0:AG * NT + 1, 0:P], negm[:, g % 2, :], K["ident"][:, :])\
                              .then_inc(S["small_full"], 1)
                        elif kind == "score":
                            m = score_no[(g, n)]
                            if n == 0:
                                pe.wait_ge(S["mput"], 96 * (g + 1))
                            if m >= 2:
                                pe.wait_ge(S["score_read"], m - 1)
                            out = score[m % 2]
                            if n < 32:
                                h, t, pair = n // 16, n % 16 // 2, n % 2
                                for i in range(2):
                                    j = 2 * pair + i
                                    mm = pe.matmul(out[:, i * HALF:(i + 1) * HALF], kb[g][0:ROWS, j, t * P:(t + 1) * P],
                                                   qb[g][0:ROWS, j, h * HALF:(h + 1) * HALF], start=True, stop=True)
                            else:
                                for t in range(NT):
                                    for j in range(AG):
                                        c = (t * AG + j) * EXTRA
                                        mm = pe.matmul(out[:, c:c + EXTRA], kb[g][0:ROWS, j, t * P:(t + 1) * P],
                                                       qx[g][0:ROWS, j, :], start=True, stop=True)
                            mm.then_inc(S["score_full"], 1)
                        elif kind == "sum":
                            m = score_no[(g, n)]
                            if m == 0:
                                pe.wait_ge(S["vload"], 16)
                            pe.wait_ge(S["score_read"], m + 1)
                            a = 3 * g + n // 16
                            out = acc[a % 2]
                            if n % 16 == 0 and a >= 2:
                                pe.wait_ge(S["acc_read"], a - 1)
                            if n < 32:
                                t, pair = n % 16 // 2, n % 2
                                for i in range(2):
                                    j = 2 * pair + i
                                    mm = pe.matmul(out[32 * j:32 * j + 32, :], v_b[:, t, AG * g + j, :],
                                                   probs[:, m % 4, i * HALF:(i + 1) * HALF], start=(t == 0), stop=(t == NT - 1))
                            else:
                                for t in range(NT):
                                    for j in range(AG):
                                        c = (t * AG + j) * EXTRA
                                        mm = pe.matmul(out[32 * j:32 * j + 32, 0:EXTRA], v_b[:, t, AG * g + j, :],
                                                       probs[:, m % 4, c:c + EXTRA], start=(t == 0), stop=(t == NT - 1))
                            mm.then_inc(S["sum_done"], 1)
                        elif kind == "turn":
                            out = small_slot(job)
                            a = 3 * g + n
                            pe.wait_ge(S["acc_read"], a + 1)
                            if n < 2:
                                for t in range(4):
                                    mm = pe.transpose(out[:, t * P:(t + 1) * P], o_sb[:, a % 2, t * P:(t + 1) * P], K["ident"][:, :])
                            else:
                                mm = pe.transpose(out[0:EXTRA, 0:P], o_sb[:, a % 2, 0:EXTRA], K["ident"][:, :])
                            mm.then_inc(S["small_full"], 1)
                    pe.wait_ge(S["half"], NG)
                    for t in range(NT):
                        mm = pe.transpose(score[0][:, t * P:(t + 1) * P], att[:, t, :, :].rearrange("p h e -> p (h e)"),
                                          K["ident"][:, :])
                    mm.then_inc(S["aturn"], 1)

                @block.scalar
                def _(ac):
                    for kind, g, n in order:
                        if kind == "score":
                            m = score_no[(g, n)]
                            ac.wait_ge(S["score_full"], m + 1)
                            if m >= 4:
                                ac.wait_ge(S["sum_done"], m - 3)
                            ac.activation(probs[:, m % 4, :], score[m % 2][:, :], ACT.Exp).then_inc(S["score_read"], 1)
                        elif kind == "take":
                            a = 3 * g + n
                            ac.wait_ge(S["sum_done"], 33 * g + (16, 32, 33)[n])
                            if a >= 2:
                                ac.wait_ge(S["small_full"], turn_no[a - 2] + 1)
                            w = HALF if n < 2 else EXTRA
                            ac.activation(o_sb[:, a % 2, 0:w], acc[a % 2][:, 0:w], ACT.Copy).then_inc(S["acc_read"], 1)
                    ac.wait_ge(S["aturn"], 1)
                    ac.activation(K["at_T"][:, bass.ds(b * L, L)], score[0][:, :], ACT.Copy).then_inc(S["aout"], 1)

                @block.vector
                def _(ve):
                    for job in order:
                        kind, g, n = job
                        if kind in ("max", "maxima", "turn"):
                            k = small_no[job]
                            src = small[k % 2]
                        if kind == "max":
                            i, h = n // 2, n % 2
                            ve.wait_ge(S["small_full"], k + 1)
                            if n == 0 and g >= 2:
                                ve.wait_ge(S["neg"], g - 1)
                            ve.tensor_reduce(mpart[:, g % 2, i, h:h + 1], src[:, :], AX.X, ALU.max).then_inc(S["small_read"], 1)
                            if n == 2 * AG * NT + 1:
                                ve.wait_ge(S["small_read"], k + 1)
                                ve.tensor_reduce(negm[:, g % 2, :], mpart[:, g % 2, :, :], AX.X, ALU.max, negate=True)\
                                  .then_inc(S["neg"], 1)
                        elif kind == "maxima":
                            ve.wait_ge(S["small_full"], k + 1)
                            ve.tensor_copy(m_row[:, :], src[0:AG * NT + 1, 0:P]).then_inc(S["small_read"], 1)
                            ve.wait_ge(S["small_read"], k + 1)
                            if g >= 2:
                                ve.wait_ge(S["mput"], 96 * (g - 1))
                            ve.tensor_copy(m_parts[:, g % 2, 0, :], m_row[:, :]).then_inc(S["mhi"], 1)
                            ve.wait_ge(S["mhi"], g + 1)
                            ve.tensor_tensor(m_res[:, 0, :], m_row[:, :], m_parts[:, g % 2, 0, :], ALU.subtract).then_inc(S["mres1"], 1)
                            ve.wait_ge(S["mres1"], g + 1)
                            ve.tensor_copy(m_parts[:, g % 2, 1, :], m_res[:, 0, :]).then_inc(S["mmid"], 1)
                            ve.wait_ge(S["mmid"], g + 1)
                            ve.tensor_tensor(m_parts[:, g % 2, 2, :], m_res[:, 0, :], m_parts[:, g % 2, 1, :], ALU.subtract)\
                              .then_inc(S["mparts"], 1)
                        elif kind == "turn":
                            ve.wait_ge(S["small_full"], k + 1)
                            a = 3 * g + n
                            q, w = (P, 4) if n < 2 else (EXTRA, 1)
                            v = src[0:q, 0:w * P].rearrange("p (a e) -> p a e", e=32)
                            if a >= 1:
                                ve.wait_ge(S["small_read"], turn_no[a - 1] + 1)
                            ve.reciprocal(rec[0:q, 0:w * AG], v[:, :, AD]).then_inc(S["rec"], 1)
                            ve.wait_ge(S["rec"], a + 1)
                            r = rec[0:q, 0:w * AG].rearrange("p (a o) -> p a o", o=1)
                            if n < 2:
                                dst = att[:, 4 * n:4 * n + 4, AG * g:AG * g + AG, :]
                                ve.tensor_tensor(dst, src[:, :].rearrange("p (t j e) -> p t j e", t=4, j=AG)[:, :, :, 0:AD],
                                                 rec[:, :].rearrange("p (t j o) -> p t j o", t=4, o=1).to_broadcast([P, 4, AG, AD]),
                                                 ALU.mult).then_inc(S["small_read"], 1)
                            else:
                                ve.tensor_tensor(ex[:, :, :], v[:, :, 0:AD], r.to_broadcast([EXTRA, AG, AD]), ALU.mult)\
                                  .then_inc(S["small_read"], 1)
                                ve.wait_ge(S["half"], g) if g else None
                                ve.wait_ge(S["small_read"], k + 1)
                                reg = att[0:REG, 0, AG * g:AG * g + AG, :]
                                ve.tensor_tensor(reg, reg, ex[0:REG, :, :], ALU.add).then_inc(S["exn"], 1)
                                ve.wait_ge(S["exn"], g + 1)
                                ve.tensor_scalar(reg, reg, 0.5, None, ALU.mult).then_inc(S["half"], 1)
            S.clear()


def phase_mamba(nc, d, keep):
    K = keep
    W = DC - 1
    CH = 2
    NCH = DS // CH
    with ExitStack() as ctx:
        sb = lambda n, s, t=fp32: ctx.enter_context(nc.sbuf_tensor(n, s, t))
        ps = lambda n, s, t=fp32: ctx.enter_context(nc.psum_tensor(n, s, t))
        w_in = sb("m_win", [P, 2, 2 * DI])
        w_x = sb("m_wx", [P, 2, DR + 2 * DS])
        w_dt = sb("m_wdt", [DR, 2, DI])
        w_out = sb("m_wout", [P, 2, DM])
        w_conv = sb("m_wconv", [P, 2, DC])
        a_log, a_neg = sb("m_alog", [P, 2, DS]), sb("m_aneg", [P, 2, DS])
        vec = sb("m_vec", [P, 2, 3])
        x_pad = sb("m_xpad", [P, 2, L + W])
        conv = sb("m_conv", [P, 2, L])
        xs, zs = sb("m_xs", [P, 2, L]), sb("m_zs", [P, 2, L])
        dt, dtx = sb("m_dt", [P, 2, L]), sb("m_dtx", [P, 2, L])
        dbc = sb("m_dbc", [DR + 2 * DS, 2, L])
        bc = sb("m_bc", [P, 2, 2, CH, L])
        da, dbx = sb("m_da", [P, 2, L]), sb("m_dbx", [P, 2, L])
        hs, hc = sb("m_hs", [P, 2, L]), sb("m_hc", [P, 2, L])
        ob = dt[:, 0, :]
        z = [ps(f"m_z{i}", [P, L]) for i in range(2)]
        y = [ps(f"m_y{i}", [P, L]) for i in range(2)]
        S = Signals(nc, ctx, "m", "load expA a pad xmm xcp zmm zcp cv xs dbcmm dbccp rowput dtmm dtz dabs dexp dln dt dtx "
                    "bc0 bc1 da dbx h hc ysum y1 y2 omm ocp mo")
        with nc.Block() as block:
            @block.sync
            def _(sp):
                n = 0
                for i in range(2):
                    q = f"m{i + 1}_"
                    col = lambda a: a.rearrange("(c o) -> c o", o=1)
                    for dst, src in ((w_in[:, i, :], d[q + "Win"]), (w_x[:, i, :], d[q + "Wx"]),
                                     (w_dt[:, i, :], d[q + "Wdt"]), (w_out[:, i, :], d[q + "Wout"]),
                                     (w_conv[:, i, :], d[q + "Wconv"]), (a_log[:, i, :], d[q + "Alog"]),
                                     (vec[:, i, 0:1], col(d[q + "bconv"])), (vec[:, i, 1:2], col(d[q + "bdt"])),
                                     (vec[:, i, 2:3], col(d[q + "Dp"]))):
                        sp.dma_start(dst, src).then_inc(S["load"], 16)
                        n += 16
                sp.wait_ge(S["load"], n)

            @block.scalar
            def _(ac):
                ac.wait_ge(S["load"], 16 * 18)
                ac.activation(a_neg[:, :, :], a_log[:, :, :], ACT.Exp).then_inc(S["expA"], 1)

            @block.vector
            def _(ve):
                ve.wait_ge(S["expA"], 1)
                ve.tensor_scalar(a_neg[:, :, :], a_neg[:, :, :], -1.0, None, ALU.mult).then_inc(S["a"], 1)
                ve.memset(x_pad[:, 0, 0:W], 0.0).then_inc(S["pad"], 1)
                ve.memset(x_pad[:, 1, L:L + W], 0.0).then_inc(S["pad"], 1)
        S.clear()

        with nc.Fori(0, B) as b:
            with nc.Block() as block:
                @block.sync
                def _(sp):
                    rows = d["bc_rows"]
                    for i in range(2):
                        sp.wait_ge(S["dbccp"], i + 1)
                        sp.dma_start(rows[i], dbc[:, i, :]).then_inc(S["rowput"], 16)
                    for i in range(2):
                        if i == 0:
                            sp.wait_ge(S["rowput"], 32)
                        for c in range(NCH):
                            k = i * NCH + c
                            if k >= 2:
                                sp.wait_ge(S["hc"], CH * (k - 1))
                                sp.wait_ge(S["dbx"], CH * (k - 1))
                            for r in range(2):
                                r0 = DR + r * DS + c * CH
                                sp.dma_start(bc[:, k % 2, r, :, :], rows[i, r0:r0 + CH, :].rearrange(
                                    "(o n) t -> o n t", o=1).to_broadcast([P, CH, L])).then_inc(S[f"bc{k % 2}"], 16)

                @block.tensor
                def _(pe):
                    h_b = lambda h: K["h_T"][:, bass.ds(b * L + h * HALF, HALF)]
                    for i in range(2):
                        if i == 1:
                            pe.wait_ge(S["dtz"], 1)
                        for h in range(2):
                            mm = pe.matmul(z[0][:, h * HALF:(h + 1) * HALF], w_in[:, i, 0:DI], h_b(h), start=True, stop=True)
                        mm.then_inc(S["xmm"], 1)
                        if i == 1:
                            pe.wait_ge(S["dbccp"], 1)
                        for h in range(2):
                            mm = pe.matmul(z[1][:, h * HALF:(h + 1) * HALF], w_in[:, i, DI:2 * DI], h_b(h), start=True, stop=True)
                        mm.then_inc(S["zmm"], 1)
                        pe.wait_ge(S["zcp"], i + 1)
                        pe.wait_ge(S["xs"], i + 1)
                        for h in range(2):
                            mm = pe.matmul(z[1][0:DR + 2 * DS, h * HALF:(h + 1) * HALF], w_x[:, i, :],
                                           xs[:, i, h * HALF:(h + 1) * HALF], start=True, stop=True)
                        mm.then_inc(S["dbcmm"], 1)
                        pe.wait_ge(S["dbccp"], i + 1)
                        pe.wait_ge(S["xcp"], i + 1)
                        for h in range(2):
                            mm = pe.matmul(z[0][:, h * HALF:(h + 1) * HALF], w_dt[:, i, :],
                                           dbc[0:DR, i, h * HALF:(h + 1) * HALF], start=True, stop=True)
                        mm.then_inc(S["dtmm"], 1)
                    for i in range(2):
                        for n in range(DS):
                            pe.wait_ge(S["hc"], i * DS + n + 1)
                            for h in range(2):
                                mm = pe.matmul(y[i][:, h * HALF:(h + 1) * HALF], K["ident"][:, :],
                                               hc[:, n % 2, h * HALF:(h + 1) * HALF], start=(n == 0), stop=(n == DS - 1))
                            mm.then_inc(S["ysum"], 1)
                        pe.wait_ge(S["y2"], i + 1)
                        if i == 0:
                            pe.wait_ge(S["dtz"], 2)
                        for h in range(2):
                            mm = pe.matmul(z[0][DM * i:DM * i + DM, h * HALF:(h + 1) * HALF], w_out[:, i, :],
                                           conv[:, i, h * HALF:(h + 1) * HALF], start=True, stop=True)
                        mm.then_inc(S["omm"], 1)

                @block.scalar
                def _(ac):
                    for i in range(2):
                        rev = slice(None) if i == 0 else slice(None, None, -1)
                        ac.wait_ge(S["xmm"], i + 1)
                        off = W if i == 0 else 0
                        ac.activation(x_pad[:, i, off:off + L], z[0][:, :], ACT.Copy).then_inc(S["xcp"], 1)
                        ac.wait_ge(S["zmm"], i + 1)
                        ac.activation(zs[:, i, rev], z[1][:, :], ACT.Silu).then_inc(S["zcp"], 1)
                        ac.wait_ge(S["cv"], DC * (i + 1))
                        ac.activation(xs[:, i, rev], conv[:, i, :], ACT.Silu, bias=vec[:, i, 0:1]).then_inc(S["xs"], 1)
                        ac.wait_ge(S["dbcmm"], i + 1)
                        ac.activation(dbc[:, i, :], z[1][0:DR + 2 * DS, :], ACT.Copy).then_inc(S["dbccp"], 1)
                    for i in range(2):
                        ac.wait_ge(S["dabs"], i + 1)
                        ac.activation(dtx[:, i, :], dtx[:, i, :], ACT.Exp, scale=-1.0).then_inc(S["dexp"], 1)
                        ac.wait_ge(S["dexp"], i + 1)
                        ac.activation(dtx[:, i, :], dtx[:, i, :], ACT.Ln, bias=1.0).then_inc(S["dln"], 1)
                    for i in range(2):
                        ac.wait_ge(S["dt"], i + 1)
                        for n in range(DS):
                            k = i * DS + n
                            if k >= 2:
                                ac.wait_ge(S["h"], k - 1)
                            ac.activation(da[:, k % 2, :], dt[:, i, :], ACT.Exp, scale=a_neg[:, i, n:n + 1]).then_inc(S["da"], 1)
                    ac.wait_ge(S["da"], 2 * DS)
                    for i in range(2):
                        ac.wait_ge(S["omm"], i + 1)
                        ac.activation(ob[DM * i:DM * i + DM, :], z[0][DM * i:DM * i + DM, :], ACT.Copy).then_inc(S["ocp"], 1)

                @block.vector
                def _(ve):
                    for i in range(2):
                        ve.wait_ge(S["xcp"], i + 1)
                        tap = lambda k: x_pad[:, i, k:k + L] if i == 0 else x_pad[:, i, W - k:W - k + L]
                        ve.tensor_scalar(conv[:, i, :], tap(0), w_conv[:, i, 0:1], None, ALU.mult).then_inc(S["cv"], 1)
                        for k in range(1, DC):
                            ve.wait_ge(S["cv"], DC * i + k)
                            ve.scalar_tensor_tensor(conv[:, i, :], tap(k), w_conv[:, i, k:k + 1], conv[:, i, :],
                                                    ALU.mult, ALU.add).then_inc(S["cv"], 1)
                        ve.wait_ge(S["dtmm"], i + 1)
                        ve.tensor_scalar(dt[:, i, :], z[0][:, :], vec[:, i, 1:2], None, ALU.add).then_inc(S["dtz"], 1)
                        ve.wait_ge(S["dtz"], i + 1)
                        ve.scalar_tensor_tensor(dtx[:, i, :], dt[:, i, :], -1.0, dt[:, i, :], ALU.mult, ALU.max).then_inc(S["dabs"], 1)
                    for i in range(2):
                        ve.wait_ge(S["dln"], i + 1)
                        ve.scalar_tensor_tensor(dt[:, i, :], dt[:, i, :], 0.0, dtx[:, i, :], ALU.max, ALU.add).then_inc(S["dt"], 1)
                        ve.wait_ge(S["dt"], i + 1)
                        ve.tensor_tensor(dtx[:, i, :], dt[:, i, :], xs[:, i, :], ALU.mult).then_inc(S["dtx"], 1)
                    ve.wait_ge(S["dtx"], 2)
                    for i in range(2):
                        for n in range(DS):
                            k = i * DS + n
                            kc = k // CH
                            if n % CH == 0:
                                ve.wait_ge(S[f"bc{kc % 2}"], 32 * (kc // 2 + 1))
                            ve.tensor_tensor(dbx[:, k % 2, :], dtx[:, i, :], bc[:, kc % 2, 0, n % CH, :], ALU.mult).then_inc(S["dbx"], 1)
                            ve.wait_ge(S["dbx"], k + 1)
                            ve.wait_ge(S["da"], k + 1)
                            if k >= 2:
                                ve.wait_ge(S["hc"], k - 1)
                            ve.tensor_tensor_scan(hs[:, k % 2, :], da[:, k % 2, :], dbx[:, k % 2, :], 0.0, ALU.mult, ALU.add)\
                              .then_inc(S["h"], 1)
                        ve.wait_ge(S["ysum"], DS * (i + 1))
                        ve.scalar_tensor_tensor(conv[:, i, :], xs[:, i, :], vec[:, i, 2:3], y[i][:, :], ALU.mult, ALU.add)\
                          .then_inc(S["y1"], 1)
                        ve.wait_ge(S["y1"], i + 1)
                        ve.tensor_tensor(conv[:, i, :], conv[:, i, :], zs[:, i, :], ALU.mult).then_inc(S["y2"], 1)
                    ve.wait_ge(S["ocp"], 2)
                    ve.tensor_tensor(K["mo_T"][:, bass.ds(b * L, L)], ob[:, :], K["xn_T"][:, bass.ds(b * L, L)], ALU.add)\
                      .then_inc(S["mo"], 1)

                @block.gpsimd
                def _(po):
                    for k in range(2 * DS):
                        kc = k // CH
                        po.wait_ge(S["h"], k + 1)
                        po.wait_ge(S[f"bc{kc % 2}"], 32 * (kc // 2 + 1))
                        if k >= 2:
                            po.wait_ge(S["ysum"], k - 1)
                        nc.gpsimd.tensor_tensor(hc[:, k % 2, :], hs[:, k % 2, :], bc[:, kc % 2, 1, k % CH, :], ALU.mult)\
                          .then_inc(S["hc"], 1)
            S.clear()


def phase_combine(nc, d, keep):
    K = keep
    with ExitStack() as ctx:
        sb = lambda n, s, t=fp32: ctx.enter_context(nc.sbuf_tensor(n, s, t))
        ps = lambda n, s, t=fp32: ctx.enter_context(nc.psum_tensor(n, s, t))
        w_proj, b_proj = sb("d_wproj", [P, P]), sb("d_bproj", [P, 1])
        gate, s0 = sb("d_gate", [P, L]), sb("d_s", [P, L])
        xn_b = sb("d_xnb", [P, NT, P])
        stats, mv, rstd = sb("d_stats", [P, NT, 6]), sb("d_mv", [P, NT, 2]), sb("d_rstd", [P, NT])
        tmp, mhalf = sb("d_tmp", [P, NT]), sb("d_mhalf", [P, NT])
        p_o, p_s, p_x = ps("d_po", [P, L]), ps("d_ps", [P, L]), ps("d_px", [P, L])
        S = Signals(nc, ctx, "d", "load proj gate act sg turn x1 stat aggr veps rstd normed xturn xT keep half")
        with nc.Block() as block:
            @block.sync
            def _(sp):
                sp.dma_start(w_proj[:, :], d["W_proj"]).then_inc(S["load"], 16)
                sp.dma_start(b_proj[:, :], d["b_proj"].rearrange("(c o) -> c o", o=1)).then_inc(S["load"], 16)
                sp.wait_ge(S["load"], 32)

            @block.gpsimd
            def _(po):
                po.memset(mhalf[:, :], -0.5).then_inc(S["half"], 1)
        S.clear()
        with nc.Fori(0, B) as b:
            with nc.Block() as block:
                x_b = flat(K["x_tok"][:, bass.ds(b, 1), :, :])
                r_b = flat(K["r_tok"][:, bass.ds(b, 1), :, :])

                @block.tensor
                def _(pe):
                    for h in range(2):
                        mm = pe.matmul(p_o[:, h * HALF:(h + 1) * HALF], w_proj[:, :],
                                       K["at_T"][:, bass.ds(b * L + h * HALF, HALF)], start=True, stop=True)
                    mm.then_inc(S["proj"], 1)
                    pe.wait_ge(S["sg"], 1)
                    for t in range(NT):
                        mm = pe.transpose(p_s[:, t * P:(t + 1) * P], gate[:, t * P:(t + 1) * P], K["ident"][:, :])
                    mm.then_inc(S["turn"], 1)
                    pe.wait_ge(S["normed"], NT)
                    for t in range(NT):
                        mm = pe.transpose(p_x[:, t * P:(t + 1) * P], xn_b[:, t, :], K["ident"][:, :])
                    mm.then_inc(S["xturn"], 1)

                @block.scalar
                def _(ac):
                    ac.activation(s0[:, :], K["mo_T"][:, bass.ds(b * L, L)], ACT.Gelu).then_inc(S["act"], 1)
                    ac.wait_ge(S["proj"], 1)
                    ac.activation(gate[:, :], p_o[:, :], ACT.Silu, bias=b_proj[:, 0:1]).then_inc(S["gate"], 1)
                    ac.wait_ge(S["xturn"], 1)
                    ac.activation(K["xn_T"][:, bass.ds(b * L, L)], p_x[:, :], ACT.Copy).then_inc(S["xT"], 1)

                @block.vector
                def _(ve):
                    ve.wait_ge(S["act"], 1)
                    ve.wait_ge(S["gate"], 1)
                    ve.tensor_tensor(gate[:, :], gate[:, :], s0[:, :], ALU.mult).then_inc(S["sg"], 1)
                    ve.wait_ge(S["turn"], 1)
                    ve.tensor_tensor(x_b.rearrange("p t c -> p (t c)"), p_s[:, :], x_b.rearrange("p t c -> p (t c)"), ALU.add)\
                      .then_inc(S["x1"], 1)
                    ve.wait_ge(S["x1"], 1)
                    token_norm(ve, S, lambda t: x_b[:, t, :], lambda t: xn_b[:, t, :], stats, mv, rstd, 1)
                    ve.wait_ge(S["normed"], NT)
                    ve.tensor_copy(r_b, xn_b[:, :, :]).then_inc(S["keep"], 1)
                    ve.tensor_copy(flat(K["xn_tok"][:, bass.ds(b, 1), :, :]), xn_b[:, :, :]).then_inc(S["keep"], 1)

                @block.gpsimd
                def _(po):
                    inverse_root(nc, po, S, mv, tmp, mhalf, rstd, 1)
            S.clear()


def phase_retention(nc, d, keep):
    K = keep
    with ExitStack() as ctx:
        sb = lambda n, s, t=fp32: ctx.enter_context(nc.sbuf_tensor(n, s, t))
        ps = lambda n, s, t=fp32: ctx.enter_context(nc.psum_tensor(n, s, t))
        xpos = sb("r_xpos", [P, 4, L])
        decay, decay_q, decay_k = sb("r_decay", [P, RH, P]), sb("r_decq", [P, P]), sb("r_deck", [P, P])
        decay_s, rblock, rhead = sb("r_decs", [P, 1]), sb("r_rblock", [P, P]), sb("r_rhead", [P, RH])
        w5 = sb("r_w5", [P, 5, RH, RD])
        w_g, w_o = sb("r_wg", [P, P]), sb("r_wo", [P, P])
        w_1, w_2 = sb("r_w1", [P, FFN]), sb("r_w2", [P, FFN // P, P])
        vec, b_1, b_2 = sb("r_vec", [P, 6]), sb("r_b1", [P, FFN // P]), sb("r_b2", [P, P])
        epsc, mhalf = sb("r_eps", [P, 1]), sb("r_mhalf", [P, NT])
        stats, mv, rstd, tmp = sb("r_stats", [P, NT, 6]), sb("r_mv", [P, NT, 2]), sb("r_rstd", [P, NT]), sb("r_tmp", [P, NT])
        xn, xnT = sb("r_xn", [P, NT, P]), sb("r_xnT", [P, L])
        qT, kT, rt = sb("r_qT", [P, L]), sb("r_kT", [P, L]), sb("r_rt", [P, 2, L])
        q_all = sb("r_qall", [P, NT, RH, P])
        qd, kd, v, gT = sb("r_qd", [P, L]), sb("r_kd", [P, NT, P]), sb("r_v", [P, NT, P]), sb("r_gT", [P, L])
        kv, state, a = sb("r_kv", [P, NT, P]), sb("r_state", [P, NT, P]), sb("r_a", [P, 2, RH, P])
        yc, ysq, gst = sb("r_yc", [P, NT * P]), sb("r_ysq", [P, NT * P]), sb("r_gst", [P, 3, NT * RH])
        gy = sb("r_gy", [P, L])
        hT = q_all[:, :, :, :].rearrange("p c h n -> p (c h n)")[:, 0:FFN // P * L].rearrange("p (f t) -> p f t", t=L)
        pA, pB, pC, pD = (ps(f"r_p{i}", [P, L]) for i in range(4))
        S = Signals(nc, ctx, "r", "load wload neg const stat aggr veps rstd normed turn xT qmm qrmm kmm krmm vmm gmm rope q k vcp g qz qd "
                    "kturn kd kvmm kvm st0 state score dec y ysum mean yc sq var sqrt gr yn yturn ynT gy omm x2 h hs f2 x3 pre")
        with nc.Block() as block:
            @block.sync
            def _(sp):
                loads = ((xpos, "xpos"), (decay, "decay"), (decay_q, "decay_q"), (decay_k, "decay_k"),
                         (decay_s, "decay_s"), (rblock, "rblock"), (rhead, "rhead"))
                for t, n in loads:
                    sp.dma_start(t[:, :, :] if len(t.shape) == 3 else t[:, :], d[n]).then_inc(S["load"], 16)
                sp.wait_ge(S["load"], 16 * len(loads))

            @block.vector
            def _(ve):
                ve.memset(epsc[:, :], EPS).then_inc(S["const"], 1)
                ve.memset(mhalf[:, :], -0.5).then_inc(S["const"], 1)
                ve.memset(state[:, 0, :], 0.0).then_inc(S["const"], 1)
        S.clear()
        with nc.Fori(0, RL) as layer:
            row = lambda n: d[n][bass.ds(layer, 1), :]
            with nc.Block() as block:
                @block.sync
                def _(sp):
                    one = lambda n: d[n][bass.ds(layer, 1), :, :].rearrange("o a c -> (o a) c")
                    loads = [(w5[:, s, :, :], d[n][bass.ds(layer, 1), :, :, :].rearrange("o h c k -> c (o h) k"))
                             for s, n in ((0, "r_WQ"), (2, "r_WK"), (4, "r_WV"))]
                    loads += [(w_g[:, :], one("r_WG")), (w_o[:, :], one("r_WO")), (w_1[:, :], one("r_ffn_w1")),
                              (w_2[:, :, :], d["r_ffn_w2"][bass.ds(layer, 1), :, :].rearrange("o (f p) c -> p (o f) c", p=P)),
                              (b_2[:, :], row("r_ffn_b2").to_broadcast([P, P]))]
                    cols = [(vec[:, i:i + 1], row("r_" + n).rearrange("o (c u) -> c (o u)", u=1))
                            for i, n in enumerate(("ln1_w", "ln1_b", "ln2_w", "ln2_b", "gn_w", "gn_b"))]
                    cols += [(b_1[:, f:f + 1], row("r_ffn_b1")[:, f * P:(f + 1) * P].rearrange("o (c u) -> c (o u)", u=1))
                             for f in range(FFN // P)]
                    for dst, src in loads + cols:
                        sp.dma_start(dst, src).then_inc(S["wload"], 16)
                    sp.wait_ge(S["wload"], 16 * len(loads + cols))

                @block.vector
                def _(ve):
                    ve.wait_ge(S["wload"], 16 * 18)
                    for s in (0, 2):
                        pair = lambda u, o: w5[:, u, :, :].rearrange("c h (i o) -> c (h i) o", o=2)[:, :, o]
                        ve.tensor_scalar(pair(s + 1, 0), pair(s, 1), -1.0, None, ALU.mult).then_inc(S["neg"], 1)
                        ve.tensor_copy(pair(s + 1, 1), pair(s, 0)).then_inc(S["neg"], 1)
            S.clear()
            with nc.Fori(0, B) as b:
                with nc.Block() as block:
                    x_b = flat(K["r_tok"][:, bass.ds(b, 1), :, :])
                    x_f = x_b.rearrange("p t c -> p (t c)")
                    halves = [(h, slice(h * HALF, (h + 1) * HALF)) for h in range(2)]
                    tiles = [slice(t * P, (t + 1) * P) for t in range(NT)]
                    w = lambda s: w5[:, s, :, :].rearrange("c h k -> c (h k)")

                    @block.tensor
                    def _(pe):
                        def project(out, lhsT, rhs, sig):
                            for _, s in halves:
                                mm = pe.matmul(out[:, s], lhsT, rhs[:, s], start=True, stop=True)
                            mm.then_inc(S[sig], 1)

                        def turn(out, src, sig):
                            for t in range(NT):
                                mm = pe.transpose(out[:, tiles[t]], src(t), K["ident"][:, :])
                            mm.then_inc(S[sig], 1)

                        pe.wait_ge(S["normed"], NT)
                        turn(pA, lambda t: xn[:, t, :], "turn")
                        pe.wait_ge(S["xT"], 1)
                        project(pB, w(0), xnT, "qmm")
                        project(pC, w(1), xnT, "qrmm")
                        for t in range(NT):
                            mm = pe.matmul(pD[:, tiles[t]], xnT[:, tiles[t]], w(4), start=True, stop=True)
                        mm.then_inc(S["vmm"], 1)
                        project(pA, w_g[:, :], xnT, "gmm")
                        pe.wait_ge(S["rope"], 1)
                        project(pB, w(2), xnT, "kmm")
                        pe.wait_ge(S["rope"], 2)
                        project(pC, w(3), xnT, "krmm")
                        pe.wait_ge(S["k"], 1)
                        pe.wait_ge(S["vcp"], 1)
                        turn(pD, lambda t: kT[:, tiles[t]], "kturn")
                        pe.wait_ge(S["kd"], 1)
                        pe.wait_ge(S["g"], 1)
                        for c in range(NT):
                            mm = pe.matmul(pA[:, tiles[c]], kd[:, c, :], v[:, c, :], start=True, stop=True)
                        mm.then_inc(S["kvmm"], 1)
                        pe.wait_ge(S["qz"], RH)
                        pe.wait_ge(S["qd"], 1)
                        for c in range(NT + 1):
                            if c < NT:
                                if c >= 2:
                                    pe.wait_ge(S["dec"], c - 1)
                                out = (pB, pC)[c % 2]
                                for h, s in halves:
                                    mm = pe.matmul(out[:, s], kT[:, tiles[c]],
                                                   q_all[:, c, 4 * h:4 * h + 4, :].rearrange("p h n -> p (h n)"),
                                                   start=True, stop=True)
                                mm.then_inc(S["score"], 1)
                            if c >= 1:
                                u = c - 1
                                pe.wait_ge(S["dec"], u + 1)
                                pe.wait_ge(S["state"], NT - 1)
                                pe.matmul(pD[:, tiles[u]], qd[:, tiles[u]], state[:, u, :], start=True, stop=False,
                                          skip_group_check=True)
                                for h in range(RH):
                                    o = u * P + h * RD
                                    mm = pe.matmul(pD[:, o:o + RD], a[:, u % 2, h, :], v[:, u, h * RD:(h + 1) * RD],
                                                   start=False, stop=(h == RH - 1), skip_group_check=True)
                                mm.then_inc(S["y"], 1)
                        pe.wait_ge(S["yn"], 1)
                        turn(pA, lambda t: yc[:, tiles[t]], "yturn")
                        pe.wait_ge(S["gy"], 1)
                        for t in range(NT):
                            mm = pe.matmul(pB[:, tiles[t]], gy[:, tiles[t]], w_o[:, :], start=True, stop=True)
                        mm.then_inc(S["omm"], 1)
                        pe.wait_ge(S["normed"], 2 * NT)
                        turn(pA, lambda t: xn[:, t, :], "turn")
                        pe.wait_ge(S["xT"], 2)
                        for f in range(FFN // P):
                            if f >= 2:
                                pe.wait_ge(S["hs"], f - 1)
                            for _, s in halves:
                                mm = pe.matmul((pC, pD)[f % 2][:, s], w_1[:, f * P:(f + 1) * P], xnT[:, s], start=True, stop=True)
                            mm.then_inc(S["h"], 1)
                        pe.wait_ge(S["hs"], FFN // P)
                        for t in range(NT):
                            for f in range(FFN // P):
                                mm = pe.matmul(pA[:, tiles[t]], hT[:, f, tiles[t]], w_2[:, f, :], start=(f == 0),
                                               stop=(f == FFN // P - 1))
                        mm.then_inc(S["f2"], 1)

                    @block.scalar
                    def _(ac):
                        ac.wait_ge(S["turn"], 1)
                        ac.activation(xnT[:, :], pA[:, :], ACT.Identity, bias=vec[:, 1:2], scale=vec[:, 0:1]).then_inc(S["xT"], 1)
                        ac.wait_ge(S["vmm"], 1)
                        ac.activation(v[:, :, :].rearrange("p t c -> p (t c)"), pD[:, :], ACT.Copy).then_inc(S["vcp"], 1)
                        ac.wait_ge(S["gmm"], 1)
                        ac.activation(gT[:, :], pA[:, :], ACT.Silu).then_inc(S["g"], 1)
                        ac.wait_ge(S["q"], 1)
                        for h in range(RH):
                            ac.activation(q_all[:, :, h, :], qT[:, :].rearrange("p (c n) -> p c n", n=P), ACT.Copy,
                                          scale=rhead[:, h:h + 1]).then_inc(S["qz"], 1)
                        ac.wait_ge(S["var"], 1)
                        ac.activation(gst[:, 2, :], gst[:, 1, :], ACT.Sqrt, bias=epsc[:, 0:1], scale=1.0 / RD).then_inc(S["sqrt"], 1)
                        ac.wait_ge(S["yturn"], 1)
                        ac.activation(gy[:, :], pA[:, :], ACT.Identity, bias=vec[:, 5:6], scale=vec[:, 4:5]).then_inc(S["ynT"], 1)
                        ac.wait_ge(S["turn"], 2)
                        ac.activation(xnT[:, :], pA[:, :], ACT.Identity, bias=vec[:, 3:4], scale=vec[:, 2:3]).then_inc(S["xT"], 1)
                        for f in range(FFN // P):
                            ac.wait_ge(S["h"], f + 1)
                            ac.activation(hT[:, f, :], (pC, pD)[f % 2][:, :], ACT.Silu, bias=b_1[:, f:f + 1]).then_inc(S["hs"], 1)

                    @block.vector
                    def _(ve):
                        token_norm(ve, S, lambda t: x_b[:, t, :], lambda t: xn[:, t, :], stats, mv, rstd, 1)
                        for i, (one, two, dst, done) in enumerate((("qmm", "qrmm", qT, "q"), ("kmm", "krmm", kT, "k"))):
                            ve.wait_ge(S[one], 1)
                            if i:
                                ve.wait_ge(S["q"], 1)
                            ve.tensor_tensor(rt[:, 0, :], pB[:, :], xpos[:, 2 * i, :], ALU.mult).then_inc(S["rope"], 1)
                            ve.wait_ge(S[two], 1)
                            ve.tensor_tensor(rt[:, 1, :], pC[:, :], xpos[:, 2 * i + 1, :], ALU.mult).then_inc(S["rope"], 1)
                            ve.wait_ge(S["rope"], 2 * i + 2)
                            ve.tensor_tensor(dst[:, :], rt[:, 0, :], rt[:, 1, :], ALU.add).then_inc(S[done], 1)
                        chunks = lambda ap: ap.rearrange("p (c n) -> p c n", n=P)
                        over = lambda t: t[:, :].rearrange("p (o n) -> p o n", o=1).to_broadcast([P, NT, P])
                        ve.tensor_tensor(chunks(qd[:, :]), chunks(qT[:, :]), over(decay_q), ALU.mult).then_inc(S["qd"], 1)
                        ve.wait_ge(S["kturn"], 1)
                        ve.tensor_tensor(kd[:, :, :], chunks(pD[:, :]), over(decay_k), ALU.mult).then_inc(S["kd"], 1)
                        ve.wait_ge(S["kvmm"], 1)
                        ve.tensor_tensor(kv[:, :, :], chunks(pA[:, :]), over(rblock), ALU.mult).then_inc(S["kvm"], 1)
                        ve.wait_ge(S["kvm"], 1)
                        for c in range(NT - 1):
                            if c:
                                ve.wait_ge(S["state"], c)
                            ve.scalar_tensor_tensor(state[:, c + 1, :], state[:, c, :], decay_s[:, 0:1], kv[:, c, :],
                                                    ALU.mult, ALU.add).then_inc(S["state"], 1)
                        for c in range(NT):
                            ve.wait_ge(S["score"], c + 1)
                            if c >= 2:
                                ve.wait_ge(S["y"], c - 1)
                            ve.tensor_tensor(a[:, c % 2, :, :].rearrange("p h n -> p (h n)"), (pB, pC)[c % 2][:, :],
                                             decay[:, :, :].rearrange("p h n -> p (h n)"), ALU.mult).then_inc(S["dec"], 1)
                        heads = lambda ap: ap.rearrange("p (a e) -> p a e", e=RD)
                        wide = lambda ap: ap.rearrange("p (a o) -> p a o", o=1).to_broadcast([P, NT * RH, RD])
                        ve.wait_ge(S["y"], NT)
                        ve.tensor_reduce(gst[:, 0, :], heads(pD[:, :]), AX.X, ALU.add).then_inc(S["ysum"], 1)
                        ve.wait_ge(S["ysum"], 1)
                        ve.tensor_scalar(gst[:, 1, :], gst[:, 0, :], 1.0 / RD, None, ALU.mult).then_inc(S["mean"], 1)
                        ve.wait_ge(S["mean"], 1)
                        ve.tensor_tensor(heads(yc[:, :]), heads(pD[:, :]), wide(gst[:, 1, :]), ALU.subtract).then_inc(S["yc"], 1)
                        ve.wait_ge(S["yc"], 1)
                        ve.tensor_tensor(ysq[:, :], yc[:, :], yc[:, :], ALU.mult).then_inc(S["sq"], 1)
                        ve.wait_ge(S["sq"], 1)
                        ve.tensor_reduce(gst[:, 1, :], heads(ysq[:, :]), AX.X, ALU.add).then_inc(S["var"], 1)
                        ve.wait_ge(S["sqrt"], 1)
                        ve.reciprocal(gst[:, 0, :], gst[:, 2, :]).then_inc(S["gr"], 1)
                        ve.wait_ge(S["gr"], 1)
                        ve.tensor_tensor(heads(yc[:, :]), heads(yc[:, :]), wide(gst[:, 0, :]), ALU.mult).then_inc(S["yn"], 1)
                        ve.wait_ge(S["ynT"], 1)
                        ve.tensor_tensor(gy[:, :], gy[:, :], gT[:, :], ALU.mult).then_inc(S["gy"], 1)
                        ve.wait_ge(S["omm"], 1)
                        ve.tensor_tensor(x_f, pB[:, :], x_f, ALU.add).then_inc(S["x2"], 1)
                        ve.wait_ge(S["x2"], 1)
                        token_norm(ve, S, lambda t: x_b[:, t, :], lambda t: xn[:, t, :], stats, mv, rstd, 2)
                        ve.wait_ge(S["normed"], 2 * NT)
                        ve.tensor_tensor(x_b, x_b, over(b_2), ALU.add).then_inc(S["pre"], 1)
                        ve.wait_ge(S["pre"], 1)
                        ve.wait_ge(S["f2"], 1)
                        ve.tensor_tensor(x_f, pA[:, :], x_f, ALU.add).then_inc(S["x3"], 1)

                    @block.gpsimd
                    def _(po):
                        for n in (1, 2):
                            inverse_root(nc, po, S, mv, tmp, mhalf, rstd, n)
                S.clear()


def phase_dispatch(nc, d, keep):
    K = keep
    CW = 256
    with ExitStack() as ctx:
        sb = lambda n, s, t=fp32: ctx.enter_context(nc.sbuf_tensor(n, s, t))
        ps = lambda n, s, t=fp32: ctx.enter_context(nc.psum_tensor(n, s, t))
        mx, rs = sb("e_mx", [P, 2, CW]), sb("e_rs", [P, 2, CW])
        e, s1, s2 = sb("e_e", [P, 2, B, CW]), sb("e_s1", [P, 2, 2, CW]), sb("e_s2", [P, 2, CW])
        w = sb("e_w", [P, 2, B, CW])
        logit = [ps(f"e_l{i}", [P, B, CW]) for i in range(2)]
        gather = ps("e_g", [P, B, CW])
        S = Signals(nc, ctx, "e", "load logit mx sub exp s1 s2 rs wa wb slots out")
        with nc.Block() as block:
            @block.sync
            def _(sp):
                sp.dma_start(K["phi"][:, :], d["e_phi"].rearrange("c n p -> c (n p)")).then_inc(S["load"], 16)
                sp.dma_start(K["w_e"][:, :, :], d["e_W"].rearrange("n c e -> c n e")).then_inc(S["load"], 16)
                for j in range(P // MP):
                    sp.dma_start(K["bias_e"][MP * j:MP * j + MP, :, :],
                                 d["e_b"].rearrange("(t j) e -> j t e", j=P // MP)[j:j + 1].to_broadcast([MP, MS // P, P]))\
                      .then_inc(S["load"], 16)
                sp.wait_ge(S["load"], 16 * 6)
        S.clear()
        with nc.Fori(0, MS // CW) as c:
            with nc.Block() as block:
                @block.tensor
                def _(pe):
                    for t in range(NT + 2):
                        if t < NT:
                            if t >= 2:
                                pe.wait_ge(S["sub"], t - 1)
                            for b in range(B):
                                mm = pe.matmul(logit[t % 2][:, b, :], K["xn_T"][:, b * L + t * P:b * L + (t + 1) * P],
                                               K["phi"][:, bass.ds(c * CW, CW)], start=True, stop=True)
                            mm.then_inc(S["logit"], 1)
                        if t >= 2:
                            u = t - 2
                            pe.wait_ge(S["wa"], u + 1)
                            pe.wait_ge(S["wb"], u + 1)
                            for b in range(B):
                                mm = pe.matmul(gather[:, b, :], K["xn_tok"][:, b, u, :], w[:, u % 2, b, :],
                                               start=(u == 0 and b % 2 == 0), stop=(u == NT - 1), skip_group_check=True)
                            mm.then_inc(S["slots"], 1)

                @block.vector
                def _(ve):
                    for t in range(NT + 1):
                        if t < NT:
                            i = t % 2
                            ve.wait_ge(S["logit"], t + 1)
                            if t >= 2:
                                ve.wait_ge(S["wa"], t - 1)
                            ve.tensor_reduce(mx[:, i, :], logit[i][:, :, :].rearrange("p b n -> p n b"), AX.X, ALU.max)\
                              .then_inc(S["mx"], 1)
                            ve.wait_ge(S["mx"], t + 1)
                            if t >= 2:
                                ve.wait_ge(S["wb"], t - 1)
                            ve.tensor_tensor(e[:, i, :, :], logit[i][:, :, :],
                                             mx[:, i, :].rearrange("p (o n) -> p o n", o=1).to_broadcast([P, B, CW]),
                                             ALU.subtract).then_inc(S["sub"], 1)
                        if t >= 1:
                            u, i = t - 1, (t - 1) % 2
                            ve.wait_ge(S["s2"], u + 1)
                            ve.reciprocal(rs[:, i, :], s2[:, i, :]).then_inc(S["rs"], 1)
                            ve.wait_ge(S["rs"], u + 1)
                            if u >= 2:
                                ve.wait_ge(S["slots"], u - 1)
                            ve.tensor_tensor(w[:, i, 2:4, :], e[:, i, 2:4, :],
                                             rs[:, i, :].rearrange("p (o n) -> p o n", o=1).to_broadcast([P, 2, CW]),
                                             ALU.mult).then_inc(S["wb"], 1)

                @block.scalar
                def _(ac):
                    for t in range(NT):
                        ac.wait_ge(S["sub"], t + 1)
                        ac.activation(e[:, t % 2, :, :], e[:, t % 2, :, :], ACT.Exp).then_inc(S["exp"], 1)
                    ac.wait_ge(S["slots"], NT)
                    ac.activation(K["slots_T"][:, :, bass.ds(c * CW, CW)], gather[:, :, :], ACT.Copy).then_inc(S["out"], 1)

                @block.gpsimd
                def _(po):
                    g = nc.gpsimd
                    for t in range(NT):
                        i = t % 2
                        po.wait_ge(S["exp"], t + 1)
                        g.tensor_tensor(s1[:, i, :, :], e[:, i, 0:2, :], e[:, i, 2:4, :], ALU.add).then_inc(S["s1"], 1)
                        po.wait_ge(S["s1"], t + 1)
                        if t >= 2:
                            po.wait_ge(S["rs"], t - 1)
                        g.tensor_tensor(s2[:, i, :], s1[:, i, 0, :], s1[:, i, 1, :], ALU.add).then_inc(S["s2"], 1)
                        po.wait_ge(S["rs"], t + 1)
                        if t >= 2:
                            po.wait_ge(S["slots"], t - 1)
                        g.tensor_tensor(w[:, i, 0:2, :], e[:, i, 0:2, :],
                                        rs[:, i, :].rearrange("p (o n) -> p o n", o=1).to_broadcast([P, 2, CW]),
                                        ALU.mult).then_inc(S["wa"], 1)
            S.clear()


def phase_experts(nc, d, keep, out):
    K = keep
    ST = MS // P
    with ExitStack() as ctx:
        sb = lambda n, s, t=fp32: ctx.enter_context(nc.sbuf_tensor(n, s, t))
        ps = lambda n, s, t=fp32: ctx.enter_context(nc.psum_tensor(n, s, t))
        slot_b, x_b = sb("f_slots", [P, MS]), sb("f_x", [P, L])
        y = sb("f_y", [P, ST, P])
        ex, exT = sb("f_ex", [P, 2, MS]), sb("f_exT", [P, 2, ST, P])
        pm, nm = sb("f_pm", [P, NT, 2]), sb("f_nm", [P, NT])
        den, dsum, rden = sb("f_den", [P, NT, 2]), sb("f_dsum", [P, NT]), sb("f_rden", [P, NT])
        o = sb("f_o", [P, NT, P])
        logit = [ps(f"f_l{i}", [P, 2 * HALF]) for i in range(2)]
        turn = [ps(f"f_t{i}", [P, HALF]) for i in range(2)]
        acc = [ps(f"f_a{i}", [P, P]) for i in range(2)]
        S = Signals(nc, ctx, "f", "cp ymm y logit pm nm exp turn ev_v ev_s acc dsum rden o silu mul fin store")
        with nc.Fori(0, B) as b:
            with nc.Block() as block:
                @block.tensor
                def _(pe):
                    pe.wait_ge(S["cp"], 2)
                    for t in range(ST):
                        dst = logit[t // 8][:, t % 8 * P:(t % 8 + 1) * P]
                        for j in range(P // MP):
                            n = t * (P // MP) + j
                            mm = pe.matmul(dst[MP * j:MP * j + MP, :], slot_b[:, n * MP:(n + 1) * MP], K["w_e"][:, n, :],
                                           start=True, stop=True)
                        if t % 8 == 7:
                            mm.then_inc(S["ymm"], 1)
                    for t in range(NT + 1):
                        if t < NT:
                            for h in range(2):
                                if t == 0:
                                    pe.wait_ge(S["y"], h + 1)
                                else:
                                    pe.wait_ge(S["exp"], 2 * (t - 1) + h + 1)
                                for q in range(2):
                                    s = h * 2 * HALF + q * HALF
                                    mm = pe.matmul(logit[h][:, q * HALF:(q + 1) * HALF], x_b[:, t * P:(t + 1) * P],
                                                   K["phi"][:, s:s + HALF], start=True, stop=True)
                                mm.then_inc(S["logit"], 1)
                        if t >= 1:
                            u = t - 1
                            pe.wait_ge(S["exp"], 2 * u + 2)
                            for q in range(4):
                                if u or q >= 2:
                                    pe.wait_ge(S[("ev_v", "ev_s")[q % 2]], 2 * u + q // 2)
                                for i in range(4):
                                    s = (4 * q + i) * P
                                    mm = pe.transpose(turn[q % 2][:, i * P:(i + 1) * P], ex[:, u % 2, s:s + P], K["ident"][:, :])
                                mm.then_inc(S["turn"], 1)
                            if u >= 2:
                                pe.wait_ge(S["o"], u - 1)
                            pe.wait_ge(S["ev_v"], 2 * u + 2)
                            pe.wait_ge(S["ev_s"], 2 * u + 2)
                            for i in range(ST):
                                mm = pe.matmul(acc[u % 2][:, :], exT[:, u % 2, i, :], y[:, i, :], start=(i == 0), stop=(i == ST - 1))
                            mm.then_inc(S["acc"], 1)

                @block.scalar
                def _(ac):
                    ac.activation(slot_b[:, :], K["slots_T"][:, bass.ds(b, 1), :].rearrange("p o n -> p (o n)"), ACT.Copy)\
                      .then_inc(S["cp"], 1)
                    ac.activation(x_b[:, :], K["xn_T"][:, bass.ds(b * L, L)], ACT.Copy).then_inc(S["cp"], 1)
                    for t in range(NT + 1):
                        if t < NT:
                            ac.wait_ge(S["nm"], t + 1)
                            if t >= 2:
                                ac.wait_ge(S["turn"], 4 * (t - 1))
                            for h in range(2):
                                ac.activation(ex[:, t % 2, h * 2 * HALF:(h + 1) * 2 * HALF], logit[h][:, :], ACT.Exp,
                                              bias=nm[:, t:t + 1], accum_out=den[:, t, h:h + 1]).then_inc(S["exp"], 1)
                        if t >= 1:
                            u = t - 1
                            for q in (1, 3):
                                ac.wait_ge(S["turn"], 4 * u + q + 1)
                                if u >= 2:
                                    ac.wait_ge(S["acc"], u - 1)
                                ac.activation(exT[:, u % 2, 4 * q:4 * q + 4, :].rearrange("p a n -> p (a n)"), turn[1][:, :],
                                              ACT.Copy).then_inc(S["ev_s"], 1)
                    ac.wait_ge(S["o"], NT)
                    ac.activation(o[:, :, :], o[:, :, :], ACT.Silu).then_inc(S["silu"], 1)

                @block.vector
                def _(ve):
                    for h in range(2):
                        ve.wait_ge(S["ymm"], h + 1)
                        ve.tensor_tensor(y[:, 8 * h:8 * h + 8, :].rearrange("p t e -> p (t e)"), logit[h][:, :],
                                         K["bias_e"][:, 8 * h:8 * h + 8, :].rearrange("p t e -> p (t e)"), ALU.add).then_inc(S["y"], 1)
                    for t in range(NT + 2):
                        if t < NT:
                            for h in range(2):
                                ve.wait_ge(S["logit"], 2 * t + h + 1)
                                ve.tensor_reduce(pm[:, t, h:h + 1], logit[h][:, :], AX.X, ALU.max).then_inc(S["pm"], 1)
                            ve.wait_ge(S["pm"], 2 * t + 2)
                            ve.tensor_reduce(nm[:, t:t + 1], pm[:, t, :], AX.X, ALU.max, negate=True).then_inc(S["nm"], 1)
                        if 1 <= t <= NT:
                            u = t - 1
                            for q in (0, 2):
                                ve.wait_ge(S["turn"], 4 * u + q + 1)
                                if u >= 2:
                                    ve.wait_ge(S["acc"], u - 1)
                                ve.tensor_copy(exT[:, u % 2, 4 * q:4 * q + 4, :].rearrange("p a n -> p (a n)"), turn[0][:, :])\
                                  .then_inc(S["ev_v"], 1)
                            ve.wait_ge(S["exp"], 2 * u + 2)
                            ve.tensor_tensor(dsum[:, u:u + 1], den[:, u, 0:1], den[:, u, 1:2], ALU.add).then_inc(S["dsum"], 1)
                            ve.wait_ge(S["dsum"], u + 1)
                            ve.reciprocal(rden[:, u:u + 1], dsum[:, u:u + 1]).then_inc(S["rden"], 1)
                        if t >= 2:
                            u = t - 2
                            ve.wait_ge(S["acc"], u + 1)
                            ve.wait_ge(S["rden"], u + 1)
                            ve.tensor_scalar(o[:, u, :], acc[u % 2][:, :], rden[:, u:u + 1], None, ALU.mult).then_inc(S["o"], 1)
                    ve.wait_ge(S["silu"], 1)
                    r_b = flat(K["r_tok"][:, bass.ds(b, 1), :, :])
                    x1 = flat(K["x_tok"][:, bass.ds(b, 1), :, :])
                    ve.tensor_tensor(o[:, :, :], o[:, :, :], r_b, ALU.mult).then_inc(S["mul"], 1)
                    ve.wait_ge(S["mul"], 1)
                    ve.tensor_tensor(o[:, :, :], o[:, :, :], x1, ALU.add).then_inc(S["fin"], 1)

                @block.sync
                def _(sp):
                    sp.wait_ge(S["fin"], 1)
                    sp.dma_start(out[bass.ds(b, 1), :, :].rearrange("o (t p) c -> p (o t) c", p=P), o[:, :, :]).then_inc(S["store"], 16)
                    sp.wait_ge(S["store"], 16)
            S.clear()


def moe(nc, d, keep, out, ctx):
    sb = lambda n, s, t=fp32: ctx.enter_context(nc.sbuf_tensor(n, s, t))
    keep.update({"phi": sb("phi", [P, MS]), "w_e": sb("w_e", [P, ME, P]), "bias_e": sb("bias_e", [P, MS // P, P]),
                 "slots_T": sb("slots_T", [P, B, MS])})
    phase_dispatch(nc, d, keep)
    phase_experts(nc, d, keep, out)


def build(nc, d, out):
    dt = nc.dram_tensor
    d["q_parts"] = dt("q_parts", (B, 3, P, L), bf16, kind="Internal").ap()
    d["k_parts"] = dt("k_parts", (B, 3, P, L), bf16, kind="Internal").ap()
    d["v_tiles"] = dt("v_tiles", (B, P, NT * AH * 32), fp32, kind="Internal").ap()
    d["k_mask"] = dt("k_mask", (2, B, L), bf16, kind="Internal").ap()
    d["bc_rows"] = dt("bc_rows", (2, DR + 2 * DS, L), fp32, kind="Internal").ap()
    d["q_mask"] = dt("q_mask", (2, B, QW), bf16, kind="Internal").ap()
    with ExitStack() as ctx:
        sb = lambda n, s, t=fp32: ctx.enter_context(nc.sbuf_tensor(n, s, t))
        keep = {"x_tok": sb("x_tok", [P, B, NT, C]), "xn_T": sb("xn_T", [P, N]), "ident": sb("ident", [P, P]),
                "at_T": sb("at_T", [P, N]), "mo_T": sb("mo_T", [P, N])}
        keep["xn_tok"] = keep["mo_T"][:, :].rearrange("p (b t c) -> p b t c", b=B, t=NT)
        keep["r_tok"] = keep["at_T"][:, :].rearrange("p (b t c) -> p b t c", b=B, t=NT)
        with ExitStack() as c0:
            s0 = lambda n, s, t=fp32: c0.enter_context(nc.sbuf_tensor(n, s, t))
            keep.update({"h_T": s0("h_T", [P, N]), "sim": s0("sim", [P, B, NT])})
            with ExitStack() as c1:
                s1 = lambda n, s, t=fp32: c1.enter_context(nc.sbuf_tensor(n, s, t))
                keep.update({"wqkv": s1("wqkv", [P, 3, P]), "wqk": s1("wqk", [P, 2, P]),
                             "same_head": s1("same_head", [P, P]), "head_of": s1("head_of", [P, AH]),
                             "gdir": s1("gdir", [P, AH]), "reg_tok": s1("reg_tok", [P, B * NT]), "ln": s1("ln", [P, 2])})
                phase_prepare(nc, d, keep)
                phase_project(nc, d, keep)
                phase_classes(nc, d, keep)
            phase_mamba(nc, d, keep)
        phase_attention(nc, d, keep)
        phase_combine(nc, d, keep)
        phase_retention(nc, d, keep)
        moe(nc, d, keep, out, ctx)


INS = ["L0_attn_x", "L0_attn_ln_g", "L0_attn_ln_b"] + \
      [f"L0_attn_m{i}_{n}" for i in (1, 2) for n in ("Win", "Wconv", "bconv", "Wx", "Wdt", "bdt", "Alog", "Dp", "Wout")] + \
      ["L0_ffn_g_info", "L0_ffn_W_qkv", "L0_ffn_W_proj", "L0_ffn_b_proj"] + \
      ["L1_attn_" + n for n in ("ln1_w", "ln1_b", "ln2_w", "ln2_b", "WQ", "WK", "WV", "gn_w", "gn_b", "WG", "WO",
                                "ffn_w1", "ffn_b1", "ffn_w2", "ffn_b2")] + \
      ["L1_ffn_phi", "L1_ffn_W", "L1_ffn_b"]


def kernel(**inputs):
    import numpy as _np
    import concourse.bacc as _bacc
    from concourse import mybir as _mybir
    from concourse.bass_utils import run_bass_kernel_spmd as _run

    nc = _bacc.Bacc("TRN2", target_bir_lowering=False, num_devices=1)
    arrays, d = {}, {}

    def give(name, key, a):
        arrays[f"in_{name}_dram"] = a
        d[key] = nc.dram_tensor(f"in_{name}_dram", a.shape, _mybir.dt.from_np(a.dtype), kind="ExternalInput").ap()

    short = {"L0_attn_": "", "L0_ffn_": "", "L1_attn_": "r_", "L1_ffn_": "e_"}
    for name in INS:
        pre = next(p for p in short if name.startswith(p))
        give(name, short[pre] + name[len(pre):], _np.ascontiguousarray(inputs[name]))
    for name, a in shape_constants().items():
        give(name, name, a)
    out = nc.dram_tensor("out_0_dram", (B, L, C), _mybir.dt.float32, kind="ExternalOutput").ap()
    build(nc, d, out)
    r = _run(nc, [arrays], core_ids=[0])
    return r.results[0]["out_0_dram"]
```

```python
import numpy as np
import concourse.bass as bass
from concourse import mybir
from contextlib import ExitStack

fp32 = mybir.dt.float32
bf16 = mybir.dt.bfloat16
ALU = mybir.AluOpType
ACT = mybir.ActivationFunctionType
AX = mybir.AxisListType

B, L, C = 4, 1024, 128
P = 128
NT = L // P
N = B * L
HALF = 512
EPS = 1e-5

AH, AD, REG = 16, 8, 5
AG = 4
NG = AH // AG
EXTRA = 32
QW = L + EXTRA
ROWS = 9 * AD + 2 + 3
BIG = float(2.0 ** 100)

DI, DS, DR, DC, DM = 128, 16, 4, 4, 64

RL, RH, RD, FFN = 2, 8, 16, 512

ME, MP = 64, 32
MS = ME * MP


def shape_constants():
    c = {}
    reg = np.zeros((P, B, NT), np.float32)
    reg[:REG, :, 0] = 1.0
    c["reg_tok"] = reg.reshape(P, B * NT)
    rr = np.zeros((B * NT, P), np.float32)
    rr[::NT, :REG] = 1.0
    c["reg_row"] = rr
    c["ident"] = np.eye(P, dtype=np.float32)
    part = np.arange(P)
    head = (part // 32) * AG + part % AG
    c["same_head"] = (head[:, None] == head[None, :]).astype(np.float32)
    c["head_of"] = (head[:, None] == np.arange(AH)[None, :]).astype(np.float32)
    pick = np.zeros((3, 32, DS, P), mybir.dt.np(bf16))
    for n in range(DS):
        pick[:, n, n, :] = 1.0
    c["pick"] = pick.reshape(96, DS, P)
    sv = (np.arange(0, RD, 2) + 0.4 * RD) / (1.4 * RD)
    scale = sv[None, :] ** (np.arange(L, dtype=np.float64) / 64)[:, None]
    half = RD // 2
    inv = 1.0 / 10000.0 ** (np.arange(half, dtype=np.float64) / half)
    ang = np.arange(L, dtype=np.float64)[:, None] * inv[None, :]
    dup = lambda m: np.tile(np.repeat(m, 2, axis=-1).astype(np.float32).T, (RH, 1))
    c["xpos"] = np.stack([dup(np.cos(ang) * scale), dup(np.sin(ang) * scale),
                          dup(np.cos(ang) / scale), dup(np.sin(ang) / scale)], axis=1).copy()
    gam = 1.0 - np.exp(np.linspace(np.log(1.0 / 32), np.log(1.0 / 64), RH))
    n = np.arange(P)
    d = n[None, :] - n[:, None]
    dec = np.where(d[:, None, :] >= 0, gam[None, :, None] ** np.maximum(d, 0)[:, None, :], 0.0)
    c["decay"] = dec.astype(np.float32)
    hk = part // RD
    c["decay_q"] = (gam[hk][:, None] ** n[None, :]).astype(np.float32)
    c["decay_k"] = (gam[hk][None, :] ** (P - n)[:, None]).astype(np.float32)
    c["decay_s"] = (gam[hk] ** P).astype(np.float32).reshape(P, 1)
    c["rblock"] = (hk[:, None] == hk[None, :]).astype(np.float32)
    c["rhead"] = (hk[:, None] == np.arange(RH)[None, :]).astype(np.float32)
    return c


class Signals:

    def __init__(self, nc, ctx, prefix, names):
        self.nc = nc
        self.all = {}
        for n in names.split():
            self.all[n] = ctx.enter_context(nc.semaphore(f"{prefix}_{n}"))

    def __getitem__(self, name):
        return self.all[name]

    def clear(self):
        engines = (self.nc.sync, self.nc.scalar, self.nc.gpsimd, self.nc.vector, self.nc.tensor)
        for i, s in enumerate(self.all.values()):
            engines[i % len(engines)].sem_clear(s)
        self.nc.all_engine_barrier()


class Chain:

    def __init__(self, eng, sem):
        self.eng, self.sem, self.n = eng, sem, 0

    def step(self, ins):
        self.n += 1
        ins.then_inc(self.sem, 1)

    def wait(self):
        self.eng.wait_ge(self.sem, self.n)


def flat(ap):
    return ap.rearrange("p o t c -> p (o t) c")


def phase_prepare(nc, d, keep):
    with ExitStack() as ctx:
        sb = lambda n, s, t=fp32: ctx.enter_context(nc.sbuf_tensor(n, s, t))
        S = Signals(nc, ctx, "p", "load w sq nrm nrm_sb pw dir step v0")
        g_col = sb("p_gcol", [P, 4])
        mh = sb("p_mh", [P, 1])
        pN = ctx.enter_context(nc.psum_tensor("p_pN", [P, HALF], fp32))
        K = keep
        with nc.Block() as block:
            @block.sync
            def _(sp):
                loads = [(K["wqkv"][:, :, :], d["W_qkv"].rearrange("c (s n) -> c s n", s=3)),
                         (K["ident"][:, :], d["ident"]), (K["same_head"][:, :], d["same_head"]),
                         (K["head_of"][:, :], d["head_of"]), (K["reg_tok"][:, :], d["reg_tok"]),
                         (K["ln"][:, 0:1], d["ln_g"].rearrange("(c o) -> c o", o=1)),
                         (K["ln"][:, 1:2], d["ln_b"].rearrange("(c o) -> c o", o=1)),
                         (K["x_tok"][:, :, :, :], d["x"].rearrange("b (t p) c -> p b t c", p=P))]
                for dst, src in loads:
                    sp.dma_start(dst, src).then_inc(S["load"], 16)
                with nc.allow_non_contiguous_dma(reason="128 values, once"):
                    for g in range(NG):
                        sp.dma_start(g_col[32 * g:32 * g + 32, 0:1],
                                     d["g_info"][0, 0:1, 32 * g:32 * g + 32].rearrange(
                                         "o (j e) -> e j o", j=AG)).then_inc(S["load"], 16)
                sp.wait_ge(S["load"], 16 * (len(loads) + NG))
                sp.wait_ge(S["dir"], 1)

            @block.vector
            def _(ve):
                ve.wait_ge(S["load"], 16 * (8 + NG))
                for s in range(2):
                    ve.tensor_copy(K["wqk"][:, s, :].rearrange("c (g e j) -> c g e j", g=NG, e=AD),
                                   K["wqkv"][:, s, :].rearrange("c (g j e) -> c g e j", g=NG, j=AG)).then_inc(S["w"], 1)
                ve.memset(mh[:, :], -0.5).then_inc(S["w"], 1)
                ve.tensor_tensor(g_col[:, 1:2], g_col[:, 0:1], g_col[:, 0:1], ALU.mult).then_inc(S["sq"], 1)
                ve.wait_ge(S["nrm"], 1)
                ve.tensor_copy(g_col[:, 2:3], pN[:, 0:1]).then_inc(S["nrm_sb"], 1)
                ve.wait_ge(S["pw"], 1)
                ve.tensor_tensor(g_col[:, 1:2], g_col[:, 0:1], g_col[:, 3:4], ALU.mult).then_inc(S["step"], 1)
                ve.wait_ge(S["step"], 1)
                ve.tensor_scalar(K["gdir"][:, :], K["head_of"][:, :], g_col[:, 1:2], None, ALU.mult).then_inc(S["dir"], 1)

            @block.tensor
            def _(pe):
                pe.wait_ge(S["sq"], 1)
                pe.matmul(pN[:, 0:1], K["same_head"][:, :], g_col[:, 1:2], start=True, stop=True).then_inc(S["nrm"], 1)

            @block.gpsimd
            def _(po):
                po.wait_ge(S["w"], 3)
                po.wait_ge(S["nrm_sb"], 1)
                po.tensor_tensor(g_col[:, 3:4], g_col[:, 2:3], mh[:, :], ALU.pow).then_inc(S["pw"], 1)
        S.clear()


def token_norm(ve, S, src, out, stats, mv, rstd, n):
    for t in range(NT):
        ve.bn_stats(stats[:, t, :], src(t)).then_inc(S["stat"], 1)
    ve.wait_ge(S["stat"], NT * n)
    for t in range(NT):
        ve.bn_aggr(mv[:, t, :], stats[:, t, :]).then_inc(S["aggr"], 1)
    ve.wait_ge(S["aggr"], NT * n)
    ve.wait_ge(S["rstd"], n)
    for t in range(NT):
        ve.tensor_scalar(out(t), src(t), mv[:, t, 0:1], rstd[:, t:t + 1], ALU.subtract, ALU.mult).then_inc(S["normed"], 1)


def inverse_root(nc, po, S, mv, tmp, mhalf, rstd, n):
    po.wait_ge(S["aggr"], NT * n)
    nc.gpsimd.tensor_scalar(tmp[:, :], mv[:, :, 1], EPS, None, ALU.add).then_inc(S["veps"], 1)
    po.wait_ge(S["veps"], n)
    nc.gpsimd.tensor_tensor(rstd[:, :], tmp[:, :], mhalf[:, :], ALU.pow).then_inc(S["rstd"], 1)


def phase_project(nc, d, keep):
    with ExitStack() as ctx:
        sb = lambda n, s, t=fp32: ctx.enter_context(nc.sbuf_tensor(n, s, t))
        ps = lambda n, s, t=fp32: ctx.enter_context(nc.psum_tensor(n, s, t))
        K = keep
        stats, mv, rstd = sb("a_stats", [P, NT, 6]), sb("a_mv", [P, NT, 2]), sb("a_rstd", [P, NT])
        tmp, mhalf = sb("a_tmp", [P, NT]), sb("a_mhalf", [P, NT])
        xn_b, h_b = sb("a_xnb", [P, NT, P]), sb("a_hb", [P, NT, P])
        xn_Tb = sb("a_xntb", [P, L])
        q_f, q_sq = sb("a_qf", [P, L]), sb("a_qsq", [P, L])
        qk_s = sb("a_qks", [P, 2, L])
        r1, r2 = sb("a_r1", [P, 2, L]), sb("a_r2", [P, 2, L])
        sp_q, sp_k = sb("a_spq", [P, 3, L], bf16), sb("a_spk", [P, 3, L], bf16)
        v_b = sb("a_vb", [P, NT, AH, 32])
        nd, rn, dn = sb("a_nd", [P, NT, 2, AH]), sb("a_rn", [P, NT, AH]), sb("a_dn", [P, NT, AH])
        p_x, p_h = ps("a_px", [P, L]), ps("a_ph", [P, L])
        p_q, p_k = ps("a_pq", [P, L]), ps("a_pk", [P, L])
        S = Signals(nc, ctx, "a", "stat aggr veps rstd normed xturn hturn xT hT copyT qmm kmm qf qsq ks vmm vout vset "
                    "half dots ndout root rn mul sim hi res1 mid res2 lo stored")
        with nc.Fori(0, B) as b:
            with nc.Block() as block:
                x_b = flat(K["x_tok"][:, bass.ds(b, 1), :, :])

                @block.sync
                def _(sp):
                    sp.wait_ge(S["vout"], 2)
                    sp.dma_start(d["v_tiles"][bass.ds(b, 1), :, :].rearrange("o p n -> p (o n)"),
                                 v_b[:, :, :, :].rearrange("p t h e -> p (t h e)")).then_inc(S["stored"], 16)
                    sp.wait_ge(S["lo"], 2)
                    sp.dma_start(d["q_parts"][bass.ds(b, 1), :, :, :].rearrange("o s p t -> p (o s) t"),
                                 sp_q[:, :, :]).then_inc(S["stored"], 16)
                    sp.dma_start(d["k_parts"][bass.ds(b, 1), :, :, :].rearrange("o s p t -> p (o s) t"),
                                 sp_k[:, :, :]).then_inc(S["stored"], 16)
                    sp.wait_ge(S["stored"], 48)

                @block.gpsimd
                def _(po):
                    po.memset(mhalf[:, :], -0.5).then_inc(S["half"], 1)
                    po.memset(v_b[:, :, :, :], 0.0).then_inc(S["vset"], 1)
                    po.wait_ge(S["vset"], 1)
                    po.memset(v_b[:, :, :, AD:AD + 1], 1.0).then_inc(S["vset"], 1)
                    po.wait_ge(S["half"], 1)
                    inverse_root(nc, po, S, mv, tmp, mhalf, rstd, 1)
                    inverse_root(nc, po, S, mv, tmp, mhalf, rstd, 2)
                    po.wait_ge(S["xT"], 1)
                    nc.gpsimd.tensor_copy(K["xn_T"][:, bass.ds(b * L, L)], xn_Tb[:, :]).then_inc(S["copyT"], 1)

                @block.vector
                def _(ve):
                    token_norm(ve, S, lambda t: x_b[:, t, :], lambda t: xn_b[:, t, :], stats, mv, rstd, 1)
                    ve.wait_ge(S["normed"], NT)
                    token_norm(ve, S, lambda t: xn_b[:, t, :], lambda t: h_b[:, t, :], stats, mv, rstd, 2)
                    ve.wait_ge(S["vmm"], 1)
                    ve.wait_ge(S["vset"], 2)
                    for t in range(2):
                        ve.tensor_copy(v_b[:, 4 * t:4 * t + 4, :, 0:AD].rearrange("p t h e -> p (t h) e"),
                                       p_x[:, t * HALF:(t + 1) * HALF].rearrange("p (a e) -> p a e", e=AD)).then_inc(S["vout"], 1)
                    for i, (part, have) in enumerate(((sp_q, "qf"), (sp_k, "ks"))):
                        ve.wait_ge(S["hi"], i + 1)
                        ve.wait_ge(S[have], 2 if i == 0 else 1)
                        ve.tensor_tensor(r1[:, i, :], qk_s[:, i, :], part[:, 0, 0:L], ALU.subtract).then_inc(S["res1"], 1)
                    for i, part in enumerate((sp_q, sp_k)):
                        ve.wait_ge(S["mid"], i + 1)
                        ve.wait_ge(S["res1"], i + 1)
                        ve.tensor_tensor(part[:, 2, 0:L], r1[:, i, :], part[:, 1, 0:L], ALU.subtract).then_inc(S["lo"], 1)
                    ve.wait_ge(S["dots"], 1)
                    ve.tensor_copy(nd[:, :, :, :].rearrange("p t k h -> p (t k h)"), p_q[:, 0:NT * 2 * AH]).then_inc(S["ndout"], 1)
                    ve.wait_ge(S["ndout"], 1)
                    ve.wait_ge(S["root"], 1)
                    ve.reciprocal(rn[:, :, :], rn[:, :, :]).then_inc(S["rn"], 1)
                    ve.wait_ge(S["rn"], 1)
                    ve.tensor_tensor(dn[:, :, :], nd[:, :, 1, :], rn[:, :, :], ALU.mult).then_inc(S["mul"], 1)
                    ve.wait_ge(S["mul"], 1)
                    ve.tensor_reduce(K["sim"][:, bass.ds(b, 1), :].rearrange("p o t -> p (o t)"), dn[:, :, :],
                                     AX.X, ALU.add).then_inc(S["sim"], 1)

                @block.tensor
                def _(pe):
                    pe.wait_ge(S["normed"], NT)
                    for t in range(NT):
                        i = pe.transpose(p_x[:, t * P:(t + 1) * P], xn_b[:, t, :], K["ident"][:, :])
                    i.then_inc(S["xturn"], 1)
                    pe.wait_ge(S["xT"], 1)
                    for s, (pt, name) in enumerate(((p_q, "qmm"), (p_k, "kmm"))):
                        for h in range(2):
                            i = pe.matmul(pt[:, h * HALF:(h + 1) * HALF], K["wqk"][:, s, :],
                                          xn_Tb[:, h * HALF:(h + 1) * HALF], start=True, stop=True)
                        i.then_inc(S[name], 1)
                    for t in range(NT):
                        i = pe.matmul(p_x[:, t * P:(t + 1) * P], xn_Tb[:, t * P:(t + 1) * P], K["wqkv"][:, 2, :],
                                      start=True, stop=True)
                    i.then_inc(S["vmm"], 1)
                    pe.wait_ge(S["normed"], 2 * NT)
                    for t in range(NT):
                        i = pe.transpose(p_h[:, t * P:(t + 1) * P], h_b[:, t, :], K["ident"][:, :])
                    i.then_inc(S["hturn"], 1)
                    pe.wait_ge(S["qf"], 2)
                    pe.wait_ge(S["qsq"], 1)
                    for t in range(NT):
                        pe.matmul(p_q[:, (2 * t) * AH:(2 * t + 1) * AH], q_sq[:, t * P:(t + 1) * P], K["head_of"][:, :],
                                  start=True, stop=True)
                        i = pe.matmul(p_q[:, (2 * t + 1) * AH:(2 * t + 2) * AH], q_f[:, t * P:(t + 1) * P], K["gdir"][:, :],
                                      start=True, stop=True)
                    i.then_inc(S["dots"], 1)

                @block.scalar
                def _(ac):
                    ac.wait_ge(S["xturn"], 1)
                    ac.activation(xn_Tb[:, :], p_x[:, :], ACT.Copy).then_inc(S["xT"], 1)
                    ac.wait_ge(S["qmm"], 1)
                    ac.activation(q_f[:, :], p_q[:, :], ACT.Copy).then_inc(S["qf"], 1)
                    ac.activation(qk_s[:, 0, :], p_q[:, :], ACT.Copy, scale=float(AD) ** -0.5).then_inc(S["qf"], 1)
                    ac.wait_ge(S["qf"], 2)
                    ac.activation(q_sq[:, :], q_f[:, :], ACT.Square).then_inc(S["qsq"], 1)
                    ac.activation(sp_q[:, 0, 0:L], qk_s[:, 0, :], ACT.Copy).then_inc(S["hi"], 1)
                    ac.wait_ge(S["kmm"], 1)
                    ac.activation(qk_s[:, 1, :], p_k[:, :], ACT.Copy).then_inc(S["ks"], 1)
                    ac.wait_ge(S["ks"], 1)
                    ac.activation(sp_k[:, 0, :], qk_s[:, 1, :], ACT.Copy).then_inc(S["hi"], 1)
                    for i, part in enumerate((sp_q, sp_k)):
                        ac.wait_ge(S["res1"], i + 1)
                        ac.activation(part[:, 1, 0:L], r1[:, i, :], ACT.Copy).then_inc(S["mid"], 1)
                    ac.wait_ge(S["hturn"], 1)
                    ac.activation(K["h_T"][:, bass.ds(b * L, L)], p_h[:, :], ACT.Identity, bias=K["ln"][:, 1:2],
                                  scale=K["ln"][:, 0:1]).then_inc(S["hT"], 1)
                    ac.wait_ge(S["ndout"], 1)
                    ac.activation(rn[:, :, :], nd[:, :, 0, :], ACT.Sqrt).then_inc(S["root"], 1)
            S.clear()


def phase_classes(nc, d, keep):
    with ExitStack() as ctx:
        sb = lambda n, s, t=fp32: ctx.enter_context(nc.sbuf_tensor(n, s, t))
        K = keep
        sim = K["sim"][:, :, :].rearrange("p b t -> p (b t)")
        ext, mm, mmr, rng = sb("c_ext", [P, 2, B * NT]), sb("c_mm", [P, 2]), sb("c_mmr", [P, 2]), sb("c_rng", [P, 2])
        pos, pos_r = sb("c_pos", [P, B * NT]), sb("c_posr", [B * NT, P])
        reg_row = sb("c_regrow", [B * NT, P])
        m = sb("c_m", [B * NT, 3, P])
        mrow = sb("c_mrow", [B * NT, 4, P], bf16)
        ex0, ex1 = sb("c_ex0", [B, EXTRA], bf16), sb("c_ex1", [B, EXTRA], bf16)
        pT = ctx.enter_context(nc.psum_tensor("c_pT", [P, HALF], fp32))
        S = Signals(nc, ctx, "c", "load red all v turn rows st ex")
        with nc.Block() as block:
            @block.sync
            def _(sp):
                sp.dma_start(reg_row[:, :], d["reg_row"]).then_inc(S["load"], 16)
                sp.wait_ge(S["ex"], 2)
                sp.dma_start(d["q_mask"][0, :, L:QW], ex0[:, :]).then_inc(S["st"], 16)
                sp.dma_start(d["q_mask"][1, :, L:QW], ex1[:, :]).then_inc(S["st"], 16)
                sp.wait_ge(S["rows"], 4)
                for r in range(4):
                    dst = (d["k_mask"], d["q_mask"])[r // 2]
                    sp.dma_start(dst[r % 2, :, 0:L].rearrange("b (t p) -> b t p", p=P), mrow[:, r, :]).then_inc(S["st"], 16)
                sp.wait_ge(S["st"], 16 * 6)

            @block.vector
            def _(ve):
                c = Chain(ve, S["v"])
                ve.memset(ex0[:, :], 0.0).then_inc(S["ex"], 1)
                ve.memset(ex1[:, :], 1.0).then_inc(S["ex"], 1)
                c.step(ve.scalar_tensor_tensor(ext[:, 0, :], K["reg_tok"][:, :], -BIG, sim, ALU.mult, ALU.add))
                c.step(ve.scalar_tensor_tensor(ext[:, 1, :], K["reg_tok"][:, :], BIG, sim, ALU.mult, ALU.add))
                c.wait()
                c.step(ve.tensor_reduce(mm[:, 0:1], ext[:, 0, :], AX.X, ALU.max))
                c.step(ve.tensor_reduce(mm[:, 1:2], ext[:, 1, :], AX.X, ALU.min, negate=True))
                c.wait()
                ve.engine_nop().then_inc(S["red"], 1)
                ve.wait_ge(S["all"], 1)
                c.step(ve.tensor_tensor(rng[:, 0:1], mmr[:, 0:1], mmr[:, 1:2], ALU.add))
                c.wait()
                c.step(ve.reciprocal(rng[:, 1:2], rng[:, 0:1]))
                c.wait()
                c.step(ve.tensor_scalar(pos[:, :], sim, mmr[:, 1:2], rng[:, 1:2], ALU.add, ALU.mult))
                c.wait()
                c.step(ve.tensor_scalar(pos[:, :], pos[:, :], 0.9, None, ALU.is_gt))
                c.wait()
                ve.engine_nop().then_inc(S["red"], 1)
                ve.wait_ge(S["turn"], 1)
                c.step(ve.tensor_copy(pos_r[:, :], pT[0:B * NT, 0:P]))
                ve.wait_ge(S["load"], 16)
                c.wait()
                c.step(ve.tensor_tensor(m[:, 0, :], pos_r[:, :], reg_row[:, :], ALU.max))
                c.step(ve.tensor_scalar(m[:, 1, :], reg_row[:, :], BIG, -BIG, ALU.mult, ALU.add))
                c.wait()
                ve.tensor_copy(mrow[:, 2, :], m[:, 0, :]).then_inc(S["rows"], 1)
                ve.tensor_scalar(mrow[:, 3, :], m[:, 0, :], -1.0, 1.0, ALU.mult, ALU.add).then_inc(S["rows"], 1)
                ve.tensor_tensor(mrow[:, 1, :], m[:, 1, :], m[:, 0, :], ALU.mult).then_inc(S["rows"], 1)
                c.step(ve.tensor_scalar(m[:, 2, :], m[:, 0, :], -1.0, 1.0, ALU.mult, ALU.add))
                c.wait()
                ve.tensor_tensor(mrow[:, 0, :], m[:, 1, :], m[:, 2, :], ALU.mult).then_inc(S["rows"], 1)

            @block.gpsimd
            def _(po):
                po.wait_ge(S["red"], 1)
                po.partition_all_reduce(mmr[:, :], mm[:, :], P, bass.bass_isa.ReduceOp.max).then_inc(S["all"], 1)

            @block.tensor
            def _(pe):
                pe.wait_ge(S["red"], 2)
                pe.transpose(pT[0:B * NT, 0:P], pos[:, :], K["ident"][:, :]).then_inc(S["turn"], 1)
        S.clear()


def maxima_jobs(g, t0, span):
    return [(t0 + i / 2, 0, "max", g, i) for i in range(2 * AG * NT + 2)] + [(t0 + span, 1, "maxima", g, 0)]


def attention_order(last):
    span, lag = 33, 5
    jobs = []
    for g in range(NG):
        if not (last and g == NG - 1):
            jobs += maxima_jobs(g + 1, g * span, span)
        t1 = g * span + (lag if g else 0)
        jobs += [(t1 + n, 2, "score", g, n) for n in range(span)]
        jobs += [(t1 + n + 2, 3, "sum", g, n) for n in range(span)]
        for u, n in enumerate((16, 32, 33)):
            jobs += [(t1 + n + 2.1, 4, "take", g, u), (t1 + n + 4.2, 5, "turn", g, u)]
    return [j[2:] for j in sorted(jobs)]


def phase_attention(nc, d, keep):
    K = keep
    QK = 9 * AD + 2
    LOADS = 3 * (1 + 3 + 3) + 3
    with ExitStack() as ctx:
        sb = lambda n, s, t=fp32: ctx.enter_context(nc.sbuf_tensor(n, s, t))
        ps = lambda n, s, t=fp32: ctx.enter_context(nc.psum_tensor(n, s, t))
        qb = [sb(f"b_q{g}", [P, AG, L], bf16) for g in range(NG)]
        qx = [sb(f"b_qx{g}", [P, AG, EXTRA], bf16) for g in range(NG)]
        kb = [sb(f"b_k{g}", [P, AG, L], bf16) for g in range(NG)]
        v_b = sb("b_v", [P, NT, AH, 32])
        probs = sb("b_probs", [P, 4, 2 * HALF])
        mpart = sb("b_mpart", [P, 2, AG * NT + 1, 2])
        negm = sb("b_negm", [P, 2, AG * NT + 1])
        m_row = sb("b_mrow", [AG * NT + 1, P])
        m_res = sb("b_mres", [AG * NT + 1, 2, P])
        m_parts = sb("b_mparts", [AG * NT + 1, 2, 3, P], bf16)
        o_sb = sb("b_o", [P, 2, HALF])
        rec = sb("b_rec", [P, 4 * AG])
        ex = sb("b_ex", [EXTRA, AG, AD])
        att = sb("b_att", [P, NT, AH, AD])
        small = [ps(f"b_small{i}", [P, HALF]) for i in range(2)]
        score = [ps(f"b_score{i}", [P, 2 * HALF]) for i in range(2)]
        acc = [ps(f"b_acc{i}", [P, HALF]) for i in range(2)]
        S = Signals(nc, ctx, "b", "load0 load1 load2 load3 vload mput small_full small_read score_full score_read sum_done "
                    "acc_read maxp neg mrow mhi mres1 mmid mres2 mparts rec norm exn half done aturn aout ones")

        with nc.Block() as block:
            @block.gpsimd
            def _(po):
                for g in range(NG):
                    po.memset(kb[g][64:96, :, :], 1.0).then_inc(S["ones"], 1)
        S.clear()

        def load_group(sp, g, b):
            ld = S[f"load{g}"]
            for r in range(3):
                sp.dma_start(kb[g][24 * r:24 * r + 24, :, :].rearrange("e j t -> e (j t)"),
                             d["k_parts"][bass.ds(b, 1), :, 32 * g:32 * g + 32, :].rearrange(
                                 "o s (e j) t -> (o s) e (j t)", j=AG)).then_inc(ld, 16)
                for a in range(3):
                    sp.dma_start(qb[g][24 * r + 8 * a:24 * r + 8 * a + 8, :, :].rearrange("e j t -> e (j t)"),
                                 d["q_parts"][bass.ds(b, 1), r:r + 1, 32 * g:32 * g + 32, :].rearrange(
                                     "o s (e j) t -> (o s e) (j t)", j=AG)).then_inc(ld, 16)
                    sp.dma_start(qx[g][24 * r + 8 * a:24 * r + 8 * a + 8, :, :],
                                 d["q_parts"][bass.ds(b, 1), r:r + 1, 32 * g:32 * g + 32, 0:EXTRA].rearrange(
                                     "o s (e j) t -> (o s e) j t", j=AG)).then_inc(ld, 16)
            sp.dma_start(kb[g][72:74, :, :], d["k_mask"][:, bass.ds(b, 1), :].to_broadcast([2, AG, L])).then_inc(ld, 16)
            sp.dma_start(qb[g][72:74, :, :], d["q_mask"][:, bass.ds(b, 1), 0:L].to_broadcast([2, AG, L])).then_inc(ld, 16)
            sp.dma_start(qx[g][72:74, :, :], d["q_mask"][:, bass.ds(b, 1), L:QW].to_broadcast([2, AG, EXTRA])).then_inc(ld, 16)

        def load_v(sp, b):
            sp.dma_start(v_b[:, :, :, :].rearrange("p t h e -> p (t h e)"),
                         d["v_tiles"][bass.ds(b, 1), :, :].rearrange("o p n -> p (o n)")).then_inc(S["vload"], 16)

        def put_maxima(sp, g, c):
            g = g % NG
            sp.wait_ge(S["mparts"], c)
            for s in range(3):
                sp.dma_start(qb[g][QK + s:QK + s + 1, :, :].rearrange("o j (t p) -> o (j t) p", p=P),
                             m_parts[0:AG * NT, g % 2, s, :]).then_inc(S["mput"], 16)
                sp.dma_start(qx[g][QK + s:QK + s + 1, :, :],
                             m_parts[AG * NT:AG * NT + 1, g % 2, s, :].rearrange("o (j q) -> o j q", j=AG))\
                  .then_inc(S["mput"], 16)
            sp.wait_ge(S["mput"], 96 * c)

        def small_slot(pe, k):
            if k >= 2:
                pe.wait_ge(S["small_read"], k - 1)
            return small[k % 2]

        def maxima_pe(pe, kind, g, n, c, k):
            g = g % NG
            out = small_slot(pe, k)
            if kind == "max":
                if n == 0 and g in (0, NG - 1):
                    pe.wait_ge(S[f"load{g}"], LOADS * 16)
                if n < 2 * AG * NT:
                    j, t, h = n // (2 * NT), n // 2 % NT, n % 2
                    i = pe.matmul(out[:, :], qb[g][0:QK, j, t * P:(t + 1) * P],
                                  kb[g][0:QK, j, h * HALF:(h + 1) * HALF], start=True, stop=True)
                else:
                    h = n % 2
                    for j in range(AG):
                        i = pe.matmul(out[32 * j:32 * j + 32, :], qx[g][0:QK, j, :],
                                      kb[g][0:QK, j, h * HALF:(h + 1) * HALF], start=True, stop=True)
                i.then_inc(S["small_full"], 1)
            else:
                pe.wait_ge(S["neg"], c)
                pe.transpose(out[0:AG * NT + 1, 0:P], negm[:, g % 2, :], K["ident"][:, :]).then_inc(S["small_full"], 1)

        def maxima_ve(ve, kind, g, n, c, k):
            g = g % NG
            src = small[k % 2]
            ve.wait_ge(S["small_full"], k + 1)
            if kind == "max":
                i, h = n // 2, n % 2
                if n == 0 and c >= 2:
                    ve.wait_ge(S["neg"], c - 1)
                ve.tensor_reduce(mpart[:, g % 2, i, h:h + 1], src[:, :], AX.X, ALU.max).then_inc(S["small_read"], 1)
                if n == 2 * AG * NT + 1:
                    ve.wait_ge(S["small_read"], k + 1)
                    ve.tensor_reduce(negm[:, g % 2, :], mpart[:, g % 2, :, :], AX.X, ALU.max, negate=True)\
                      .then_inc(S["neg"], 1)
            else:
                ve.tensor_copy(m_row[:, :], src[0:AG * NT + 1, 0:P]).then_inc(S["small_read"], 1)
                ve.wait_ge(S["small_read"], k + 1)
                if c >= 3:
                    ve.wait_ge(S["mput"], 96 * (c - 2))
                ve.tensor_copy(m_parts[:, g % 2, 0, :], m_row[:, :]).then_inc(S["mhi"], 1)
                ve.wait_ge(S["mhi"], c)
                ve.tensor_tensor(m_res[:, 0, :], m_row[:, :], m_parts[:, g % 2, 0, :], ALU.subtract).then_inc(S["mres1"], 1)
                ve.wait_ge(S["mres1"], c)
                ve.tensor_copy(m_parts[:, g % 2, 1, :], m_res[:, 0, :]).then_inc(S["mmid"], 1)
                ve.wait_ge(S["mmid"], c)
                ve.tensor_tensor(m_parts[:, g % 2, 2, :], m_res[:, 0, :], m_parts[:, g % 2, 1, :], ALU.subtract)\
                  .then_inc(S["mparts"], 1)

        first = [j[2:] for j in maxima_jobs(0, 0, 33)]
        with nc.Block() as block:
            @block.sync
            def _(sp):
                for g in range(NG - 1):
                    load_group(sp, g, 0)
                put_maxima(sp, 0, 1)
                for g in range(1, NG - 1):
                    sp.wait_ge(S[f"load{g}"], LOADS * 16)

            @block.tensor
            def _(pe):
                for k, (kind, g, n) in enumerate(first):
                    maxima_pe(pe, kind, g, n, 1, k)

            @block.vector
            def _(ve):
                for k, (kind, g, n) in enumerate(first):
                    maxima_ve(ve, kind, g, n, 1, k)
        S.clear()

        def attend(b, last):
            groups = range(1, NG) if last else range(1, NG + 1)
            order = attention_order(last)
            small_no = {j: k for k, j in enumerate([j for j in order if j[0] in ("max", "maxima", "turn")])}
            turn_no = [small_no[("turn", g, u)] for g in range(NG) for u in range(3)]
            score_no = {j[1:]: k for k, j in enumerate([j for j in order if j[0] == "score"])}
            with nc.Block() as block:
                @block.sync
                def _(sp):
                    load_v(sp, b)
                    load_group(sp, NG - 1, b)
                    for g in groups:
                        put_maxima(sp, g, g)
                        if g < NG and not last:
                            sp.wait_ge(S["score_full"], 33 * g)
                            load_group(sp, g - 1, b + 1)
                    if not last:
                        for g in range(1, NG - 1):
                            sp.wait_ge(S[f"load{g}"], LOADS * 16)

                @block.tensor
                def _(pe):
                    for job in order:
                        kind, g, n = job
                        if kind in ("max", "maxima"):
                            maxima_pe(pe, kind, g, n, g, small_no[job])
                        elif kind == "score":
                            m = score_no[(g, n)]
                            if n == 0 and g:
                                pe.wait_ge(S["mput"], 96 * g)
                            if m >= 2:
                                pe.wait_ge(S["score_read"], m - 1)
                            out = score[m % 2]
                            if n < 32:
                                h, t, pair = n // 16, n % 16 // 2, n % 2
                                for i in range(2):
                                    j = 2 * pair + i
                                    mm = pe.matmul(out[:, i * HALF:(i + 1) * HALF], kb[g][0:ROWS, j, t * P:(t + 1) * P],
                                                   qb[g][0:ROWS, j, h * HALF:(h + 1) * HALF], start=True, stop=True)
                            else:
                                for t in range(NT):
                                    for j in range(AG):
                                        c = (t * AG + j) * EXTRA
                                        mm = pe.matmul(out[:, c:c + EXTRA], kb[g][0:ROWS, j, t * P:(t + 1) * P],
                                                       qx[g][0:ROWS, j, :], start=True, stop=True)
                            mm.then_inc(S["score_full"], 1)
                        elif kind == "sum":
                            m = score_no[(g, n)]
                            if m == 0:
                                pe.wait_ge(S["vload"], 16)
                            pe.wait_ge(S["score_read"], m + 1)
                            a = 3 * g + n // 16
                            out = acc[a % 2]
                            if n % 16 == 0 and a >= 2:
                                pe.wait_ge(S["acc_read"], a - 1)
                            if n < 32:
                                t, pair = n % 16 // 2, n % 2
                                for i in range(2):
                                    j = 2 * pair + i
                                    mm = pe.matmul(out[32 * j:32 * j + 32, :], v_b[:, t, AG * g + j, :],
                                                   probs[:, m % 4, i * HALF:(i + 1) * HALF], start=(t == 0), stop=(t == NT - 1))
                            else:
                                for t in range(NT):
                                    for j in range(AG):
                                        c = (t * AG + j) * EXTRA
                                        mm = pe.matmul(out[32 * j:32 * j + 32, 0:EXTRA], v_b[:, t, AG * g + j, :],
                                                       probs[:, m % 4, c:c + EXTRA], start=(t == 0), stop=(t == NT - 1))
                            mm.then_inc(S["sum_done"], 1)
                        elif kind == "turn":
                            out = small_slot(pe, small_no[job])
                            a = 3 * g + n
                            pe.wait_ge(S["acc_read"], a + 1)
                            if n < 2:
                                for t in range(4):
                                    mm = pe.transpose(out[:, t * P:(t + 1) * P], o_sb[:, a % 2, t * P:(t + 1) * P], K["ident"][:, :])
                            else:
                                mm = pe.transpose(out[0:EXTRA, 0:P], o_sb[:, a % 2, 0:EXTRA], K["ident"][:, :])
                            mm.then_inc(S["small_full"], 1)
                    pe.wait_ge(S["half"], NG)
                    for t in range(NT):
                        mm = pe.transpose(score[0][:, t * P:(t + 1) * P], att[:, t, :, :].rearrange("p h e -> p (h e)"),
                                          K["ident"][:, :])
                    mm.then_inc(S["aturn"], 1)

                @block.scalar
                def _(ac):
                    for kind, g, n in order:
                        if kind == "score":
                            m = score_no[(g, n)]
                            ac.wait_ge(S["score_full"], m + 1)
                            if m >= 4:
                                ac.wait_ge(S["sum_done"], m - 3)
                            ac.activation(probs[:, m % 4, :], score[m % 2][:, :], ACT.Exp).then_inc(S["score_read"], 1)
                        elif kind == "take":
                            a = 3 * g + n
                            ac.wait_ge(S["sum_done"], 33 * g + (16, 32, 33)[n])
                            if a >= 2:
                                ac.wait_ge(S["small_full"], turn_no[a - 2] + 1)
                            w = HALF if n < 2 else EXTRA
                            ac.activation(o_sb[:, a % 2, 0:w], acc[a % 2][:, 0:w], ACT.Copy).then_inc(S["acc_read"], 1)
                    ac.wait_ge(S["aturn"], 1)
                    ac.activation(K["at_T"][:, bass.ds(b * L, L)], score[0][:, :], ACT.Copy).then_inc(S["aout"], 1)

                @block.vector
                def _(ve):
                    for job in order:
                        kind, g, n = job
                        if kind in ("max", "maxima"):
                            maxima_ve(ve, kind, g, n, g, small_no[job])
                        elif kind == "turn":
                            k = small_no[job]
                            src = small[k % 2]
                            ve.wait_ge(S["small_full"], k + 1)
                            a = 3 * g + n
                            q, w = (P, 4) if n < 2 else (EXTRA, 1)
                            v = src[0:q, 0:w * P].rearrange("p (a e) -> p a e", e=32)
                            if a >= 1:
                                ve.wait_ge(S["small_read"], turn_no[a - 1] + 1)
                            ve.reciprocal(rec[0:q, 0:w * AG], v[:, :, AD]).then_inc(S["rec"], 1)
                            ve.wait_ge(S["rec"], a + 1)
                            r = rec[0:q, 0:w * AG].rearrange("p (a o) -> p a o", o=1)
                            if n < 2:
                                dst = att[:, 4 * n:4 * n + 4, AG * g:AG * g + AG, :]
                                ve.tensor_tensor(dst, src[:, :].rearrange("p (t j e) -> p t j e", t=4, j=AG)[:, :, :, 0:AD],
                                                 rec[:, :].rearrange("p (t j o) -> p t j o", t=4, o=1).to_broadcast([P, 4, AG, AD]),
                                                 ALU.mult).then_inc(S["small_read"], 1)
                            else:
                                ve.tensor_tensor(ex[:, :, :], v[:, :, 0:AD], r.to_broadcast([EXTRA, AG, AD]), ALU.mult)\
                                  .then_inc(S["small_read"], 1)
                                ve.wait_ge(S["half"], g) if g else None
                                ve.wait_ge(S["small_read"], k + 1)
                                reg = att[0:REG, 0, AG * g:AG * g + AG, :]
                                ve.tensor_tensor(reg, reg, ex[0:REG, :, :], ALU.add).then_inc(S["exn"], 1)
                                ve.wait_ge(S["exn"], g + 1)
                                ve.tensor_scalar(reg, reg, 0.5, None, ALU.mult).then_inc(S["half"], 1)
            S.clear()

        with nc.Fori(0, B - 1) as b:
            attend(b, last=False)
        attend(B - 1, last=True)


def phase_mamba(nc, d, keep):
    K = keep
    W = DC - 1
    RING = 4
    PARTS = 3 * 32
    rows = d["bc_rows"]
    with ExitStack() as ctx:
        sb = lambda n, s, t=fp32: ctx.enter_context(nc.sbuf_tensor(n, s, t))
        ps = lambda n, s, t=fp32: ctx.enter_context(nc.psum_tensor(n, s, t))
        w_in = sb("m_win", [P, 2, 2 * DI])
        w_x = sb("m_wx", [P, 2, DR + 2 * DS])
        w_dt = sb("m_wdt", [DR, 2, DI])
        w_out = sb("m_wout", [P, 2, DM])
        w_conv = sb("m_wconv", [P, 2, DC])
        a_log, a_neg = sb("m_alog", [P, 2, DS]), sb("m_aneg", [P, 2, DS])
        vec = sb("m_vec", [P, 2, 3])
        w_b = sb("m_wb", [P, 2, PARTS])
        pick = sb("m_pick", [PARTS, DS, P], bf16)
        x_pad, conv = sb("m_xpad", [P, L + 2 * W]), sb("m_conv", [P, L])
        dbc, b_res = sb("m_dbc", [DR + 2 * DS, L]), sb("m_bres", [PARTS, L])
        xs, zs = sb("m_xs", [P, 2, L]), sb("m_zs", [P, 2, L])
        dt, dtx = sb("m_dt", [P, 2, L]), sb("m_dtx", [P, 2, L])
        b_parts = sb("m_bparts", [PARTS, 2, L], bf16)
        c_row = sb("m_crow", [P, RING, L])
        da = sb("m_da", [P, RING, L])
        hs, hc = sb("m_hs", [P, 2, L]), sb("m_hc", [P, 2, L])
        gated, ob = sb("m_gated", [P, L]), sb("m_ob", [P, L])
        z = ps("m_z", [P, L])
        bb = [ps(f"m_bb{i}", [P, L]) for i in range(2)]
        y = ps("m_y", [P, L])
        S = Signals(nc, ctx, "m", "load expA a pad wb xmm xcp zmm zcp cv xs dbcmm dbccp rowput bmm bhi bres bmid blo bput dtmm "
                    "dtz dabs dexp dln dt dtx c0 c1 c2 c3 da dbx h hc ysum y1 y2 omm ocp mo")
        halves = [slice(h * HALF, (h + 1) * HALF) for h in range(2)]

        with nc.Block() as block:
            @block.sync
            def _(sp):
                n = 0
                for i in range(2):
                    q = f"m{i + 1}_"
                    col = lambda a: a.rearrange("(c o) -> c o", o=1)
                    for dst, src in ((w_in[:, i, :], d[q + "Win"]), (w_x[:, i, :], d[q + "Wx"]),
                                     (w_dt[:, i, :], d[q + "Wdt"]), (w_out[:, i, :], d[q + "Wout"]),
                                     (w_conv[:, i, :], d[q + "Wconv"]), (a_log[:, i, :], d[q + "Alog"]),
                                     (vec[:, i, 0:1], col(d[q + "bconv"])), (vec[:, i, 1:2], col(d[q + "bdt"])),
                                     (vec[:, i, 2:3], col(d[q + "Dp"]))):
                        sp.dma_start(dst, src).then_inc(S["load"], 16)
                        n += 16
                sp.dma_start(pick[:, :, :], d["pick"]).then_inc(S["load"], 16)
                sp.wait_ge(S["load"], n + 16)

            @block.scalar
            def _(ac):
                ac.wait_ge(S["load"], 16 * 19)
                ac.activation(a_neg[:, :, :], a_log[:, :, :], ACT.Exp).then_inc(S["expA"], 1)

            @block.vector
            def _(ve):
                ve.wait_ge(S["expA"], 1)
                ve.tensor_scalar(a_neg[:, :, :], a_neg[:, :, :], -1.0, None, ALU.mult).then_inc(S["a"], 1)
                ve.memset(x_pad[:, 0:W], 0.0).then_inc(S["pad"], 1)
                ve.memset(x_pad[:, L + W:L + 2 * W], 0.0).then_inc(S["pad"], 1)
                ve.memset(w_b[:, :, :], 0.0).then_inc(S["wb"], 1)
                ve.wait_ge(S["wb"], 1)
                for a in range(3):
                    ve.tensor_copy(w_b[:, :, 32 * a:32 * a + DS], w_x[:, :, DR:DR + DS]).then_inc(S["wb"], 1)
        S.clear()

        def prepare_pe(pe, j, b, q, n):
            def project(out, lhsT, rhs, sig):
                for h in range(2):
                    mm = pe.matmul(out[:, halves[h]], lhsT, rhs(h), start=True, stop=True)
                mm.then_inc(S[sig], 1)
            h_b = lambda h: K["h_T"][:, bass.ds(b * L + h * HALF, HALF)]
            xs_j = lambda h: xs[:, j, halves[h]]
            if n == 0:
                if q:
                    pe.wait_ge(S["dtz"], q)
                project(z, w_in[:, j, 0:DI], h_b, "xmm")
            elif n == 2:
                pe.wait_ge(S["xcp"], q + 1)
                project(z, w_in[:, j, DI:2 * DI], h_b, "zmm")
            elif n == 7:
                pe.wait_ge(S["zcp"], q + 1)
                pe.wait_ge(S["xs"], q + 1)
                project(z[0:DR + 2 * DS, :], w_x[:, j, :], xs_j, "dbcmm")
            elif n == 9:
                pe.wait_ge(S["dbccp"], q + 1)
                project(z[0:PARTS, :], w_b[:, j, :], xs_j, "bmm")
            elif n == 11:
                pe.wait_ge(S["bres"], q + 1)
                project(z, w_dt[:, j, :], lambda h: dbc[0:DR, halves[h]], "dtmm")

        def prepare_ac(ac, j, q, n):
            rev = slice(None) if j == 0 else slice(None, None, -1)
            if n == 1:
                ac.wait_ge(S["xmm"], q + 1)
                if q:
                    ac.wait_ge(S["cv"], DC * q)
                ac.activation(x_pad[:, W:W + L], z[:, :], ACT.Copy).then_inc(S["xcp"], 1)
            elif n == 6:
                ac.wait_ge(S["zmm"], q + 1)
                ac.wait_ge(S["cv"], DC * (q + 1))
                if q:
                    ac.wait_ge(S["y2"], 1)
                ac.activation(zs[:, j, rev], z[:, :], ACT.Silu).then_inc(S["zcp"], 1)
                ac.activation(xs[:, j, rev], conv[:, :], ACT.Silu, bias=vec[:, j, 0:1]).then_inc(S["xs"], 1)
            elif n == 8:
                ac.wait_ge(S["dbcmm"], q + 1)
                if q:
                    ac.wait_ge(S["rowput"], 16 * q)
                    ac.wait_ge(S["dtmm"], q)
                ac.activation(dbc[:, :], z[0:DR + 2 * DS, :], ACT.Copy).then_inc(S["dbccp"], 1)
            elif n == 9:
                ac.wait_ge(S["bmm"], q + 1)
                if q:
                    ac.wait_ge(S["bput"], DS)
                ac.activation(b_parts[:, j, :], z[0:PARTS, :], ACT.Copy).then_inc(S["bhi"], 1)
            elif n == 11:
                ac.wait_ge(S["bres"], q + 1)
                for g in (1, 2):
                    ac.activation(b_parts[32 * g:32 * g + 32, j, :], b_res[32 * g:32 * g + 32, :], ACT.Copy)\
                      .then_inc(S["bmid"], 1)
            elif n == 13:
                ac.wait_ge(S["dabs"], q + 1)
                ac.activation(dtx[:, j, :], dtx[:, j, :], ACT.Exp, scale=-1.0).then_inc(S["dexp"], 1)
                ac.wait_ge(S["dexp"], q + 1)
                ac.activation(dtx[:, j, :], dtx[:, j, :], ACT.Ln, bias=1.0).then_inc(S["dln"], 1)

        def prepare_ve(ve, j, q, n):
            tap = lambda k: x_pad[:, k:k + L] if j == 0 else x_pad[:, 2 * W - k:2 * W - k + L]
            if n == 2:
                ve.wait_ge(S["xcp"], q + 1)
                if q:
                    ve.wait_ge(S["xs"], q)
                ve.tensor_scalar(conv[:, :], tap(0), w_conv[:, j, 0:1], None, ALU.mult).then_inc(S["cv"], 1)
            elif 3 <= n < 3 + DC - 1:
                k = n - 2
                ve.wait_ge(S["cv"], DC * q + k)
                ve.scalar_tensor_tensor(conv[:, :], tap(k), w_conv[:, j, k:k + 1], conv[:, :], ALU.mult, ALU.add)\
                  .then_inc(S["cv"], 1)
            elif n == 10:
                ve.wait_ge(S["bhi"], q + 1)
                if q:
                    ve.wait_ge(S["bmid"], 2 * q)
                    ve.wait_ge(S["blo"], q)
                ve.tensor_tensor(b_res[:, :], z[0:PARTS, :], b_parts[:, j, :], ALU.subtract).then_inc(S["bres"], 1)
            elif n == 12:
                ve.wait_ge(S["bmid"], 2 * (q + 1))
                ve.tensor_tensor(b_parts[64:96, j, :], b_res[64:96, :], b_parts[64:96, j, :], ALU.subtract).then_inc(S["blo"], 1)
                ve.wait_ge(S["dtmm"], q + 1)
                if q:
                    ve.wait_ge(S["da"], DS)
                    ve.wait_ge(S["dbx"], DS)
                ve.tensor_scalar(dt[:, j, :], z[:, :], vec[:, j, 1:2], None, ALU.add).then_inc(S["dtz"], 1)
                ve.wait_ge(S["dtz"], q + 1)
                ve.scalar_tensor_tensor(dtx[:, j, :], dt[:, j, :], -1.0, dt[:, j, :], ALU.mult, ALU.max).then_inc(S["dabs"], 1)
            elif n == 14:
                ve.wait_ge(S["dln"], q + 1)
                ve.scalar_tensor_tensor(dt[:, j, :], dt[:, j, :], 0.0, dtx[:, j, :], ALU.max, ALU.add).then_inc(S["dt"], 1)
                ve.wait_ge(S["dt"], q + 1)
                ve.tensor_tensor(dtx[:, j, :], dt[:, j, :], xs[:, j, :], ALU.mult).then_inc(S["dtx"], 1)

        def prepare_sp(sp, j, q, n):
            if n == 12:
                sp.wait_ge(S["dbccp"], q + 1)
                sp.dma_start(rows[j], dbc[:, :]).then_inc(S["rowput"], 16)

        with nc.Block() as block:
            @block.sync
            def _(sp):
                prepare_sp(sp, 0, 0, 12)
                sp.wait_ge(S["rowput"], 16)

            @block.tensor
            def _(pe):
                for n in range(DS):
                    prepare_pe(pe, 0, 0, 0, n)

            @block.scalar
            def _(ac):
                for n in range(DS):
                    prepare_ac(ac, 0, 0, n)

            @block.vector
            def _(ve):
                for n in range(DS):
                    prepare_ve(ve, 0, 0, n)
        S.clear()

        def scan_round(b, last):
            prepares = 1 if last else 2
            with nc.Block() as block:
                @block.sync
                def _(sp):
                    for i in range(2):
                        if i == 1:
                            sp.wait_ge(S["rowput"], 16)
                        for n in range(DS):
                            if i < prepares:
                                prepare_sp(sp, 1 - i, i, n)
                            k = i * DS + n
                            if k >= RING:
                                sp.wait_ge(S["hc"], k - RING + 1)
                            r0 = DR + DS + n
                            sp.dma_start(c_row[:, k % RING, :], rows[i, r0:r0 + 1, :].to_broadcast([P, L]))\
                              .then_inc(S[f"c{k % RING}"], 16)
                    sp.wait_ge(S["rowput"], 16 * prepares)

                @block.tensor
                def _(pe):
                    def spread_b(k):
                        if k == DS:
                            pe.wait_ge(S["blo"], 1)
                        if k >= 2:
                            pe.wait_ge(S["h"], k - 1)
                        for h in range(2):
                            mm = pe.matmul(bb[k % 2][:, halves[h]], pick[:, k % DS, :], b_parts[:, k // DS, halves[h]],
                                           start=True, stop=True)
                        mm.then_inc(S["bput"], 1)

                    def project_out(i):
                        pe.wait_ge(S["y2"], i + 1)
                        for h in range(2):
                            mm = pe.matmul(y[DM * i:DM * i + DM, halves[h]], w_out[:, i, :], gated[:, halves[h]],
                                           start=True, stop=True)
                        mm.then_inc(S["omm"], 1)

                    def sum_y(k):
                        pe.wait_ge(S["hc"], k + 1)
                        for h in range(2):
                            mm = pe.matmul(y[:, halves[h]], K["ident"][:, :], hc[:, k % 2, halves[h]],
                                           start=(k % DS == 0), stop=(k % DS == DS - 1))
                        mm.then_inc(S["ysum"], 1)

                    spread_b(0)
                    spread_b(1)
                    for k in range(2 * DS):
                        i, n = k // DS, k % DS
                        if k + 2 < 2 * DS:
                            spread_b(k + 2)
                        if i < prepares:
                            prepare_pe(pe, 1 - i, b + i, i, n)
                        if k == DS + 2:
                            project_out(0)
                            pe.wait_ge(S["ocp"], 1)
                            sum_y(DS)
                        if k >= 1 and k != DS + 1:
                            sum_y(k - 1)
                    sum_y(2 * DS - 1)
                    project_out(1)

                @block.scalar
                def _(ac):
                    def copy_out(i):
                        ac.wait_ge(S["omm"], i + 1)
                        ac.activation(ob[DM * i:DM * i + DM, :], y[DM * i:DM * i + DM, :], ACT.Copy).then_inc(S["ocp"], 1)

                    def decay(k):
                        if k == DS:
                            ac.wait_ge(S["dt"], 1)
                        if k >= RING:
                            ac.wait_ge(S["h"], k - RING + 1)
                        i, n = k // DS, k % DS
                        ac.activation(da[:, k % RING, :], dt[:, i, :], ACT.Exp, scale=a_neg[:, i, n:n + 1]).then_inc(S["da"], 1)

                    decay(0)
                    decay(1)
                    for k in range(2 * DS):
                        i, n = k // DS, k % DS
                        if k + 2 < 2 * DS:
                            decay(k + 2)
                        if k == DS + 4:
                            copy_out(0)
                        if i < prepares:
                            prepare_ac(ac, 1 - i, i, n)
                    copy_out(1)

                @block.vector
                def _(ve):
                    def gate(i):
                        ve.wait_ge(S["ysum"], DS * (i + 1))
                        ve.scalar_tensor_tensor(gated[:, :], xs[:, i, :], vec[:, i, 2:3], y[:, :], ALU.mult, ALU.add)\
                          .then_inc(S["y1"], 1)
                        ve.wait_ge(S["y1"], i + 1)
                        ve.tensor_tensor(gated[:, :], gated[:, :], zs[:, i, :], ALU.mult).then_inc(S["y2"], 1)

                    for k in range(2 * DS):
                        i, n = k // DS, k % DS
                        ve.wait_ge(S["bput"], k + 1)
                        if k == DS:
                            ve.wait_ge(S["dtx"], 1)
                        ve.tensor_tensor(bb[k % 2][:, :], dtx[:, i, :], bb[k % 2][:, :], ALU.mult).then_inc(S["dbx"], 1)
                        ve.wait_ge(S["dbx"], k + 1)
                        ve.wait_ge(S["da"], k + 1)
                        if k >= 2:
                            ve.wait_ge(S["hc"], k - 1)
                        ve.tensor_tensor_scan(hs[:, k % 2, :], da[:, k % RING, :], bb[k % 2][:, :], 0.0, ALU.mult, ALU.add)\
                          .then_inc(S["h"], 1)
                        if k == DS + 2:
                            gate(0)
                        if i < prepares:
                            prepare_ve(ve, 1 - i, i, n)
                    ve.wait_ge(S["omm"], 1)
                    gate(1)
                    ve.wait_ge(S["ocp"], 2)
                    ve.tensor_tensor(K["mo_T"][:, bass.ds(b * L, L)], ob[:, :], K["xn_T"][:, bass.ds(b * L, L)], ALU.add)\
                      .then_inc(S["mo"], 1)

                @block.gpsimd
                def _(po):
                    for k in range(2 * DS):
                        po.wait_ge(S["h"], k + 1)
                        po.wait_ge(S[f"c{k % RING}"], 16 * (k // RING + 1))
                        if k >= 2:
                            po.wait_ge(S["ysum"], k - 1)
                        nc.gpsimd.tensor_tensor(hc[:, k % 2, :], hs[:, k % 2, :], c_row[:, k % RING, :], ALU.mult)\
                          .then_inc(S["hc"], 1)
            S.clear()

        with nc.Fori(0, B - 1) as b:
            scan_round(b, last=False)
        scan_round(B - 1, last=True)


def phase_combine(nc, d, keep):
    K = keep
    with ExitStack() as ctx:
        sb = lambda n, s, t=fp32: ctx.enter_context(nc.sbuf_tensor(n, s, t))
        ps = lambda n, s, t=fp32: ctx.enter_context(nc.psum_tensor(n, s, t))
        w_proj, b_proj = sb("d_wproj", [P, P]), sb("d_bproj", [P, 1])
        gate, s0 = sb("d_gate", [P, L]), sb("d_s", [P, L])
        xn_b = sb("d_xnb", [P, NT, P])
        stats, mv, rstd = sb("d_stats", [P, NT, 6]), sb("d_mv", [P, NT, 2]), sb("d_rstd", [P, NT])
        tmp, mhalf = sb("d_tmp", [P, NT]), sb("d_mhalf", [P, NT])
        p_o, p_s, p_x = ps("d_po", [P, L]), ps("d_ps", [P, L]), ps("d_px", [P, L])
        S = Signals(nc, ctx, "d", "load proj gate act sg turn x1 stat aggr veps rstd normed xturn xT keep half")
        with nc.Block() as block:
            @block.sync
            def _(sp):
                sp.dma_start(w_proj[:, :], d["W_proj"]).then_inc(S["load"], 16)
                sp.dma_start(b_proj[:, :], d["b_proj"].rearrange("(c o) -> c o", o=1)).then_inc(S["load"], 16)
                sp.wait_ge(S["load"], 32)

            @block.gpsimd
            def _(po):
                po.memset(mhalf[:, :], -0.5).then_inc(S["half"], 1)
        S.clear()
        with nc.Fori(0, B) as b:
            with nc.Block() as block:
                x_b = flat(K["x_tok"][:, bass.ds(b, 1), :, :])
                r_b = flat(K["r_tok"][:, bass.ds(b, 1), :, :])

                x_f = x_b.rearrange("p t c -> p (t c)")
                HT = NT // 2
                half = [slice(h * HALF, (h + 1) * HALF) for h in range(2)]
                of_half = [range(h * HT, (h + 1) * HT) for h in range(2)]
                xn_out = flat(K["xn_tok"][:, bass.ds(b, 1), :, :])

                @block.tensor
                def _(pe):
                    for h in range(2):
                        pe.matmul(p_o[:, half[h]], w_proj[:, :], K["at_T"][:, bass.ds(b * L + h * HALF, HALF)],
                                  start=True, stop=True).then_inc(S["proj"], 1)
                    for h in range(2):
                        pe.wait_ge(S["sg"], h + 1)
                        for t in of_half[h]:
                            mm = pe.transpose(p_s[:, t * P:(t + 1) * P], gate[:, t * P:(t + 1) * P], K["ident"][:, :])
                        mm.then_inc(S["turn"], 1)
                    for h in range(2):
                        pe.wait_ge(S["normed"], HT * (h + 1))
                        for t in of_half[h]:
                            mm = pe.transpose(p_x[:, t * P:(t + 1) * P], xn_b[:, t, :], K["ident"][:, :])
                        mm.then_inc(S["xturn"], 1)

                @block.scalar
                def _(ac):
                    ac.activation(s0[:, :], K["mo_T"][:, bass.ds(b * L, L)], ACT.Gelu).then_inc(S["act"], 1)
                    for h in range(2):
                        ac.wait_ge(S["proj"], h + 1)
                        ac.activation(gate[:, half[h]], p_o[:, half[h]], ACT.Silu, bias=b_proj[:, 0:1]).then_inc(S["gate"], 1)
                    for h in range(2):
                        ac.wait_ge(S["xturn"], h + 1)
                        ac.activation(K["xn_T"][:, bass.ds(b * L + h * HALF, HALF)], p_x[:, half[h]], ACT.Copy)\
                          .then_inc(S["xT"], 1)

                @block.vector
                def _(ve):
                    ve.wait_ge(S["act"], 1)
                    for h in range(2):
                        ve.wait_ge(S["gate"], h + 1)
                        ve.tensor_tensor(gate[:, half[h]], gate[:, half[h]], s0[:, half[h]], ALU.mult).then_inc(S["sg"], 1)
                    for h in range(2):
                        ve.wait_ge(S["turn"], h + 1)
                        ve.tensor_tensor(x_f[:, half[h]], p_s[:, half[h]], x_f[:, half[h]], ALU.add).then_inc(S["x1"], 1)
                        ve.wait_ge(S["x1"], h + 1)
                        for t in of_half[h]:
                            ve.bn_stats(stats[:, t, :], x_b[:, t, :]).then_inc(S["stat"], 1)
                        ve.wait_ge(S["stat"], HT * (h + 1))
                        for t in of_half[h]:
                            ve.bn_aggr(mv[:, t, :], stats[:, t, :]).then_inc(S["aggr"], 1)
                    for h in range(2):
                        ve.wait_ge(S["aggr"], HT * (h + 1))
                        ve.wait_ge(S["rstd"], h + 1)
                        for t in of_half[h]:
                            ve.tensor_scalar(xn_b[:, t, :], x_b[:, t, :], mv[:, t, 0:1], rstd[:, t:t + 1], ALU.subtract, ALU.mult)\
                              .then_inc(S["normed"], 1)
                    for h in range(2):
                        of = slice(h * HT, (h + 1) * HT)
                        ve.wait_ge(S["normed"], HT * (h + 1))
                        ve.tensor_copy(r_b[:, of, :], xn_b[:, of, :]).then_inc(S["keep"], 1)
                        ve.tensor_copy(xn_out[:, of, :], xn_b[:, of, :]).then_inc(S["keep"], 1)

                @block.gpsimd
                def _(po):
                    for h in range(2):
                        of = slice(h * HT, (h + 1) * HT)
                        po.wait_ge(S["aggr"], HT * (h + 1))
                        nc.gpsimd.tensor_scalar(tmp[:, of], mv[:, of, 1], EPS, None, ALU.add).then_inc(S["veps"], 1)
                        po.wait_ge(S["veps"], h + 1)
                        nc.gpsimd.tensor_tensor(rstd[:, of], tmp[:, of], mhalf[:, of], ALU.pow).then_inc(S["rstd"], 1)
            S.clear()


def phase_retention(nc, d, keep):
    K = keep
    with ExitStack() as ctx:
        sb = lambda n, s, t=fp32: ctx.enter_context(nc.sbuf_tensor(n, s, t))
        ps = lambda n, s, t=fp32: ctx.enter_context(nc.psum_tensor(n, s, t))
        xpos = sb("r_xpos", [P, 4, L])
        decay, decay_q, decay_k = sb("r_decay", [P, RH, P]), sb("r_decq", [P, P]), sb("r_deck", [P, P])
        decay_s, rblock, rhead = sb("r_decs", [P, 1]), sb("r_rblock", [P, P]), sb("r_rhead", [P, RH])
        w5 = sb("r_w5", [P, 5, RH, RD])
        w_g, w_o = sb("r_wg", [P, P]), sb("r_wo", [P, P])
        w_1, w_2 = sb("r_w1", [P, FFN]), sb("r_w2", [P, FFN // P, P])
        vec, b_1, b_2 = sb("r_vec", [P, 6]), sb("r_b1", [P, FFN // P]), sb("r_b2", [P, P])
        epsc, mhalf = sb("r_eps", [P, 1]), sb("r_mhalf", [P, NT])
        stats, mv, rstd, tmp = sb("r_stats", [P, NT, 6]), sb("r_mv", [P, NT, 2]), sb("r_rstd", [P, NT]), sb("r_tmp", [P, NT])
        xn, xnT = sb("r_xn", [P, NT, P]), sb("r_xnT", [P, L])
        qT, kT, rt = sb("r_qT", [P, L]), sb("r_kT", [P, L]), sb("r_rt", [P, 2, L])
        q_all = sb("r_qall", [P, NT, RH, P])
        qd, kd, v, gT = sb("r_qd", [P, L]), sb("r_kd", [P, NT, P]), sb("r_v", [P, NT, P]), sb("r_gT", [P, L])
        kv, state, a = sb("r_kv", [P, NT, P]), sb("r_state", [P, NT, P]), sb("r_a", [P, 2, RH, P])
        yc, ysq, gst = sb("r_yc", [P, NT * P]), sb("r_ysq", [P, NT * P]), sb("r_gst", [P, 3, NT * RH])
        gy = sb("r_gy", [P, L])
        hT = q_all[:, :, :, :].rearrange("p c h n -> p (c h n)")[:, 0:FFN // P * L].rearrange("p (f t) -> p f t", t=L)
        pA, pB, pC, pD = (ps(f"r_p{i}", [P, L]) for i in range(4))
        S = Signals(nc, ctx, "r", "load wload neg const stat aggr veps rstd normed turn xT qmm qrmm kmm krmm vmm gmm rope q k vcp g qz qd "
                    "kturn kd kvmm kvm st0 state score dec y ysum mean yc sq var sqrt gr yn yturn ynT gy omm x2 h hs f2 x3 pre")
        with nc.Block() as block:
            @block.sync
            def _(sp):
                loads = ((xpos, "xpos"), (decay, "decay"), (decay_q, "decay_q"), (decay_k, "decay_k"),
                         (decay_s, "decay_s"), (rblock, "rblock"), (rhead, "rhead"))
                for t, n in loads:
                    sp.dma_start(t[:, :, :] if len(t.shape) == 3 else t[:, :], d[n]).then_inc(S["load"], 16)
                sp.wait_ge(S["load"], 16 * len(loads))

            @block.vector
            def _(ve):
                ve.memset(epsc[:, :], EPS).then_inc(S["const"], 1)
                ve.memset(mhalf[:, :], -0.5).then_inc(S["const"], 1)
                ve.memset(state[:, 0, :], 0.0).then_inc(S["const"], 1)
        S.clear()
        with nc.Fori(0, RL) as layer:
            row = lambda n: d[n][bass.ds(layer, 1), :]
            with nc.Block() as block:
                @block.sync
                def _(sp):
                    one = lambda n: d[n][bass.ds(layer, 1), :, :].rearrange("o a c -> (o a) c")
                    loads = [(w5[:, s, :, :], d[n][bass.ds(layer, 1), :, :, :].rearrange("o h c k -> c (o h) k"))
                             for s, n in ((0, "r_WQ"), (2, "r_WK"), (4, "r_WV"))]
                    loads += [(w_g[:, :], one("r_WG")), (w_o[:, :], one("r_WO")), (w_1[:, :], one("r_ffn_w1")),
                              (w_2[:, :, :], d["r_ffn_w2"][bass.ds(layer, 1), :, :].rearrange("o (f p) c -> p (o f) c", p=P)),
                              (b_2[:, :], row("r_ffn_b2").to_broadcast([P, P]))]
                    cols = [(vec[:, i:i + 1], row("r_" + n).rearrange("o (c u) -> c (o u)", u=1))
                            for i, n in enumerate(("ln1_w", "ln1_b", "ln2_w", "ln2_b", "gn_w", "gn_b"))]
                    cols += [(b_1[:, f:f + 1], row("r_ffn_b1")[:, f * P:(f + 1) * P].rearrange("o (c u) -> c (o u)", u=1))
                             for f in range(FFN // P)]
                    for dst, src in loads + cols:
                        sp.dma_start(dst, src).then_inc(S["wload"], 16)
                    sp.wait_ge(S["wload"], 16 * len(loads + cols))

                @block.vector
                def _(ve):
                    ve.wait_ge(S["wload"], 16 * 18)
                    for s in (0, 2):
                        pair = lambda u, o: w5[:, u, :, :].rearrange("c h (i o) -> c (h i) o", o=2)[:, :, o]
                        ve.tensor_scalar(pair(s + 1, 0), pair(s, 1), -1.0, None, ALU.mult).then_inc(S["neg"], 1)
                        ve.tensor_copy(pair(s + 1, 1), pair(s, 0)).then_inc(S["neg"], 1)
            S.clear()
            with nc.Fori(0, B) as b:
                with nc.Block() as block:
                    x_b = flat(K["r_tok"][:, bass.ds(b, 1), :, :])
                    x_f = x_b.rearrange("p t c -> p (t c)")
                    HT, HR = NT // 2, NT // 2 * RH
                    half = [slice(h * HALF, (h + 1) * HALF) for h in range(2)]
                    of_half = [range(h * HT, (h + 1) * HT) for h in range(2)]
                    tiles = [slice(t * P, (t + 1) * P) for t in range(NT)]
                    w = lambda s: w5[:, s, :, :].rearrange("c h k -> c (h k)")

                    @block.tensor
                    def _(pe):
                        def project(out, h, lhsT, rhs, sig):
                            pe.matmul(out[:, half[h]], lhsT, rhs[:, half[h]], start=True, stop=True).then_inc(S[sig], 1)

                        def turn(out, h, src, sig):
                            for t in of_half[h]:
                                mm = pe.transpose(out[:, tiles[t]], src(t), K["ident"][:, :])
                            mm.then_inc(S[sig], 1)

                        for h in range(2):
                            pe.wait_ge(S["normed"], HT * (h + 1))
                            turn(pA, h, lambda t: xn[:, t, :], "turn")
                        for h in range(2):
                            pe.wait_ge(S["xT"], h + 1)
                            project(pB, h, w(0), xnT, "qmm")
                            project(pC, h, w(1), xnT, "qrmm")
                        for h in range(2):
                            for t in of_half[h]:
                                mm = pe.matmul(pD[:, tiles[t]], xnT[:, tiles[t]], w(4), start=True, stop=True)
                            mm.then_inc(S["vmm"], 1)
                        for h in range(2):
                            project(pA, h, w_g[:, :], xnT, "gmm")
                        for h in range(2):
                            pe.wait_ge(S["rope"], 2 * h + 2)
                            project(pB, h, w(2), xnT, "kmm")
                            project(pC, h, w(3), xnT, "krmm")
                        for h in range(2):
                            pe.wait_ge(S["k"], h + 1)
                            pe.wait_ge(S["vcp"], h + 1)
                            turn(pD, h, lambda t: kT[:, tiles[t]], "kturn")
                        for h in range(2):
                            pe.wait_ge(S["kd"], h + 1)
                            pe.wait_ge(S["g"], h + 1)
                            for c in of_half[h]:
                                mm = pe.matmul(pA[:, tiles[c]], kd[:, c, :], v[:, c, :], start=True, stop=True)
                            mm.then_inc(S["kvmm"], 1)
                        for c in range(NT + 1):
                            if c < NT:
                                if c % HT == 0:
                                    pe.wait_ge(S["qz"], RH * (c // HT + 1))
                                    pe.wait_ge(S["qd"], c // HT + 1)
                                if c >= 2:
                                    pe.wait_ge(S["dec"], c - 1)
                                out = (pB, pC)[c % 2]
                                for g, s in enumerate(half):
                                    mm = pe.matmul(out[:, s], kT[:, tiles[c]],
                                                   q_all[:, c, 4 * g:4 * g + 4, :].rearrange("p h n -> p (h n)"),
                                                   start=True, stop=True)
                                mm.then_inc(S["score"], 1)
                            if c >= 1:
                                u = c - 1
                                pe.wait_ge(S["dec"], u + 1)
                                if u:
                                    pe.wait_ge(S["state"], u)
                                pe.matmul(pD[:, tiles[u]], qd[:, tiles[u]], state[:, u, :], start=True, stop=False,
                                          skip_group_check=True)
                                for h in range(RH):
                                    o = u * P + h * RD
                                    mm = pe.matmul(pD[:, o:o + RD], a[:, u % 2, h, :], v[:, u, h * RD:(h + 1) * RD],
                                                   start=False, stop=(h == RH - 1), skip_group_check=True)
                                mm.then_inc(S["y"], 1)
                        for h in range(2):
                            pe.wait_ge(S["yn"], h + 1)
                            turn(pA, h, lambda t: yc[:, tiles[t]], "yturn")
                            pe.wait_ge(S["gy"], h + 1)
                            for t in of_half[h]:
                                mm = pe.matmul(pB[:, tiles[t]], gy[:, tiles[t]], w_o[:, :], start=True, stop=True)
                            mm.then_inc(S["omm"], 1)
                        for h in range(2):
                            pe.wait_ge(S["normed"], NT + HT * (h + 1))
                            turn(pA, h, lambda t: xn[:, t, :], "turn")
                        for h in range(2):
                            pe.wait_ge(S["xT"], 2 + h + 1)
                            for f in range(FFN // P):
                                u = h * (FFN // P) + f
                                if u >= 4:
                                    pe.wait_ge(S["hs"], u - 3)
                                pe.matmul((pC, pD)[f // 2][:, half[f % 2]], w_1[:, f * P:(f + 1) * P], xnT[:, half[h]],
                                          start=True, stop=True).then_inc(S["h"], 1)
                        for h in range(2):
                            pe.wait_ge(S["hs"], FFN // P * (h + 1))
                            for t in of_half[h]:
                                for f in range(FFN // P):
                                    mm = pe.matmul(pA[:, tiles[t]], hT[:, f, tiles[t]], w_2[:, f, :], start=(f == 0),
                                                   stop=(f == FFN // P - 1))
                            mm.then_inc(S["f2"], 1)

                    @block.scalar
                    def _(ac):
                        def scaled(h, n, i):
                            ac.wait_ge(S["turn"], n)
                            ac.activation(xnT[:, half[h]], pA[:, half[h]], ACT.Identity, bias=vec[:, i + 1:i + 2],
                                          scale=vec[:, i:i + 1]).then_inc(S["xT"], 1)

                        for h in range(2):
                            scaled(h, h + 1, 0)
                        for h in range(2):
                            ac.wait_ge(S["vmm"], h + 1)
                            ac.activation(v[:, h * HT:(h + 1) * HT, :].rearrange("p t c -> p (t c)"), pD[:, half[h]], ACT.Copy)\
                              .then_inc(S["vcp"], 1)
                        for h in range(2):
                            ac.wait_ge(S["gmm"], h + 1)
                            ac.activation(gT[:, half[h]], pA[:, half[h]], ACT.Silu).then_inc(S["g"], 1)
                        for h in range(2):
                            ac.wait_ge(S["q"], h + 1)
                            for n in range(RH):
                                ac.activation(q_all[:, h * HT:(h + 1) * HT, n, :],
                                              qT[:, half[h]].rearrange("p (c n) -> p c n", n=P), ACT.Copy,
                                              scale=rhead[:, n:n + 1]).then_inc(S["qz"], 1)
                        for h in range(2):
                            ac.wait_ge(S["var"], h + 1)
                            ac.activation(gst[:, 2, h * HR:(h + 1) * HR], gst[:, 1, h * HR:(h + 1) * HR], ACT.Sqrt,
                                          bias=epsc[:, 0:1], scale=1.0 / RD).then_inc(S["sqrt"], 1)
                            ac.wait_ge(S["yturn"], h + 1)
                            ac.activation(gy[:, half[h]], pA[:, half[h]], ACT.Identity, bias=vec[:, 5:6], scale=vec[:, 4:5])\
                              .then_inc(S["ynT"], 1)
                        for h in range(2):
                            scaled(h, 2 + h + 1, 2)
                        for h in range(2):
                            for f in range(FFN // P):
                                ac.wait_ge(S["h"], h * (FFN // P) + f + 1)
                                ac.activation(hT[:, f, half[h]], (pC, pD)[f // 2][:, half[f % 2]], ACT.Silu,
                                              bias=b_1[:, f:f + 1]).then_inc(S["hs"], 1)

                    @block.vector
                    def _(ve):
                        def statistics(h, n):
                            for t in of_half[h]:
                                ve.bn_stats(stats[:, t, :], x_b[:, t, :]).then_inc(S["stat"], 1)
                            ve.wait_ge(S["stat"], HT * n)
                            for t in of_half[h]:
                                ve.bn_aggr(mv[:, t, :], stats[:, t, :]).then_inc(S["aggr"], 1)

                        def normalize(h, n):
                            ve.wait_ge(S["aggr"], HT * n)
                            ve.wait_ge(S["rstd"], n)
                            for t in of_half[h]:
                                ve.tensor_scalar(xn[:, t, :], x_b[:, t, :], mv[:, t, 0:1], rstd[:, t:t + 1], ALU.subtract,
                                                 ALU.mult).then_inc(S["normed"], 1)

                        for h in range(2):
                            statistics(h, h + 1)
                        for h in range(2):
                            normalize(h, h + 1)
                        for i, (one, two, dst, done) in enumerate((("qmm", "qrmm", qT, "q"), ("kmm", "krmm", kT, "k"))):
                            for h in range(2):
                                ve.wait_ge(S[one], h + 1)
                                if i:
                                    ve.wait_ge(S["q"], h + 1)
                                ve.tensor_tensor(rt[:, 0, half[h]], pB[:, half[h]], xpos[:, 2 * i, half[h]], ALU.mult)\
                                  .then_inc(S["rope"], 1)
                                ve.wait_ge(S[two], h + 1)
                                ve.tensor_tensor(rt[:, 1, half[h]], pC[:, half[h]], xpos[:, 2 * i + 1, half[h]], ALU.mult)\
                                  .then_inc(S["rope"], 1)
                                ve.wait_ge(S["rope"], 4 * i + 2 * h + 2)
                                ve.tensor_tensor(dst[:, half[h]], rt[:, 0, half[h]], rt[:, 1, half[h]], ALU.add)\
                                  .then_inc(S[done], 1)
                        chunks = lambda ap: ap.rearrange("p (c n) -> p c n", n=P)
                        over = lambda t: t[:, :].rearrange("p (o n) -> p o n", o=1).to_broadcast([P, HT, P])
                        for h in range(2):
                            ve.wait_ge(S["kturn"], h + 1)
                            ve.tensor_tensor(kd[:, h * HT:(h + 1) * HT, :], chunks(pD[:, half[h]]), over(decay_k), ALU.mult)\
                              .then_inc(S["kd"], 1)
                        for h in range(2):
                            ve.tensor_tensor(chunks(qd[:, half[h]]), chunks(qT[:, half[h]]), over(decay_q), ALU.mult)\
                              .then_inc(S["qd"], 1)
                        for h in range(2):
                            ve.wait_ge(S["kvmm"], h + 1)
                            ve.tensor_tensor(kv[:, h * HT:(h + 1) * HT, :], chunks(pA[:, half[h]]), over(rblock), ALU.mult)\
                              .then_inc(S["kvm"], 1)

                        def next_state(c):
                            ve.wait_ge(S["kvm"], c // HT + 1)
                            if c:
                                ve.wait_ge(S["state"], c)
                            ve.scalar_tensor_tensor(state[:, c + 1, :], state[:, c, :], decay_s[:, 0:1], kv[:, c, :],
                                                    ALU.mult, ALU.add).then_inc(S["state"], 1)

                        heads = lambda ap: ap.rearrange("p (a e) -> p a e", e=RD)
                        wide = lambda ap: ap.rearrange("p (a o) -> p a o", o=1).to_broadcast([P, HR, RD])

                        def group_norm(h, step):
                            g = lambda i: gst[:, i, h * HR:(h + 1) * HR]
                            y_h, yc_h, ysq_h = heads(pD[:, half[h]]), heads(yc[:, half[h]]), heads(ysq[:, half[h]])
                            if step == 0:
                                ve.wait_ge(S["y"], HT * (h + 1))
                                ve.tensor_reduce(g(0), y_h, AX.X, ALU.add).then_inc(S["ysum"], 1)
                                ve.wait_ge(S["ysum"], h + 1)
                                ve.tensor_scalar(g(1), g(0), 1.0 / RD, None, ALU.mult).then_inc(S["mean"], 1)
                            elif step == 1:
                                ve.wait_ge(S["mean"], h + 1)
                                ve.tensor_tensor(yc_h, y_h, wide(g(1)), ALU.subtract).then_inc(S["yc"], 1)
                            elif step == 2:
                                ve.wait_ge(S["yc"], h + 1)
                                ve.tensor_tensor(ysq_h, yc_h, yc_h, ALU.mult).then_inc(S["sq"], 1)
                                ve.wait_ge(S["sq"], h + 1)
                                ve.tensor_reduce(g(1), ysq_h, AX.X, ALU.add).then_inc(S["var"], 1)
                            elif step == 3:
                                ve.wait_ge(S["sqrt"], h + 1)
                                ve.reciprocal(g(0), g(2)).then_inc(S["gr"], 1)
                                ve.wait_ge(S["gr"], h + 1)
                                ve.tensor_tensor(yc_h, yc_h, wide(g(0)), ALU.mult).then_inc(S["yn"], 1)

                        def gate(h):
                            ve.wait_ge(S["ynT"], h + 1)
                            ve.tensor_tensor(gy[:, half[h]], gy[:, half[h]], gT[:, half[h]], ALU.mult).then_inc(S["gy"], 1)

                        def add_retained(h):
                            ve.wait_ge(S["omm"], h + 1)
                            ve.tensor_tensor(x_f[:, half[h]], pB[:, half[h]], x_f[:, half[h]], ALU.add).then_inc(S["x2"], 1)
                            ve.wait_ge(S["x2"], h + 1)

                        for c in range(NT):
                            ve.wait_ge(S["score"], c + 1)
                            if c >= 2:
                                ve.wait_ge(S["y"], c - 1)
                            ve.tensor_tensor(a[:, c % 2, :, :].rearrange("p h n -> p (h n)"), (pB, pC)[c % 2][:, :],
                                             decay[:, :, :].rearrange("p h n -> p (h n)"), ALU.mult).then_inc(S["dec"], 1)
                            if c < NT - 1:
                                next_state(c)
                            if c >= HT:
                                group_norm(0, c - HT)
                        for step in range(3):
                            group_norm(1, step)
                        gate(0)
                        group_norm(1, 3)
                        add_retained(0)
                        statistics(0, 3)
                        gate(1)
                        normalize(0, 3)
                        add_retained(1)
                        statistics(1, 4)
                        normalize(1, 4)
                        for h in range(2):
                            x_h = x_b[:, h * HT:(h + 1) * HT, :]
                            ve.wait_ge(S["normed"], NT + HT * (h + 1))
                            ve.tensor_tensor(x_h, x_h, over(b_2), ALU.add).then_inc(S["pre"], 1)
                        for h in range(2):
                            ve.wait_ge(S["pre"], h + 1)
                            ve.wait_ge(S["f2"], h + 1)
                            ve.tensor_tensor(x_f[:, half[h]], pA[:, half[h]], x_f[:, half[h]], ALU.add).then_inc(S["x3"], 1)

                    @block.gpsimd
                    def _(po):
                        for n in range(4):
                            s = slice(n % 2 * HT, n % 2 * HT + HT)
                            po.wait_ge(S["aggr"], HT * (n + 1))
                            nc.gpsimd.tensor_scalar(tmp[:, s], mv[:, s, 1], EPS, None, ALU.add).then_inc(S["veps"], 1)
                            po.wait_ge(S["veps"], n + 1)
                            nc.gpsimd.tensor_tensor(rstd[:, s], tmp[:, s], mhalf[:, s], ALU.pow).then_inc(S["rstd"], 1)
                S.clear()


def phase_dispatch(nc, d, keep):
    K = keep
    CW, SUB = 256, 4
    STEPS = SUB * NT
    RING = 6
    with ExitStack() as ctx:
        sb = lambda n, s, t=fp32: ctx.enter_context(nc.sbuf_tensor(n, s, t))
        ps = lambda n, s, t=fp32: ctx.enter_context(nc.psum_tensor(n, s, t))
        mx, rs = sb("e_mx", [P, 2, CW]), sb("e_rs", [P, 2, CW])
        e = sb("e_e", [P, RING, B, CW])
        w = sb("e_w", [P, 2, B, CW])
        logit = [ps(f"e_l{i}", [P, B, CW]) for i in range(2)]
        gather = ps("e_g", [P, B, CW])
        total = [ps(f"e_s{i}", [P, CW]) for i in range(2)]
        S = Signals(nc, ctx, "e", "load logit mx sub exp total rs wa wb slots out")
        with nc.Block() as block:
            @block.sync
            def _(sp):
                sp.dma_start(K["phi"][:, :], d["e_phi"].rearrange("c n p -> c (n p)")).then_inc(S["load"], 16)
                sp.dma_start(K["w_e"][:, :, :], d["e_W"].rearrange("n c e -> c n e")).then_inc(K["experts_in"], 16)
                for j in range(P // MP):
                    sp.dma_start(K["bias_e"][MP * j:MP * j + MP, :, :],
                                 d["e_b"].rearrange("(t j) e -> j t e", j=P // MP)[j:j + 1].to_broadcast([MP, MS // P, P]))\
                      .then_inc(K["experts_in"], 16)
                sp.wait_ge(S["load"], 16)
        S.clear()
        with nc.Fori(0, MS // (CW * SUB)) as c:
            with nc.Block() as block:
                @block.tensor
                def _(pe):
                    for t in range(STEPS + 4):
                        if t < STEPS:
                            if t >= 2:
                                pe.wait_ge(S["sub"], t - 1)
                            for b in range(B):
                                mm = pe.matmul(logit[t % 2][:, b, :], K["xn_T"][:, b * L + t % NT * P:b * L + (t % NT + 1) * P],
                                               K["phi"][:, bass.ds(c * (CW * SUB) + t // NT * CW, CW)], start=True, stop=True)
                            mm.then_inc(S["logit"], 1)
                        if 2 <= t < STEPS + 2:
                            u = t - 2
                            pe.wait_ge(S["exp"], u + 1)
                            if u >= 2:
                                pe.wait_ge(S["rs"], u - 1)
                            for b in range(B):
                                mm = pe.matmul(total[u % 2][:, :], K["ident"][:, :], e[:, u % RING, b, :],
                                               start=(b == 0), stop=(b == B - 1))
                            mm.then_inc(S["total"], 1)
                        if t >= 4:
                            u = t - 4
                            pe.wait_ge(S["wa"], u + 1)
                            pe.wait_ge(S["wb"], u + 1)
                            if u % NT == 0 and u:
                                pe.wait_ge(S["out"], u // NT)
                            for b in range(B):
                                mm = pe.matmul(gather[:, b, :], K["xn_tok"][:, b, u % NT, :], w[:, u % 2, b, :],
                                               start=(u % NT == 0 and b % 2 == 0), stop=(u % NT == NT - 1), skip_group_check=True)
                            mm.then_inc(S["slots"], 1)

                @block.vector
                def _(ve):
                    for t in range(STEPS + 3):
                        if t < STEPS:
                            i = t % 2
                            ve.wait_ge(S["logit"], t + 1)
                            if t >= 2:
                                ve.wait_ge(S["sub"], t - 1)
                            ve.tensor_reduce(mx[:, i, :], logit[i][:, :, :].rearrange("p b n -> p n b"), AX.X, ALU.max)\
                              .then_inc(S["mx"], 1)
                            ve.wait_ge(S["mx"], t + 1)
                            if t >= RING:
                                ve.wait_ge(S["wa"], t - RING + 1)
                                ve.wait_ge(S["wb"], t - RING + 1)
                            ve.tensor_tensor(e[:, t % RING, :, :], logit[i][:, :, :],
                                             mx[:, i, :].rearrange("p (o n) -> p o n", o=1).to_broadcast([P, B, CW]),
                                             ALU.subtract).then_inc(S["sub"], 1)
                        if t >= 3:
                            u, i = t - 3, (t - 3) % 2
                            ve.wait_ge(S["total"], u + 1)
                            if u >= 2:
                                ve.wait_ge(S["wa"], u - 1)
                                ve.wait_ge(S["wb"], u - 1)
                            ve.reciprocal(rs[:, i, :], total[i][:, :]).then_inc(S["rs"], 1)
                            ve.wait_ge(S["rs"], u + 1)
                            if u >= 2:
                                ve.wait_ge(S["slots"], u - 1)
                            ve.tensor_tensor(w[:, i, 2:4, :], e[:, u % RING, 2:4, :],
                                             rs[:, i, :].rearrange("p (o n) -> p o n", o=1).to_broadcast([P, 2, CW]),
                                             ALU.mult).then_inc(S["wb"], 1)

                @block.scalar
                def _(ac):
                    for t in range(STEPS + 4):
                        if t < STEPS:
                            ac.wait_ge(S["sub"], t + 1)
                            ac.activation(e[:, t % RING, :, :], e[:, t % RING, :, :], ACT.Exp).then_inc(S["exp"], 1)
                        if t >= 4 and (t - 4) % NT == NT - 1:
                            u = (t - 4) // NT
                            ac.wait_ge(S["slots"], (u + 1) * NT)
                            ac.activation(K["slots_T"][:, :, bass.ds(c * (CW * SUB) + u * CW, CW)], gather[:, :, :], ACT.Copy)\
                              .then_inc(S["out"], 1)

                @block.gpsimd
                def _(po):
                    g = nc.gpsimd
                    for u in range(STEPS):
                        i = u % 2
                        po.wait_ge(S["rs"], u + 1)
                        if u >= 2:
                            po.wait_ge(S["slots"], u - 1)
                        g.tensor_tensor(w[:, i, 0:2, :], e[:, u % RING, 0:2, :],
                                        rs[:, i, :].rearrange("p (o n) -> p o n", o=1).to_broadcast([P, 2, CW]),
                                        ALU.mult).then_inc(S["wa"], 1)
            S.clear()


def phase_experts(nc, d, keep, out):
    K = keep
    ST = MS // P
    with ExitStack() as ctx:
        sb = lambda n, s, t=fp32: ctx.enter_context(nc.sbuf_tensor(n, s, t))
        ps = lambda n, s, t=fp32: ctx.enter_context(nc.psum_tensor(n, s, t))
        slot_b, x_b = sb("f_slots", [P, MS]), sb("f_x", [P, L])
        y = sb("f_y", [P, ST, P])
        ex, exT = sb("f_ex", [P, 2, MS]), sb("f_exT", [P, 2, ST, P])
        pm, nm = sb("f_pm", [P, NT, 2]), sb("f_nm", [P, NT])
        den, dsum, rden = sb("f_den", [P, NT, 2]), sb("f_dsum", [P, NT]), sb("f_rden", [P, NT])
        o = sb("f_o", [P, NT, P])
        logit = [ps(f"f_l{i}", [P, 2 * HALF]) for i in range(2)]
        turn = [ps(f"f_t{i}", [P, HALF]) for i in range(2)]
        acc = [ps(f"f_a{i}", [P, P]) for i in range(2)]
        S = Signals(nc, ctx, "f", "cp ymm y logit pm nm exp turn ev_v ev_s acc dsum rden o silu mul fin store")
        with nc.Block() as block:
            @block.sync
            def _(sp):
                sp.wait_ge(K["experts_in"], 16 * (1 + P // MP))
        with nc.Fori(0, B) as b:
            with nc.Block() as block:
                @block.tensor
                def _(pe):
                    pe.wait_ge(S["cp"], 2)
                    for t in range(ST):
                        dst = logit[t // 8][:, t % 8 * P:(t % 8 + 1) * P]
                        for j in range(P // MP):
                            n = t * (P // MP) + j
                            mm = pe.matmul(dst[MP * j:MP * j + MP, :], slot_b[:, n * MP:(n + 1) * MP], K["w_e"][:, n, :],
                                           start=True, stop=True)
                        if t % 8 == 7:
                            mm.then_inc(S["ymm"], 1)
                    for t in range(NT + 1):
                        if t < NT:
                            for h in range(2):
                                if t == 0:
                                    pe.wait_ge(S["y"], h + 1)
                                else:
                                    pe.wait_ge(S["exp"], 2 * (t - 1) + h + 1)
                                for q in range(2):
                                    s = h * 2 * HALF + q * HALF
                                    mm = pe.matmul(logit[h][:, q * HALF:(q + 1) * HALF], x_b[:, t * P:(t + 1) * P],
                                                   K["phi"][:, s:s + HALF], start=True, stop=True)
                                mm.then_inc(S["logit"], 1)
                        if t >= 1:
                            u = t - 1
                            pe.wait_ge(S["exp"], 2 * u + 2)
                            for q in range(4):
                                if u or q >= 2:
                                    pe.wait_ge(S[("ev_v", "ev_s")[q % 2]], 2 * u + q // 2)
                                for i in range(4):
                                    s = (4 * q + i) * P
                                    mm = pe.transpose(turn[q % 2][:, i * P:(i + 1) * P], ex[:, u % 2, s:s + P], K["ident"][:, :])
                                mm.then_inc(S["turn"], 1)
                            if u >= 2:
                                pe.wait_ge(S["o"], u - 1)
                            pe.wait_ge(S["ev_v"], 2 * u + 2)
                            pe.wait_ge(S["ev_s"], 2 * u + 2)
                            for i in range(ST):
                                mm = pe.matmul(acc[u % 2][:, :], exT[:, u % 2, i, :], y[:, i, :], start=(i == 0), stop=(i == ST - 1))
                            mm.then_inc(S["acc"], 1)

                @block.scalar
                def _(ac):
                    ac.activation(slot_b[:, :], K["slots_T"][:, bass.ds(b, 1), :].rearrange("p o n -> p (o n)"), ACT.Copy)\
                      .then_inc(S["cp"], 1)
                    ac.activation(x_b[:, :], K["xn_T"][:, bass.ds(b * L, L)], ACT.Copy).then_inc(S["cp"], 1)
                    for t in range(NT + 1):
                        if t >= 1:
                            u = t - 1
                            for q in (1, 3):
                                ac.wait_ge(S["turn"], 4 * u + q + 1)
                                if u >= 2:
                                    ac.wait_ge(S["acc"], u - 1)
                                ac.activation(exT[:, u % 2, 4 * q:4 * q + 4, :].rearrange("p a n -> p (a n)"), turn[1][:, :],
                                              ACT.Copy).then_inc(S["ev_s"], 1)
                        if t < NT:
                            ac.wait_ge(S["nm"], t + 1)
                            if t >= 2:
                                ac.wait_ge(S["turn"], 4 * (t - 1))
                            for h in range(2):
                                ac.activation(ex[:, t % 2, h * 2 * HALF:(h + 1) * 2 * HALF], logit[h][:, :], ACT.Exp,
                                              bias=nm[:, t:t + 1], accum_out=den[:, t, h:h + 1]).then_inc(S["exp"], 1)
                    ac.wait_ge(S["o"], NT)
                    ac.activation(o[:, :, :], o[:, :, :], ACT.Silu).then_inc(S["silu"], 1)

                @block.vector
                def _(ve):
                    for h in range(2):
                        ve.wait_ge(S["ymm"], h + 1)
                        ve.tensor_tensor(y[:, 8 * h:8 * h + 8, :].rearrange("p t e -> p (t e)"), logit[h][:, :],
                                         K["bias_e"][:, 8 * h:8 * h + 8, :].rearrange("p t e -> p (t e)"), ALU.add).then_inc(S["y"], 1)
                    for t in range(NT + 2):
                        for h in range(2):
                            if t < NT:
                                ve.wait_ge(S["logit"], 2 * t + h + 1)
                                ve.tensor_reduce(pm[:, t, h:h + 1], logit[h][:, :], AX.X, ALU.max).then_inc(S["pm"], 1)
                                if h == 1:
                                    ve.wait_ge(S["pm"], 2 * t + 2)
                                    ve.tensor_reduce(nm[:, t:t + 1], pm[:, t, :], AX.X, ALU.max, negate=True).then_inc(S["nm"], 1)
                            if 1 <= t <= NT:
                                u, q = t - 1, 2 * h
                                ve.wait_ge(S["turn"], 4 * u + q + 1)
                                if u >= 2:
                                    ve.wait_ge(S["acc"], u - 1)
                                ve.tensor_copy(exT[:, u % 2, 4 * q:4 * q + 4, :].rearrange("p a n -> p (a n)"), turn[0][:, :])\
                                  .then_inc(S["ev_v"], 1)
                        if 1 <= t <= NT:
                            u = t - 1
                            ve.wait_ge(S["exp"], 2 * u + 2)
                            ve.tensor_tensor(dsum[:, u:u + 1], den[:, u, 0:1], den[:, u, 1:2], ALU.add).then_inc(S["dsum"], 1)
                            ve.wait_ge(S["dsum"], u + 1)
                            ve.reciprocal(rden[:, u:u + 1], dsum[:, u:u + 1]).then_inc(S["rden"], 1)
                        if t >= 2:
                            u = t - 2
                            ve.wait_ge(S["acc"], u + 1)
                            ve.wait_ge(S["rden"], u + 1)
                            ve.tensor_scalar(o[:, u, :], acc[u % 2][:, :], rden[:, u:u + 1], None, ALU.mult).then_inc(S["o"], 1)
                    ve.wait_ge(S["silu"], 1)
                    r_b = flat(K["r_tok"][:, bass.ds(b, 1), :, :])
                    x1 = flat(K["x_tok"][:, bass.ds(b, 1), :, :])
                    ve.tensor_tensor(o[:, :, :], o[:, :, :], r_b, ALU.mult).then_inc(S["mul"], 1)
                    ve.wait_ge(S["mul"], 1)
                    ve.tensor_tensor(o[:, :, :], o[:, :, :], x1, ALU.add).then_inc(S["fin"], 1)

                @block.sync
                def _(sp):
                    sp.wait_ge(S["fin"], 1)
                    sp.dma_start(out[bass.ds(b, 1), :, :].rearrange("o (t p) c -> p (o t) c", p=P), o[:, :, :]).then_inc(S["store"], 16)
                    sp.wait_ge(S["store"], 16)
            S.clear()


def moe(nc, d, keep, out, ctx):
    sb = lambda n, s, t=fp32: ctx.enter_context(nc.sbuf_tensor(n, s, t))
    keep.update({"phi": sb("phi", [P, MS]), "w_e": sb("w_e", [P, ME, P]), "bias_e": sb("bias_e", [P, MS // P, P]),
                 "slots_T": sb("slots_T", [P, B, MS])})
    keep["experts_in"] = ctx.enter_context(nc.semaphore("experts_in"))
    phase_dispatch(nc, d, keep)
    phase_experts(nc, d, keep, out)


def build(nc, d, out):
    dt = nc.dram_tensor
    d["q_parts"] = dt("q_parts", (B, 3, P, L), bf16, kind="Internal").ap()
    d["k_parts"] = dt("k_parts", (B, 3, P, L), bf16, kind="Internal").ap()
    d["v_tiles"] = dt("v_tiles", (B, P, NT * AH * 32), fp32, kind="Internal").ap()
    d["k_mask"] = dt("k_mask", (2, B, L), bf16, kind="Internal").ap()
    d["bc_rows"] = dt("bc_rows", (2, DR + 2 * DS, L), fp32, kind="Internal").ap()
    d["q_mask"] = dt("q_mask", (2, B, QW), bf16, kind="Internal").ap()
    with ExitStack() as ctx:
        sb = lambda n, s, t=fp32: ctx.enter_context(nc.sbuf_tensor(n, s, t))
        keep = {"x_tok": sb("x_tok", [P, B, NT, C]), "xn_T": sb("xn_T", [P, N]), "ident": sb("ident", [P, P]),
                "at_T": sb("at_T", [P, N]), "mo_T": sb("mo_T", [P, N])}
        keep["xn_tok"] = keep["mo_T"][:, :].rearrange("p (b t c) -> p b t c", b=B, t=NT)
        keep["r_tok"] = keep["at_T"][:, :].rearrange("p (b t c) -> p b t c", b=B, t=NT)
        with ExitStack() as c0:
            s0 = lambda n, s, t=fp32: c0.enter_context(nc.sbuf_tensor(n, s, t))
            keep.update({"h_T": s0("h_T", [P, N]), "sim": s0("sim", [P, B, NT])})
            with ExitStack() as c1:
                s1 = lambda n, s, t=fp32: c1.enter_context(nc.sbuf_tensor(n, s, t))
                keep.update({"wqkv": s1("wqkv", [P, 3, P]), "wqk": s1("wqk", [P, 2, P]),
                             "same_head": s1("same_head", [P, P]), "head_of": s1("head_of", [P, AH]),
                             "gdir": s1("gdir", [P, AH]), "reg_tok": s1("reg_tok", [P, B * NT]), "ln": s1("ln", [P, 2])})
                phase_prepare(nc, d, keep)
                phase_project(nc, d, keep)
                phase_classes(nc, d, keep)
            phase_mamba(nc, d, keep)
        phase_attention(nc, d, keep)
        phase_combine(nc, d, keep)
        phase_retention(nc, d, keep)
        moe(nc, d, keep, out, ctx)


INS = ["L0_attn_x", "L0_attn_ln_g", "L0_attn_ln_b"] + \
      [f"L0_attn_m{i}_{n}" for i in (1, 2) for n in ("Win", "Wconv", "bconv", "Wx", "Wdt", "bdt", "Alog", "Dp", "Wout")] + \
      ["L0_ffn_g_info", "L0_ffn_W_qkv", "L0_ffn_W_proj", "L0_ffn_b_proj"] + \
      ["L1_attn_" + n for n in ("ln1_w", "ln1_b", "ln2_w", "ln2_b", "WQ", "WK", "WV", "gn_w", "gn_b", "WG", "WO",
                                "ffn_w1", "ffn_b1", "ffn_w2", "ffn_b2")] + \
      ["L1_ffn_phi", "L1_ffn_W", "L1_ffn_b"]


def kernel(**inputs):
    import numpy as _np
    import concourse.bacc as _bacc
    from concourse import mybir as _mybir
    from concourse.bass_utils import run_bass_kernel_spmd as _run

    nc = _bacc.Bacc("TRN2", target_bir_lowering=False, num_devices=1)
    arrays, d = {}, {}

    def give(name, key, a):
        arrays[f"in_{name}_dram"] = a
        d[key] = nc.dram_tensor(f"in_{name}_dram", a.shape, _mybir.dt.from_np(a.dtype), kind="ExternalInput").ap()

    short = {"L0_attn_": "", "L0_ffn_": "", "L1_attn_": "r_", "L1_ffn_": "e_"}
    for name in INS:
        pre = next(p for p in short if name.startswith(p))
        give(name, short[pre] + name[len(pre):], _np.ascontiguousarray(inputs[name]))
    for name, a in shape_constants().items():
        give(name, name, a)
    out = nc.dram_tensor("out_0_dram", (B, L, C), _mybir.dt.float32, kind="ExternalOutput").ap()
    build(nc, d, out)
    r = _run(nc, [arrays], core_ids=[0])
    return r.results[0]["out_0_dram"]
```
